# Optimizing a Trainium2 kernel written in Bass

```python
import numpy as np
import jax
import jax.numpy as jnp

def _softmax(x, axis=-1):
    return jax.nn.softmax(x, axis=axis)

def _gelu(x):
    return jax.nn.gelu(x, approximate=True)

def _silu(x):
    return jax.nn.silu(x)

def _sigmoid(x):
    return jax.nn.sigmoid(x)

def _layernorm(x, axis=-1, eps=1e-05):
    m = jnp.mean(x, axis=axis, keepdims=True)
    v = jnp.var(x, axis=axis, keepdims=True)
    return (x - m) / jnp.sqrt(v + eps)

def _scatter_add(tgt, idx, src, axis=0):
    return tgt.at[idx].add(src)

def _segment_sum(src, seg, n):
    return jax.ops.segment_sum(src, seg, n)
kernel_name = 'mk_decoder_preln_d1_seqx_r4_8d1f09'

def setup_inputs(seed: int=0):
    np.random.seed(seed)
    _w = jnp.asarray

    def _rec_inputs():
        import jax
        import jax.numpy as jnp
        _rk = jax.random.key(seed)
        x = -0.0003929 + 0.9999 * jax.random.normal(jax.random.fold_in(_rk, 1), (32, 112, 512), jnp.float32)
        _lenS = 112 - jax.random.randint(jax.random.fold_in(_rk, 7), (32,), 0, max(1, 112 // 4) + 1, jnp.int32)
        _lenS2 = 375 - jax.random.randint(jax.random.fold_in(_rk, 8), (32,), 0, max(1, 375 // 4) + 1, jnp.int32)
        _ctx_1024P = jax.random.normal(jax.random.fold_in(_rk, 11), (32, 16, 256), jnp.float32)
        _ctx_1024c = jax.random.dirichlet(jax.random.fold_in(_rk, 511), 0.3 * jnp.ones((16,), jnp.float32), (32, 375))
        _ctx_1024t = jnp.einsum('bsk,bkd->bsd', _ctx_1024c, _ctx_1024P)
        _ctx_1024t = _ctx_1024t * jax.lax.rsqrt(jnp.mean(jnp.square(_ctx_1024t)) + 1e-12) * 0.953939
        ctx_1024 = -0.000494167 + 1.00018 * (_ctx_1024t + 0.3 * jax.random.normal(jax.random.fold_in(_rk, 611), (32, 375, 256), jnp.float32))
        _validS = jnp.arange(112)[None, :] < _lenS[:, None]
        _validS2 = jnp.arange(375)[None, :] < _lenS2[:, None]
        _causal = jnp.tril(jnp.ones((112, 112), dtype=bool))
        mask_BxS2_bf1 = jnp.ones((32, 375), dtype=bool)
        return (x, ctx_1024, mask_BxS2_bf1)
    x, ctx_1024, mask_BxS2_bf1 = _rec_inputs()

    def _L0_attn_setup():
        import jax, jax.numpy as jnp
        import numpy as np
        EMBED_DIM = 512
        NUM_HEADS = 16
        HEAD_DIM = EMBED_DIM // NUM_HEADS
        NUM_KV_GROUPS = 2
        WINDOW = 64
        KV_DIM = NUM_KV_GROUPS * HEAD_DIM
        key = jax.random.key(seed)
        ks = jax.random.split(key, 9)
        B, L, C = (2, 1024, EMBED_DIM)
        s = 1.0 / np.sqrt(C)
        return {'x': jax.random.normal(ks[0], (B, L, C), dtype=jnp.float32), 'Wq': jax.random.normal(ks[1], (C, C), dtype=jnp.float32) * s, 'bq': jnp.zeros((C,), dtype=jnp.float32), 'Wk': jax.random.normal(ks[2], (C, KV_DIM), dtype=jnp.float32) * s, 'bk': jnp.zeros((KV_DIM,), dtype=jnp.float32), 'Wv': jax.random.normal(ks[3], (C, KV_DIM), dtype=jnp.float32) * s, 'bv': jnp.zeros((KV_DIM,), dtype=jnp.float32), 'Wo': jax.random.normal(ks[4], (C, C), dtype=jnp.float32) * s, 'bo': jnp.zeros((C,), dtype=jnp.float32)}
    _L0_attn_all = _L0_attn_setup()
    _L0_attn_in = {k: v for k, v in _L0_attn_all.items() if k in ('Wq', 'bq', 'Wk', 'bk', 'Wv', 'bv', 'Wo', 'bo')}
    del _L0_attn_all

    def _L0_xattn_setup():
        import jax, jax.numpy as jnp
        import numpy as np
        N_HEADS = 16
        N_KV_HEADS = 8
        HEAD_DIM = 128
        D_TEXT = 512
        D_VISION = 256
        GROUPS = N_HEADS // N_KV_HEADS
        key = jax.random.key(seed)
        ks = jax.random.split(key, 6)
        B, T_text, T_vis = (4, 512, 144)
        text_hidden = jax.random.normal(ks[0], (B, T_text, D_TEXT), dtype=jnp.float32)
        vision_tokens = jax.random.normal(ks[1], (B, T_vis, D_VISION), dtype=jnp.float32)
        vision_mask = jnp.ones((B, T_vis), dtype=bool)
        s = 0.02
        Wq = jax.random.normal(ks[2], (D_TEXT, N_HEADS * HEAD_DIM), dtype=jnp.float32) * s
        Wk = jax.random.normal(ks[3], (D_VISION, N_KV_HEADS * HEAD_DIM), dtype=jnp.float32) * s
        Wv = jax.random.normal(ks[4], (D_VISION, N_KV_HEADS * HEAD_DIM), dtype=jnp.float32) * s
        Wo = jax.random.normal(ks[5], (N_HEADS * HEAD_DIM, D_TEXT), dtype=jnp.float32) * s
        return {'text_hidden': text_hidden, 'vision_tokens': vision_tokens, 'vision_mask': vision_mask, 'Wq': Wq, 'Wk': Wk, 'Wv': Wv, 'Wo': Wo}
    _L0_xattn_all = _L0_xattn_setup()
    _L0_xattn_in = {k: v for k, v in _L0_xattn_all.items() if k in ('Wq', 'Wk', 'Wv', 'Wo')}
    del _L0_xattn_all

    def _L0_ffn_setup():
        import jax, jax.numpy as jnp
        import numpy as np
        B, S, H, E = (4, 512, 512, 8)
        key = jax.random.key(seed)
        k_x, k_wg, k_w, k_b = jax.random.split(key, 4)
        x = jax.random.normal(k_x, (B, S, H), dtype=jnp.float32)
        wg = jax.random.normal(k_wg, (H, E), dtype=jnp.float32) * (1.0 / np.sqrt(H))
        W = jax.random.normal(k_w, (E, H, H), dtype=jnp.float32) * (1.0 / np.sqrt(H))
        b = jax.random.normal(k_b, (E, H), dtype=jnp.float32) * 0.01
        return {'x': x, 'wg': wg, 'W': W, 'b': b}
    _L0_ffn_all = _L0_ffn_setup()
    _L0_ffn_in = {k: v for k, v in _L0_ffn_all.items() if k in ('wg', 'W', 'b')}
    del _L0_ffn_all
    return {'x': x, 'ctx_1024': ctx_1024, 'mask_BxS2_bf1': mask_BxS2_bf1, 'L0_attn_Wq': _L0_attn_in['Wq'], 'L0_attn_bq': _L0_attn_in['bq'], 'L0_attn_Wk': _L0_attn_in['Wk'], 'L0_attn_bk': _L0_attn_in['bk'], 'L0_attn_Wv': _L0_attn_in['Wv'], 'L0_attn_bv': _L0_attn_in['bv'], 'L0_attn_Wo': _L0_attn_in['Wo'], 'L0_attn_bo': _L0_attn_in['bo'], 'L0_xattn_Wq': _L0_xattn_in['Wq'], 'L0_xattn_Wk': _L0_xattn_in['Wk'], 'L0_xattn_Wv': _L0_xattn_in['Wv'], 'L0_xattn_Wo': _L0_xattn_in['Wo'], 'L0_ffn_wg': _L0_ffn_in['wg'], 'L0_ffn_W': _L0_ffn_in['W'], 'L0_ffn_b': _L0_ffn_in['b']}

def reference(x, ctx_1024, mask_BxS2_bf1, L0_attn_Wq, L0_attn_bq, L0_attn_Wk, L0_attn_bk, L0_attn_Wv, L0_attn_bv, L0_attn_Wo, L0_attn_bo, L0_xattn_Wq, L0_xattn_Wk, L0_xattn_Wv, L0_xattn_Wo, L0_ffn_wg, L0_ffn_W, L0_ffn_b):
    import jax
    import jax.numpy as jnp

    def _L0_attn_ref(x, Wq, bq, Wk, bk, Wv, bv, Wo, bo):
        import jax, jax.numpy as jnp
        import numpy as np
        EMBED_DIM = 512
        NUM_HEADS = 16
        HEAD_DIM = EMBED_DIM // NUM_HEADS
        NUM_KV_GROUPS = 2
        WINDOW = 64
        KV_DIM = NUM_KV_GROUPS * HEAD_DIM
        B, L, C = x.shape
        W = WINDOW
        H, G, D = (NUM_HEADS, NUM_KV_GROUPS, HEAD_DIM)
        R = H // G
        pad_l = (W - L % W) % W
        xp = jnp.pad(x, ((0, 0), (0, pad_l), (0, 0)))
        Lp = xp.shape[1]
        q = (xp @ Wq + bq).reshape(B, Lp, H, D).transpose(0, 2, 1, 3)
        k = (xp @ Wk + bk).reshape(B, Lp, G, D).transpose(0, 2, 1, 3)
        v = (xp @ Wv + bv).reshape(B, Lp, G, D).transpose(0, 2, 1, 3)
        num_windows = (Lp - W) // (W // 2) + 1
        starts = jnp.arange(num_windows) * (W // 2)
        idx = starts[:, None] + jnp.arange(W)
        qw = q[:, :, idx, :]
        kw = k[:, :, idx, :]
        vw = v[:, :, idx, :]
        qg = qw.reshape(B, R, G, num_windows, W, D)
        scale = 1.0 / np.sqrt(D)
        scores = jnp.einsum('brgnqd,bgnkd->brgnqk', qg, kw) * scale
        attn = jax.nn.softmax(scores, axis=-1)
        og = jnp.einsum('brgnqk,bgnkd->brgnqd', attn, vw)
        o = og.reshape(B, H, num_windows, W, D)
        o = o.transpose(0, 2, 3, 1, 4).reshape(B, num_windows * W, H * D)
        o = o[:, :L, :]
        return o @ Wo + bo

    def _L0_xattn_ref(text_hidden, vision_tokens, vision_mask, Wq, Wk, Wv, Wo):
        import jax, jax.numpy as jnp
        import numpy as np
        N_HEADS = 16
        N_KV_HEADS = 8
        HEAD_DIM = 128
        D_TEXT = 512
        D_VISION = 256
        GROUPS = N_HEADS // N_KV_HEADS
        B, T_text, _ = text_hidden.shape
        T_vis = vision_tokens.shape[1]
        scale = jnp.float32(np.sqrt(HEAD_DIM))
        q = (text_hidden @ Wq).reshape(B, T_text, N_HEADS, HEAD_DIM).transpose(0, 2, 1, 3)
        k = (vision_tokens @ Wk).reshape(B, T_vis, N_KV_HEADS, HEAD_DIM).transpose(0, 2, 1, 3)
        v = (vision_tokens @ Wv).reshape(B, T_vis, N_KV_HEADS, HEAD_DIM).transpose(0, 2, 1, 3)
        k = jnp.repeat(k, GROUPS, axis=1)
        v = jnp.repeat(v, GROUPS, axis=1)
        scores = jnp.einsum('bhtd,bhsd->bhts', q, k) / scale
        mask = vision_mask[:, None, None, :]
        scores = jnp.where(mask, scores, -jnp.inf)
        attn = jax.nn.softmax(scores, axis=-1)
        attn = jnp.nan_to_num(attn, nan=0.0)
        out = jnp.einsum('bhts,bhsd->bhtd', attn, v)
        out = out.transpose(0, 2, 1, 3).reshape(B, T_text, N_HEADS * HEAD_DIM)
        return out @ Wo

    def _L0_ffn_ref(x, wg, W, b):
        import jax, jax.numpy as jnp
        import numpy as np
        B, S, H, E = (4, 512, 512, 8)
        Bv, Sv, Hv = x.shape
        Ev = W.shape[0]
        xt = x.reshape(-1, Hv)
        logits = xt @ wg
        probs = jax.nn.softmax(logits, axis=-1)
        idx = jnp.argmax(probs, axis=-1)
        gate = jnp.take_along_axis(probs, idx[:, None], axis=1)
        onehot = jax.nn.one_hot(idx, Ev, dtype=x.dtype)
        expert_out = jnp.einsum('nh,eoh->neo', xt, W) + b[None, :, :]
        combine = onehot * gate
        out = jnp.einsum('ne,neo->no', combine, expert_out)
        return out.reshape(Bv, Sv, Hv)
    x = x + _L0_attn_ref(_layernorm(x, axis=-1), L0_attn_Wq, L0_attn_bq, L0_attn_Wk, L0_attn_bk, L0_attn_Wv, L0_attn_bv, L0_attn_Wo, L0_attn_bo)
    x = x + _L0_xattn_ref(_layernorm(x, axis=-1), ctx_1024, mask_BxS2_bf1, L0_xattn_Wq, L0_xattn_Wk, L0_xattn_Wv, L0_xattn_Wo)
    x = x + _L0_ffn_ref(_layernorm(x, axis=-1), L0_ffn_wg, L0_ffn_W, L0_ffn_b)
    return x

_drawn_inputs = setup_inputs


def setup_inputs(seed=0):
    import zlib

    import numpy as np

    out = dict(_drawn_inputs(seed))
    spreads = {'L0_attn_bq': (0.0, 0.1),
     'L0_attn_bk': (0.0, 0.8),
     'L0_attn_bv': (0.0, 0.1),
     'L0_attn_bo': (0.0, 0.1)}
    factors = {'L0_xattn_Wq': 2.68, 'L0_ffn_b': 8.0}
    for name, (base, spread) in spreads.items():
        noise = np.random.default_rng([zlib.crc32(name.encode()), seed]).standard_normal(out[name].shape)
        drawn = base * np.exp(spread * noise) if base else spread * noise
        out[name] = jnp.asarray(drawn.astype(out[name].dtype))
    for name, factor in factors.items():
        out[name] = (out[name] * factor).astype(out[name].dtype)
    return out
```

```python
from contextlib import ExitStack, contextmanager

import numpy as np

import concourse.bass as bass
from concourse import mybir

F32 = mybir.dt.float32
F32R = mybir.dt.float32r
I32 = mybir.dt.int32
U32 = mybir.dt.uint32
ALU = mybir.AluOpType
ACT = mybir.ActivationFunctionType
AX = mybir.AxisListType
P = 128
HI, LO = 0, 1
PASSES = ((HI, HI), (HI, LO), (LO, HI))
NEG = 1.0e30


class Turn:

    def __init__(self, at, reg=None):
        self.at, self.reg = at, reg

    def count(self, per, more):
        if self.reg is None:
            return self.at * per + more
        return self.reg * per + (self.at * per + more)

    def before(self):
        return Turn(self.at - 1, self.reg)


def make_identity(pool, tile, done):
    pool.memset(tile, 0.0).then_inc(done, 1)
    pool.wait_ge(done, 1)
    pool.affine_select(out=tile, in_=tile, compare_op=ALU.not_equal, fill=1.0, base=0,
                       pattern=[[-1, tile.shape[-1]]], channel_multiplier=1).then_inc(done, 1)


@contextmanager
def semaphores(nc, phase):
    used = []

    def sem(name):
        used.append(nc.alloc_semaphore(name=f"{phase}_{name}"))
        return used[-1]

    yield sem
    nc.clear_and_free_semaphores(used)
    nc.all_engine_barrier()


class Fills:

    def __init__(self, head, first, full, last, tail, turns, banks):
        self.lists = {"head": head, "first": first, "full": full, "last": last, "tail": tail}
        self.turns, self.banks = turns, banks
        assert len(self.flat("full")) % banks == 0

    def flat(self, which):
        steps = self.lists[which]
        return [f for fs in steps for f in fs]

    def which(self, turn):
        if turn.reg is None and turn.at < 0:
            return "head"
        if turn.reg is None and turn.at == 0:
            return "first"
        if turn.reg is None and turn.at == self.turns:
            return "tail"
        return "last" if turn.reg is None and turn.at == self.turns - 1 else "full"

    def before(self, turn, kinds=None):
        def number(which):
            return sum(kinds is None or f[0] in kinds for f in self.flat(which))

        which = self.which(turn)
        if which == "head":
            return 0
        if which == "first":
            return number("head")
        if which == "tail":
            return self.before(Turn(self.turns - 1), kinds) + number("last")
        return turn.count(number("full"), number("head") + number("first") - number("full"))

    def until(self, turn, fill, kinds=None):
        flat = self.flat(self.which(turn))
        n = flat.index(fill) + 1
        return self.before(turn, kinds) + sum(kinds is None or f[0] in kinds for f in flat[:n])

    def bank(self, turn, fill):
        base = self.before(Turn(1) if turn.reg is not None else turn)
        return (base + self.flat(self.which(turn)).index(fill)) % self.banks

    def free(self, turn, fill):
        if turn.reg is None and self.until(turn, fill) <= self.banks:
            return 0
        return self.until(turn, fill) - self.banks


def window_attention(nc, B, T, x, Wq, bq, Wk, bk, Wv, bv, Wo, bo, x1, h2T):
    C = x.shape[2]
    KC = C // P
    WIN, D = 64, 32
    HEADS = C // D
    R0, R1 = WIN, T - WIN
    QT, KT = WIN // 2 + R1, WIN // 2 + WIN
    TB = 4
    TURNS = B // TB
    SCALE = float(1.0 / np.sqrt(D))
    EPS = 1e-5

    KQ = [("K", 0)] + [("Q", m) for m in range(KC)]
    HEAD = [[("N", s) for s in range(TB)] + KQ]
    FULL = [
        [("V", 0), ("O", 0), ("A", 0), ("W", 0), ("W", 1), ("M", 0), ("N", 0)],
        [("O", 1), ("A", 1), ("M", 1), ("N", 1)],
        [("O", 2), ("A", 2), ("M", 2), ("N", 2)],
        [("N", 3), ("O", 3), KQ[0], ("A", 3)] + KQ[1:] + [("M", 3)],
    ]
    FIRST = [[f for f in fs if not (f[0] == "A" and s < 1 or f[0] == "O" and s < 2 or f[0] == "M" and s < 3)]
             for s, fs in enumerate(FULL)]
    LAST = [[f for f in fs if f[0] not in "NKQ"] for fs in FULL]
    TAIL = [[("O", 0), ("A", 0), ("M", 0)], [("O", 1), ("M", 1)], [("M", 2)]]
    fills = Fills(HEAD, FIRST, FULL, LAST, TAIL, TURNS, 4)
    AHEAD = [[0, 1], [2], [3], []]
    HALVED = "KQVWANM"

    def back(turn, s, n):
        return (turn, s - n) if s >= n else (turn.before(), s - n + TB)

    with ExitStack() as stack:
        def sb(name, shape, dt=F32):
            return stack.enter_context(nc.sbuf_tensor(f"w_{name}", shape, dt))

        sem = stack.enter_context(semaphores(nc, "w"))

        wq = sb("wq", [P, 2, KC, C], F32R)
        wk = sb("wk", [P, 2, KC, P], F32R)
        wv = sb("wv", [P, 2, KC, P], F32R)
        wo = sb("wo", [P, 2, KC, C], F32R)
        stage = sb("stage", [P, 2, 1024])
        bqs, bks, bvs = sb("bqs", [P, KC]), sb("bks", [P, 1]), sb("bvs", [P, 1])
        bos = sb("bos", [T, C])
        ident = sb("ident", [P, P])
        power = sb("power", [P, 1])
        xa = sb("xa", [T, TB, C])
        xr = sb("xr", [T, TB, C])
        h1 = sb("h1", [T, 2, C])
        h2 = sb("h2", [T, 2, C])
        hT = sb("hT", [P, 2, KC, TB, T], F32R)
        qa = sb("qa", [P, 2, KC, TB, T], F32R)
        qb = sb("qb", [P, 2, KC, TB, T], F32R)
        kd = sb("kd", [P, 2, TB, 2, 4 * WIN], F32R)
        vt = sb("vt", [WIN, 2, TB, 2, WIN])
        vd = sb("vd", [P, 2, TB, 2, 2, P], F32R)
        probs = sb("probs", [T, 2, HEADS // 2, WIN])
        pT = sb("pT", [P, 2, HEADS // 2, T], F32R)
        oT = sb("oT", [P, 2, 2, KC, T], F32R)
        hs = sb("hs", [P, 2, 2, KC, 2 * T], F32R)
        top = sb("top", [T, 2, HEADS // 2])
        total = sb("total", [T, 2, HEADS // 2])
        inv = sb("inv", [T, 2, HEADS // 2])
        st1, st2 = sb("st1", [T, 2, 6]), sb("st2", [T, 2, 6])
        mv1, mv2 = sb("mv1", [T, 2, 2]), sb("mv2", [T, 2, 2])
        rs1, rs2 = sb("rs1", [T, 2, 1]), sb("rs2", [T, 2, 1])
        nb1, nb2 = sb("nb1", [T, 2, 1]), sb("nb2", [T, 2, 1])

        def bank(name):
            return stack.enter_context(nc.psum_tensor(f"w_{name}", [P, 512], F32))

        ps_s = [bank(f"ps_s{u}") for u in range(2)]
        ps_t = [bank(f"ps_t{u}") for u in range(2)]
        ps_f = [bank(f"ps_f{n}") for n in range(4)]

        w_in = [sem(f"w_in{n}") for n in range(2)]
        w_hi, w_lo, b_in = sem("w_hi"), sem("w_lo"), sem("b_in")
        ident_done, power_ready, zeroed = sem("ident"), sem("power"), sem("zeroed")
        xa_in = [sem(f"xa_in{s}") for s in range(TB)]
        xr_in = [sem(f"xr_in{s}") for s in range(TB)]
        x1_out = [sem(f"x1_out{s}") for s in range(TB)]
        h2_out = [sem(f"h2_out{s}") for s in range(2)]
        st1_ready, mv1_ready, rs1_ready, h1_ready = sem("st1"), sem("mv1"), sem("rs1"), sem("h1")
        st2_ready, mv2_ready, rs2_ready, h2_ready = sem("st2"), sem("mv2"), sem("rs2"), sem("h2")
        ve1_ready, ve2_ready, pw1_ready, pw2_ready = sem("ve1"), sem("ve2"), sem("pw1"), sem("pw2")
        scores_ready, top_ready, less_ready, exp_ready = sem("scores"), sem("top"), sem("less"), sem("exp")
        total_ready, inv_ready, normed = sem("total"), sem("inv"), sem("normed")
        probsT_ready, pT_hi, pT_lo = sem("probsT"), sem("pT_hi"), sem("pT_lo")
        biased = sem("biased")
        fill_ready, fill_hi, fill_done = sem("fill_ready"), sem("fill_hi"), sem("fill_done")

        half = KC // 2
        stages = []
        for w, dst in ((Wq, wq), (Wo, wo)):
            for n in range(2):
                stages.append(([(w[n * half * P:(n + 1) * half * P, :].rearrange("(c p) n -> p c n", p=P), None)],
                               [dst[:, a, n * half:(n + 1) * half, :] for a in (HI, LO)], half))
        kv = 2 * D
        kv_src = [(w.rearrange("(c p) n -> p c n", p=P), (j, e)) for j, w in enumerate((Wk, Wv)) for e in range(2)]
        N_KV = 2

        def staged(n, c):
            return stage[:, n % 2, :].rearrange("p (c n) -> p c n", c=c)

        plan = [stages[0], stages[1], "kv", stages[2], stages[3]]

        with nc.Block() as block:
            loop = TURNS - 2

            @block.sync
            def _(sp):
                def row(turn, s):
                    n = turn.count(TB, s)
                    return sp.snap(n) if turn.reg is not None else n

                def load_xa(turn, s, free):
                    n = row(turn, s)
                    if free is not None:
                        sp.wait_ge(h1_ready, free)
                        sp.nop(nofuse=True)
                    sp.dma_start(xa[:, s, :], x[bass.ds(n, 1)].rearrange("a t c -> (a t) c")).then_inc(xa_in[s], 16)

                def load_xr(turn, s):
                    n = row(turn, s)
                    if not (turn.reg is None and turn.at == 0):
                        sp.wait_ge(h2_ready, turn.count(TB, s + 1 - TB))
                        sp.nop(nofuse=True)
                        sp.wait_ge(x1_out[s], turn.count(16, 0))
                        sp.nop(nofuse=True)
                    sp.dma_start(xr[:, s, :], x[bass.ds(n, 1)].rearrange("a t c -> (a t) c")).then_inc(xr_in[s], 16)

                for s in range(TB):
                    load_xa(Turn(0), s, None)
                for n, what in enumerate(plan):
                    if n >= 2:
                        sp.wait_ge(w_lo, n - 1)
                    if what == "kv":
                        for src, (j, e) in kv_src:
                            at = staged(n, 2 * KC)[:, j * KC:(j + 1) * KC, e * kv:(e + 1) * kv]
                            sp.dma_start(at, src).then_inc(w_in[n % 2], 16)
                    else:
                        sp.dma_start(staged(n, half), what[0][0][0]).then_inc(w_in[n % 2], 16)
                for c in range(KC):
                    sp.dma_start(bqs[:, c:c + 1], bq[c * P:(c + 1) * P].rearrange("(p a) -> p a", a=1)) \
                        .then_inc(b_in, 16)
                for e in range(2):
                    sp.dma_start(bks[e * kv:(e + 1) * kv, :], bk.rearrange("(p a) -> p a", a=1)).then_inc(b_in, 16)
                    sp.dma_start(bvs[e * kv:(e + 1) * kv, :], bv.rearrange("(p a) -> p a", a=1)).then_inc(b_in, 16)
                sp.dma_start(bos[:], bo.rearrange("(a n) -> a n", a=1).to_broadcast([T, C])).then_inc(b_in, 16)

                def store_x1(turn, s, at, f):
                    n = turn.count(TB, s)
                    n = sp.snap(n) if turn.reg is not None else n
                    sp.wait_ge(fill_done, fills.until(at, f))
                    sp.nop(nofuse=True)
                    sp.dma_start(x1[bass.ds(n, 1)].rearrange("a t c -> (a t) c"), xr[:, s, :]).then_inc(x1_out[s], 16)

                def store_h2(turn, s, at, f):
                    t = turn.count(TB * T, (s - 1) * T)
                    t = sp.snap(t) if turn.reg is not None else t
                    sp.wait_ge(fill_done, fills.until(at, f))
                    sp.nop(nofuse=True)
                    for a in (HI, LO):
                        sp.dma_start(h2T[a, :, :, bass.ds(t, 2 * T)].rearrange("c p t -> p c t"),
                                      hs[:, s // 2, a].bitcast(F32)).then_inc(h2_out[s // 2], 16)

                def stores(turn, s, fs):
                    for f in fs:
                        if f[0] == "O":
                            store_x1(*back(turn, s, 2), turn, f)
                        if f[0] == "M" and (s - 3) % 2:
                            store_h2(*back(turn, s, 3), turn, f)

                def turn_of(turn, last=False):
                    for s, fs in enumerate(fills.lists[fills.which(turn)]):
                        if s == 0 and not last:
                            for n in range(TB):
                                load_xa(Turn(turn.at + 1, turn.reg), n, turn.count(TB, n + 1))
                        load_xr(turn, s)
                        stores(turn, s, fs)

                turn_of(Turn(0))
                with sp.Fori(0, loop) as j:
                    turn_of(Turn(1, j))
                turn_of(Turn(TURNS - 1), last=True)
                for s, fs in enumerate(TAIL):
                    stores(Turn(TURNS), s, fs)
                for s in range(TB):
                    sp.wait_ge(x1_out[s], 16 * TURNS)
                for s in range(2):
                    sp.wait_ge(h2_out[s], 32 * TURNS)

            B_ALL = 16 * (KC + 5)

            @block.gpsimd
            def _(pool):
                make_identity(pool, ident[:], ident_done)
                pool.wait_ge(power_ready, 1)

                def factors(turn, s, mv, rs, nb, mv_ready, ve_ready, pw_ready, rs_ready):
                    par = s % 2
                    pool.wait_ge(mv_ready, turn.count(TB, s + 1))
                    pool.nop(nofuse=True)
                    pool.tensor_scalar(rs[:, par, :], mv[:, par, 1:2], EPS, None, ALU.add).then_inc(ve_ready, 1)
                    pool.wait_ge(ve_ready, turn.count(TB, s + 1))
                    pool.nop(nofuse=True)
                    pool.tensor_tensor(rs[:, par, :], rs[:, par, :], power[0:T, :], ALU.pow).then_inc(pw_ready, 1)
                    pool.wait_ge(pw_ready, turn.count(TB, s + 1))
                    pool.nop(nofuse=True)
                    pool.tensor_scalar(nb[:, par, :], mv[:, par, 0:1], rs[:, par, :], -1.0, ALU.mult, ALU.mult) \
                        .then_inc(rs_ready, 1)

                def factors1(turn, s):
                    factors(turn, s, mv1, rs1, nb1, mv1_ready, ve1_ready, pw1_ready, rs1_ready)

                def factors2(turn, s):
                    factors(turn, s, mv2, rs2, nb2, mv2_ready, ve2_ready, pw2_ready, rs2_ready)

                def add_bias(turn, s):
                    pool.wait_ge(xr_in[s], turn.count(16, 16))
                    pool.nop(nofuse=True)
                    pool.tensor_tensor(xr[:, s, :], xr[:, s, :], bos[:], ALU.add).then_inc(biased, 1)

                def normalise(turn, s):
                    for u in range(2):
                        pool.wait_ge(inv_ready, turn.count(8, 2 * s + u + 1))
                        pool.nop(nofuse=True)
                        pool.tensor_tensor(probs[:, u], probs[:, u],
                                           inv[:, u, :].unsqueeze(2).to_broadcast([T, HEADS // 2, WIN]),
                                           ALU.mult).then_inc(normed, 1)

                def turn_of(turn, last=False):
                    first = turn.reg is None and turn.at == 0
                    for s in range(TB):
                        if not last:
                            for n in AHEAD[s]:
                                factors1(Turn(turn.at + 1, turn.reg), n)
                        normalise(turn, s)
                        if not (first and s < 1):
                            add_bias(*back(turn, s, 1))
                        if not (first and s < 2):
                            factors2(*back(turn, s, 2))

                for s in range(TB):
                    factors1(Turn(0), s)
                for tile in (kd, vd):
                    for a in (HI, LO):
                        last = pool.memset(tile[:, a].bitcast(F32), 0.0)
                last.then_inc(zeroed, 1)
                pool.wait_ge(b_in, B_ALL)
                turn_of(Turn(0))
                with pool.Fori(0, loop) as j:
                    turn_of(Turn(1, j))
                turn_of(Turn(TURNS - 1), last=True)
                add_bias(Turn(TURNS - 1), TB - 1)
                factors2(Turn(TURNS - 1), 2)
                factors2(Turn(TURNS - 1), 3)

            def places(f, b):
                kind, n = f
                if kind == "K":
                    src = b[:, 0:TB * KT].rearrange("p (b t) -> p b t", b=TB)
                    return [(src[D * j:D * (j + 1), :, 32 * w:32 * w + WIN],
                             *[kd[D * j:D * (j + 1), a, :, w, WIN * j:WIN * (j + 1)] for a in (HI, LO)],
                             bks[D * j:D * (j + 1), :]) for w in range(2) for j in range(4)]
                if kind == "Q":
                    src = b[:, 0:TB * QT].rearrange("p (b t) -> p b t", b=TB)
                    return [(src[:, :, 0:R0], *[qa[:, a, n, :, 0:R0] for a in (HI, LO)], bqs[:, n:n + 1]),
                            (src[:, :, WIN // 2:QT], *[qb[:, a, n, :, R0:T] for a in (HI, LO)], bqs[:, n:n + 1])]
                if kind == "W":
                    src = b[:, 0:TB * WIN].rearrange("p (b t) -> p b t", b=TB)
                    return [(src[WIN * g:WIN * (g + 1), :, D * g:D * (g + 1)],
                             *[vd[WIN * g:WIN * (g + 1), a, :, n, q, WIN * q + D * g:WIN * q + D * (g + 1)]
                               for a in (HI, LO)], None) for q in range(2) for g in range(2)]
                src = b[:, 0:KC * T].rearrange("p (c t) -> p c t", c=KC)
                if kind == "N":
                    return [(src, *[hT[:, a, :, n, :] for a in (HI, LO)], None)]
                if kind == "A":
                    par = (n - 1) % 2
                    return [(src, *[oT[:, par, a] for a in (HI, LO)], None)]
                batch = (n - 3) % TB
                return [(src, *[hs[:, batch // 2, a, :, (batch % 2) * T:(batch % 2 + 1) * T] for a in (HI, LO)], None)]

            @block.scalar
            def _(act):
                def fill(turn, f):
                    b = ps_f[fills.bank(turn, f)]
                    act.wait_ge(fill_ready, fills.until(turn, f))
                    if f[0] == "V":
                        src = b[0:WIN, 0:TB * KT].rearrange("p (b t) -> p b t", b=TB)[:, :, 0:WIN]
                        for e in range(2):
                            last = act.activation(vt[:, 0, :, e, :], src, ACT.Identity, bias=bvs[0:WIN, :])
                        last.then_inc(fill_hi, 1)
                        return
                    if f[0] == "M" and f[1] % 2 and not (turn.reg is None and turn.at == 0):
                        act.wait_ge(h2_out[((f[1] - 3) % TB) // 2], turn.count(32, 0) if f[1] == 3 else turn.count(32, -32))
                    for src, hi, lo, bias in places(f, b):
                        if bias is None:
                            last = act.activation(hi, src, ACT.Copy)
                        else:
                            last = act.activation(hi, src, ACT.Identity, bias=bias)
                    last.then_inc(fill_hi, 1)

                def probsT(turn, s):
                    for u in range(2):
                        act.wait_ge(probsT_ready, turn.count(8, 2 * s + u + 1))
                        act.activation(pT[:, HI, 4 * u:4 * u + 4, :],
                                       ps_t[u][:, 0:4 * T].rearrange("p (c t) -> p c t", c=4), ACT.Copy) \
                            .then_inc(pT_hi, 1)

                def exps(turn, s):
                    for u in range(2):
                        act.wait_ge(less_ready, turn.count(8, 2 * s + u + 1))
                        act.activation(probs[:, u], probs[:, u], ACT.Exp, scale=SCALE).then_inc(exp_ready, 1)

                def norm(turn, s, xin, rs, nb, h, rs_ready, free, done):
                    par = s % 2
                    act.wait_ge(rs_ready, turn.count(TB, s + 1))
                    if free is not None:
                        act.wait_ge(fill_ready, free)
                    act.activation(h[:, par, :], xin[:, s, :], ACT.Identity, bias=nb[:, par, :], scale=rs[:, par, :]) \
                        .then_inc(done, 1)

                def norm1(turn, s):
                    at = turn.before()
                    if at.reg is None and at.at < 0:
                        free = fills.until(at, ("N", s - 2)) if s >= 2 else None
                    elif s >= 2:
                        free = fills.until(at, ("N", s - 2))
                    else:
                        free = fills.until(at.before(), ("N", s + 2))
                    norm(turn, s, xa, rs1, nb1, h1, rs1_ready, free, h1_ready)

                def norm2(turn, s):
                    first = turn.reg is None and turn.at == 0
                    at, step = (turn, s + 1) if s + 1 < TB else (Turn(turn.at + 1, turn.reg), 0)
                    free = None if first and s < 2 else fills.until(at, ("M", step))
                    norm(turn, s, xr, rs2, nb2, h2, rs2_ready, free, h2_ready)

                def step(turn, s, fs, kinds):
                    first = turn.reg is None and turn.at == 0
                    if "T" in kinds and not (first and s < 1):
                        probsT(*back(turn, s, 1))
                    if not (first and s < 3):
                        norm2(*back(turn, s, 3))
                    if "S" in kinds:
                        exps(turn, s)
                    if "N" in [f[0] for f in fs]:
                        for n in AHEAD[s]:
                            norm1(Turn(turn.at + 1, turn.reg), n)
                    for f in fs:
                        if f[0] in HALVED:
                            fill(turn, f)

                def turn_of(turn):
                    for s, fs in enumerate(fills.lists[fills.which(turn)]):
                        step(turn, s, fs, "TS")

                norm1(Turn(0), 0)
                norm1(Turn(0), 1)
                for n in range(TB):
                    fill(Turn(-1), ("N", n))
                    if n + 2 < TB:
                        norm1(Turn(0), n + 2)
                for n, what in enumerate(plan):
                    act.wait_ge(w_in[n % 2], {0: 16, 1: 16, 2: 16 + 16 * len(kv_src), 3: 32, 4: 32 + 16 * len(kv_src)}[n])
                    if what == "kv":
                        act.activation(wk[:, HI], staged(n, 2 * KC)[:, 0:KC], ACT.Copy)
                        act.activation(wv[:, HI], staged(n, 2 * KC)[:, KC:2 * KC], ACT.Copy).then_inc(w_hi, 1)
                    else:
                        act.activation(what[1][HI], staged(n, half), ACT.Copy).then_inc(w_hi, 1)
                act.wait_ge(b_in, B_ALL)
                act.wait_ge(zeroed, 2)
                for f in KQ:
                    fill(Turn(-1), f)
                turn_of(Turn(0))
                with act.Fori(0, loop) as j:
                    turn_of(Turn(1, j))
                turn_of(Turn(TURNS - 1))
                for s, fs in enumerate(TAIL):
                    step(Turn(TURNS), s, fs, "T" if s == 0 else "")

            @block.vector
            def _(dve):
                dve.memset(power[:], -0.5).then_inc(power_ready, 1)

                def stats(turn, s, xin, st, mv, st_ready, mv_ready):
                    dve.bn_stats(st[:, s % 2, :], xin[:, s, :]).then_inc(st_ready, 1)
                    dve.wait_ge(st_ready, turn.count(TB, s + 1))
                    dve.nop(nofuse=True)
                    dve.bn_aggr(mv[:, s % 2, :], st[:, s % 2, :]).then_inc(mv_ready, 1)

                def stats1(turn, s):
                    dve.wait_ge(xa_in[s], turn.count(16, 16))
                    if not (turn.reg is None and turn.at == 0 and s < 2):
                        dve.wait_ge(h1_ready, turn.count(TB, s - 1))
                    stats(turn, s, xa, st1, mv1, st1_ready, mv1_ready)

                def fill(turn, f):
                    b = ps_f[fills.bank(turn, f)]
                    dve.wait_ge(fill_hi, fills.until(turn, f, HALVED))
                    if f[0] == "V":
                        src = b[0:WIN, 0:TB * KT].rearrange("p (b t) -> p b t", b=TB)[:, :, WIN // 2:WIN // 2 + WIN]
                        for e in range(2):
                            last = dve.tensor_scalar(vt[:, 1, :, e, :], src, bvs[0:WIN, :], None, ALU.add)
                        last.then_inc(fill_done, 1)
                        return
                    for src, hi, lo, bias in places(f, b):
                        if bias is None:
                            last = dve.tensor_tensor(lo, src, hi.bitcast(F32), ALU.subtract)
                        else:
                            last = dve.scalar_tensor_tensor(out=lo, in0=src, scalar=bias, in1=hi.bitcast(F32),
                                                            op0=ALU.add, op1=ALU.subtract)
                    last.then_inc(fill_done, 1)

                def probsT(turn, s):
                    for u in range(2):
                        dve.wait_ge(pT_hi, turn.count(8, 2 * s + u + 1))
                        dve.tensor_tensor(pT[:, LO, 4 * u:4 * u + 4, :],
                                          ps_t[u][:, 0:4 * T].rearrange("p (c t) -> p c t", c=4),
                                          pT[:, HI, 4 * u:4 * u + 4, :].bitcast(F32), ALU.subtract) \
                            .then_inc(pT_lo, 1)

                def less_top(turn, s):
                    for u in range(2):
                        n = turn.count(8, 2 * s + u + 1)
                        scores = ps_s[u][0:T, :].rearrange("p (h k) -> p h k", k=WIN)
                        dve.wait_ge(scores_ready, n)
                        dve.tensor_reduce(top[:, u, :], scores, AX.X, ALU.max).then_inc(top_ready, 1)
                        dve.wait_ge(top_ready, n)
                        if not (turn.reg is None and turn.at == 0 and s == 0):
                            dve.wait_ge(probsT_ready, turn.count(8, 2 * s + u - 1))
                        dve.tensor_tensor(probs[:, u], scores,
                                          top[:, u, :].unsqueeze(2).to_broadcast([T, HEADS // 2, WIN]),
                                          ALU.subtract).then_inc(less_ready, 1)

                def totals(turn, s):
                    for u in range(2):
                        n = turn.count(8, 2 * s + u + 1)
                        dve.wait_ge(exp_ready, n)
                        dve.tensor_reduce(total[:, u, :], probs[:, u], AX.X, ALU.add).then_inc(total_ready, 1)
                        dve.wait_ge(total_ready, n)
                        dve.reciprocal(inv[:, u, :], total[:, u, :]).then_inc(inv_ready, 1)

                def residual(at, f, turn, s):
                    dve.wait_ge(fill_ready, fills.until(at, f))
                    dve.wait_ge(biased, turn.count(TB, s + 1))
                    dve.tensor_tensor(xr[:, s, :], ps_f[fills.bank(at, f)][0:T, :], xr[:, s, :], ALU.add) \
                        .then_inc(fill_done, 1)
                    dve.wait_ge(fill_done, fills.until(at, f))
                    if not (turn.reg is None and turn.at == 0 and s < 2):
                        dve.wait_ge(h2_ready, turn.count(TB, s - 1))
                    dve.bn_stats(st2[:, s % 2, :], xr[:, s, :]).then_inc(st2_ready, 1)
                    dve.wait_ge(st2_ready, turn.count(TB, s + 1))
                    dve.nop(nofuse=True)
                    dve.bn_aggr(mv2[:, s % 2, :], st2[:, s % 2, :]).then_inc(mv2_ready, 1)

                def step(turn, s, fs, kinds):
                    first = turn.reg is None and turn.at == 0
                    if "T" in kinds and not (first and s < 1):
                        probsT(*back(turn, s, 1))
                    if "S" in kinds:
                        less_top(turn, s)
                    if "N" in [f[0] for f in fs]:
                        for n in AHEAD[s]:
                            stats1(Turn(turn.at + 1, turn.reg), n)
                    if "S" in kinds:
                        totals(turn, s)
                    for f in fs:
                        if f[0] == "O":
                            residual(turn, f, *back(turn, s, 2))
                        else:
                            fill(turn, f)

                def turn_of(turn):
                    for s, fs in enumerate(fills.lists[fills.which(turn)]):
                        step(turn, s, fs, "TS")

                for s in range(TB):
                    stats1(Turn(0), s)
                for n in range(TB):
                    fill(Turn(-1), ("N", n))
                for a in (HI, LO):
                    dve.memset(qa[:, a, :, :, R0:T].bitcast(F32), 0.0)
                    last = dve.memset(qb[:, a, :, :, 0:R0].bitcast(F32), 0.0)
                last.then_inc(zeroed, 1)
                for n, what in enumerate(plan):
                    dve.wait_ge(w_hi, n + 1)
                    if what == "kv":
                        dve.tensor_tensor(wk[:, LO], staged(n, 2 * KC)[:, 0:KC], wk[:, HI].bitcast(F32), ALU.subtract)
                        dve.tensor_tensor(wv[:, LO], staged(n, 2 * KC)[:, KC:2 * KC], wv[:, HI].bitcast(F32),
                                          ALU.subtract).then_inc(w_lo, 1)
                    else:
                        dve.tensor_tensor(what[1][LO], staged(n, half), what[1][HI].bitcast(F32), ALU.subtract) \
                            .then_inc(w_lo, 1)
                for f in KQ:
                    fill(Turn(-1), f)
                turn_of(Turn(0))
                with dve.Fori(0, loop) as j:
                    turn_of(Turn(1, j))
                turn_of(Turn(TURNS - 1))
                for s, fs in enumerate(TAIL):
                    step(Turn(TURNS), s, fs, "T" if s == 0 else "")

            @block.tensor
            def _(pe):
                pe.wait_ge(ident_done, 2)

                def product(out, jobs):
                    for m, (w, r) in enumerate(jobs):
                        last = pe.matmul(out, w, r, start=m == 0, stop=m == len(jobs) - 1)
                    return last

                def fill(turn, f):
                    kind, n = f
                    k = fills.free(turn, f)
                    if not (isinstance(k, int) and k == 0):
                        pe.wait_ge(fill_done, k)
                        if turn.reg is not None and (kind in "KOW" or (kind, n) == ("A", 0)):
                            pe.nop(nofuse=True)
                    out = ps_f[fills.bank(turn, f)]
                    if kind in "NM":
                        at, s = (Turn(turn.at + 1, turn.reg), n) if kind == "N" else back(turn, n, 3)
                        h, ready = (h1, h1_ready) if kind == "N" else (h2, h2_ready)
                        pe.wait_ge(ready, at.count(TB, s + 1))
                        for c in range(KC):
                            last = pe.transpose(out[:, c * T:(c + 1) * T], h[:, s % 2, c * P:(c + 1) * P],
                                                ident[0:T, 0:T])
                    elif kind in "KV":
                        w = wk if kind == "K" else wv
                        if kind == "K":
                            pe.wait_ge(fill_done, fills.until(turn, ("N", TB - 1)))
                        last = product(out[:, 0:TB * KT].rearrange("p (b t) -> p b t", b=TB),
                                       [(w[:, a, c, :], hT[:, b_, c, :, 0:KT]) for c in range(KC) for a, b_ in PASSES])
                    elif kind == "Q":
                        last = product(out[:, 0:TB * QT].rearrange("p (b t) -> p b t", b=TB),
                                       [(wq[:, a, c, n * P:(n + 1) * P], hT[:, b_, c, :, 0:QT])
                                        for c in range(KC) for a, b_ in PASSES])
                    elif kind == "W":
                        pe.wait_ge(fill_done, fills.until(turn, ("V", 0)))
                        pe.nop(nofuse=True)
                        for b in range(TB):
                            last = pe.transpose(out[:, b * WIN:(b + 1) * WIN], vt[:, n, b, :, :].rearrange("p e k -> p (e k)"),
                                                ident[0:WIN, 0:WIN])
                    elif kind == "A":
                        at, s = back(turn, n, 1)
                        pe.wait_ge(pT_lo, at.count(8, 2 * s + 2))
                        if s == 0:
                            pe.wait_ge(fill_done, fills.until(at, ("W", 1)))
                        rows = out[:, 0:KC * T].rearrange("p (c t) -> p c t", c=KC)
                        for w, (lo, hi) in enumerate(((0, R0), (R0, T))):
                            last = product(rows[:, :, lo:hi],
                                           [(vd[:, a, s, w, q, :],
                                             pT[:, b_].rearrange("p (c q) t -> p q c t", q=2)[:, q, :, lo:hi])
                                            for q in range(2) for a, b_ in PASSES])
                    else:
                        at, s = back(turn, n, 2)
                        a_turn, a_step = (at, s + 1) if s + 1 < TB else (Turn(at.at + 1, at.reg), 0)
                        pe.wait_ge(fill_done, fills.until(a_turn, ("A", a_step)))
                        last = product(out[0:T, :], [(oT[:, s % 2, a, c, :], wo[:, b_, c, :])
                                                     for c in range(KC) for a, b_ in PASSES])
                    last.then_inc(fill_ready, 1)

                def scores(turn, s):
                    if s == 0:
                        pe.wait_ge(fill_done, fills.until(turn.before(), ("Q", KC - 1)))
                    for u in range(2):
                        if not (turn.reg is None and turn.at == 0 and s == 0):
                            pe.wait_ge(less_ready, turn.count(8, 2 * s + u - 1))
                        for m in range(2 * u, 2 * u + 2):
                            last = product(ps_s[u][0:T, (m % 2) * 4 * WIN:(m % 2 + 1) * 4 * WIN],
                                           [(q[:, a, m, s, :], kd[:, b_, s, w, :])
                                            for w, q in enumerate((qa, qb)) for a, b_ in PASSES])
                        last.then_inc(scores_ready, 1)

                def probsT(turn, s):
                    for u in range(2):
                        pe.wait_ge(normed, turn.count(8, 2 * s + u + 1))
                        if not (turn.reg is None and turn.at == 0 and s == 0):
                            pe.wait_ge(pT_lo, turn.count(8, 2 * s + u - 1))
                        for c in range(4):
                            last = pe.transpose(ps_t[u][:, c * T:(c + 1) * T],
                                                probs[:, u, 2 * c:2 * c + 2, :].rearrange("p h k -> p (h k)"),
                                                ident[0:T, 0:T])
                        last.then_inc(probsT_ready, 1)

                def turn_of(turn):
                    first = turn.reg is None and turn.at == 0
                    for s, fs in enumerate(fills.lists[fills.which(turn)]):
                        if not (first and s < 1):
                            probsT(*back(turn, s, 1))
                        scores(turn, s)
                        for f in fs:
                            fill(turn, f)

                for s in range(TB):
                    fill(Turn(-1), ("N", s))
                pe.wait_ge(zeroed, 2)
                pe.wait_ge(w_lo, len(plan))
                for f in KQ:
                    fill(Turn(-1), f)
                turn_of(Turn(0))
                with pe.Fori(0, loop) as j:
                    turn_of(Turn(1, j))
                turn_of(Turn(TURNS - 1))
                for s, fs in enumerate(TAIL):
                    if s == 0:
                        probsT(Turn(TURNS - 1), TB - 1)
                    for f in fs:
                        fill(Turn(TURNS), f)


def cross_attention(nc, half, B, T, S, h2T, ctx, mask, Wq, Wk, Wv, Wo, part):
    D = 128
    C = h2T.shape[1] * P
    KC = C // P
    CD = ctx.shape[2]
    CC = CD // P
    G = 4
    H = 2 * G
    SE = S + S % 2
    CHUNKS = [(k, min(P, SE - k)) for k in range(0, SE, P)]
    NKC = len(CHUNKS)
    WIDE = NKC * P
    assert 0 < SE - S or S % 2 == 0
    T2 = 2 * T
    TURNS = B // 2
    SCALE = float(1.0 / np.sqrt(D))
    mdt = mask.dtype

    LATE = [("Q", 0, 3), ("K", 0, 3), ("V", 0, 1), ("V", 0, 2)]
    FULL = [
        [("Q", 0, 3), ("K", 1, 0), ("V", 0, 1)],
        [("K", 0, 3), ("V", 0, 2), ("K", 1, 1), ("V", 1, 0)],
        [("O", 0, 0), ("O", 0, 1)],
        [("K", 1, 2), ("C", 0, 0), ("V", 1, 1), ("C", 0, 1)],
        [("K", 1, 3), ("V", 1, 2), ("Q", 0, 0)],
        [("K", 0, 0), ("Q", 0, 1)],
        [("K", 0, 1), ("Q", 0, 2)],
        [("K", 0, 2), ("C", 1, 0), ("V", 0, 0), ("C", 1, 1)],
    ]
    HEAD = [f for f in [("C", 0, 0), ("C", 0, 1)] + [("K", 0, g) for g in range(G)] + [("V", 0, c) for c in range(NKC)] +
            [("C", 1, 0), ("C", 1, 1)] + [("Q", 0, g) for g in range(G)] if f not in LATE]
    FIRST = [[f for f in fs if f[0] != "O"] for fs in FULL]
    LAST = [[f for f in fs if f[0] == "O" or f in LATE or (f[0] in "KV" and f[1] == 1)] for fs in FULL]
    TAIL = [("O", 0, 0), ("O", 0, 1)]
    NF = sum(map(len, FULL))
    NF0 = sum(map(len, FIRST))
    BASE = len(HEAD) + NF0 - NF
    flat = [f for fs in FULL for f in fs]
    flat0 = [f for fs in FIRST for f in fs]
    flatl = [f for fs in LAST for f in fs]

    def fills_until(turn, fill):
        if turn.reg is None and turn.at == -1:
            return HEAD.index(fill) + 1
        if turn.reg is None and turn.at == 0:
            return len(HEAD) + flat0.index(fill) + 1
        if turn.reg is None and turn.at == TURNS - 1:
            return BASE + NF * turn.at + flatl.index(fill) + 1
        return turn.count(NF, BASE + flat.index(fill) + 1)

    def made(turn, fill):
        return fills_until(turn if fill[1] == 1 or fill in LATE else turn.before(), fill)

    def fills_of(turn):
        steps = LAST if turn.at == TURNS - 1 else FIRST if turn.at == 0 and turn.reg is None else FULL
        n, out = 0, []
        for fs in steps:
            row = []
            for f in fs:
                if turn.at == 0 and turn.reg is None:
                    before = len(HEAD) + n
                    row.append((f, before, before % 3))
                else:
                    row.append((f, turn.count(NF, BASE + n), (BASE + n) % 3))
                n += 1
            out.append(row)
        return out

    assert NF % 3 == 0 and BASE >= 0

    with ExitStack() as stack:
        def sb(name, shape, dt=F32):
            return stack.enter_context(nc.sbuf_tensor(f"x{half}_{name}", shape, dt))

        sem = stack.enter_context(semaphores(nc, f"x{half}"))

        wq = sb("wq", [P, 2, KC, H * D], F32R)
        wk = sb("wk", [P, 2, CC, G * D], F32R)
        wv = sb("wv", [P, 2, CC, G * D], F32R)
        wo = sb("wo", [P, 2, H, C], F32R)
        stage = sb("stage", [P, 4, 512])
        ident = sb("ident", [P, P])
        x2 = sb("xT", [P, 2, KC, T2], F32R)
        ctxn = sb("ctxn", [P, 2, NKC, CD])
        ctxT = sb("ctxT", [P, 2, 2, CC, SE], F32R)
        kT = sb("kT", [P, 2, G, SE], F32R)
        v = sb("v", [P, 2, 2, NKC, G * D], F32R)
        qT = sb("qT", [P, 2, H, T2], F32R)
        oT = sb("oT", [P, 2, H, T2], F32R)
        probs = sb("probs", [P, 4, WIDE])
        pT = sb("pT", [P, 2, 2, NKC, T2], F32R)
        mraw = sb("mraw", [T, 2, S], mdt)
        mrow = sb("mrow", [T, 2, SE])
        top = sb("top", [T, 4])
        bias = sb("bias", [T, 4])
        total = sb("total", [T, 4])
        inv = sb("inv", [T, 4])
        ost = sb("ost", [P, 2, 2 * T2])

        def bank(name):
            return stack.enter_context(nc.psum_tensor(f"x{half}_{name}", [P, 512], F32))

        ps_s = [bank(f"ps_s{h}") for h in range(2)]
        ps_t = [bank(f"ps_t{h}") for h in range(2)]
        ps_o = bank("ps_o")
        ps_f = [bank(f"ps_f{n}") for n in range(3)]

        w_in = [sem(f"w_in{n}") for n in range(8)]
        w_hi, w_lo = sem("w_hi"), sem("w_lo")
        ident_done = sem("ident_done")
        padded = sem("padded")
        ctx_in = [sem(f"ctx_in{n}") for n in range(2)]
        mask_in = [sem(f"mask_in{n}") for n in range(2)]
        x_in = sem("x_in")
        mrow_ready = sem("mrow_ready")
        scores_ready, masked, bias_ready, exp_ready = sem("scores"), sem("masked"), sem("bias_ready"), sem("exp")
        total_ready, inv_ready, normed, probsT_ready = sem("total"), sem("inv_ready"), sem("normed"), sem("probsT")
        pT_hi, pT_lo, pv_ready, o_hi, o_lo = sem("pT_hi"), sem("pT_lo"), sem("pv"), sem("o_hi"), sem("o_lo")
        fill_ready, fill_hi, fill_done = sem("fill_ready"), sem("fill_hi"), sem("fill_done")
        stored = [sem(f"stored{n}") for n in range(2)]

        WIDTH = 512
        lo_col = half * H * D
        kv_col = half * G * D
        stages = [(W[c * P:(c + 1) * P, kv_col:kv_col + G * D], w[:, :, c, :]) for W, w in ((Wk, wk), (Wv, wv))
                  for c in range(CC)]
        stages += [(Wq[k * P:(k + 1) * P, lo_col + n:lo_col + n + WIDTH], wq[:, :, k, n:n + WIDTH])
                   for k in range(KC) for n in range(0, H * D, WIDTH)]
        stages += [(Wo[lo_col + h * D:lo_col + (h + 1) * D, :], wo[:, :, h, :]) for h in range(H)]
        W_KV, W_Q, W_ALL = 2 * CC, 2 * CC + KC * H * D // WIDTH, len(stages)
        assert G * D == C == WIDTH and H * D % WIDTH == 0

        probs_flat = probs[:].rearrange("t n k -> t (n k)")
        slots = [stage[:, n, :] for n in range(4)] + \
                [probs_flat[:, n:n + WIDTH] for n in range(0, 4 * WIDE - WIDTH + 1, WIDTH)] + \
                [ost[:].rearrange("p n t -> p (n t)")[:, 0:WIDTH]]
        SLOTS = len(slots)

        with nc.Block() as block:
            turns_in_loop = TURNS - 2

            @block.sync
            def _(sp):
                def load_ctx(turn, odd, waits):
                    b = sp.snap(turn.count(2, odd)) if turn.reg is not None else turn.count(2, odd)
                    for s, value in waits:
                        sp.wait_ge(s, value)
                        sp.nop(nofuse=True)
                    whole = S // P * P
                    sp.dma_start(ctxn[:, odd, 0:S // P, :],
                                 ctx[bass.ds(b, 1), 0:whole, :].rearrange("a (c p) d -> p (a c) d", p=P)) \
                        .then_inc(ctx_in[odd], 16)
                    sp.dma_start(ctxn[0:S - whole, odd, NKC - 1, :],
                                 ctx[bass.ds(b, 1), whole:S, :].rearrange("a p d -> (a p) d")) \
                        .then_inc(ctx_in[odd], 16)
                    sp.dma_start(mraw[:, odd], mask[bass.ds(b, 1), :].to_broadcast([T, S])).then_inc(mask_in[odd], 16)

                def load_x(turn, waits):
                    t = sp.snap(turn.count(T2, 0)) if turn.reg is not None else turn.count(T2, 0)
                    for s, value in waits:
                        sp.wait_ge(s, value)
                        sp.nop(nofuse=True)
                    for a in (HI, LO):
                        sp.dma_start(x2[:, a].bitcast(F32), h2T[a, :, :, bass.ds(t, T2)].rearrange("c p t -> p c t")) \
                            .then_inc(x_in, 16)

                def store(turn, until):
                    t = sp.snap(turn.count(T2, 0)) if turn.reg is not None else turn.count(T2, 0)
                    for n in range(2):
                        sp.wait_ge(fill_done, until(n))
                        sp.nop(nofuse=True)
                        sp.dma_start(part[2 * n:2 * n + 2, :, bass.ds(t, T2)].rearrange("c p t -> p c t"),
                                     ost[:, n, :].rearrange("p (c t) -> p c t", c=2)).then_inc(stored[n], 16)

                for n, (src, _) in enumerate(stages):
                    if n >= SLOTS:
                        sp.wait_ge(w_lo, n - SLOTS + 1)
                    sp.dma_start(slots[n % SLOTS], src).then_inc(w_in[n % SLOTS], 16)
                    if n == 2 * CC - 1:
                        sp.wait_ge(padded, 1)
                        load_ctx(Turn(0), 0, [])
                        load_ctx(Turn(0), 1, [])
                        load_x(Turn(0), [])

                def turn_of(turn, last=False):
                    after = Turn(turn.at + 1, turn.reg)
                    if not last:
                        load_ctx(after, 0, [(fill_ready, fills_until(turn.before(), ("C", 0, 1))),
                                            (mrow_ready, turn.count(2, 1))])
                        load_x(after, [(fill_ready, made(turn, ("Q", 0, G - 1)))])
                    if not (turn.at == 0 and turn.reg is None):
                        store(turn.before(), lambda n: fills_until(turn, ("O", 0, n)))
                    if not last:
                        load_ctx(after, 1, [(fill_ready, fills_until(turn.before(), ("C", 1, 1))),
                                            (mrow_ready, turn.count(2, 2))])

                turn_of(Turn(0))
                with sp.Fori(0, turns_in_loop) as j:
                    turn_of(Turn(1, j))
                turn_of(Turn(TURNS - 1), last=True)
                store(Turn(TURNS - 1), lambda n: BASE + NF * (TURNS - 1) + len(flatl) + n + 1)
                for n in range(2):
                    sp.wait_ge(stored[n], 16 * TURNS)

            @block.gpsimd
            def _(pool):
                make_identity(pool, ident[:], ident_done)

                def heads(turn, s):
                    for h in range(2):
                        n = 2 * s + h
                        m = n % 4
                        pool.wait_ge(masked, turn.count(16, n + 1))
                        pool.nop(nofuse=True)
                        pool.tensor_scalar(bias[:, m:m + 1], top[:, m:m + 1], -0.1 * NEG, -SCALE, ALU.max, ALU.mult) \
                            .then_inc(bias_ready, 1)
                    for h in range(2):
                        n = 2 * s + h
                        m = n % 4
                        pool.wait_ge(inv_ready, turn.count(16, n + 1))
                        pool.nop(nofuse=True)
                        pool.tensor_scalar(probs[0:T, m, 0:SE], probs[0:T, m, 0:SE], inv[:, m:m + 1], None,
                                           ALU.mult).then_inc(normed, 1)

                def turn_of(turn):
                    for s in range(8):
                        heads(turn, s)

                turn_of(Turn(0))
                with pool.Fori(0, turns_in_loop) as j:
                    turn_of(Turn(1, j))
                turn_of(Turn(TURNS - 1))

            def source(f, b):
                kind, odd, n = f
                if kind == "K":
                    return b[:, 0:SE], [kT[:, a, n, :] for a in (HI, LO)]
                if kind == "V":
                    rows = CHUNKS[n][1]
                    return b[0:rows, 0:G * D], [v[0:rows, odd, a, n, :] for a in (HI, LO)]
                if kind == "Q":
                    return (b[:, 0:2 * T2].rearrange("p (h t) -> p h t", h=2),
                            [qT[:, a, 2 * n:2 * n + 2, :] for a in (HI, LO)])
                return b[:, 0:SE], [ctxT[:, odd, a, n, :] for a in (HI, LO)]

            @block.scalar
            def _(act):
                for n, (_, dst) in enumerate(stages):
                    act.wait_ge(w_in[n % SLOTS], 16 * (n // SLOTS + 1))
                    act.activation(dst[:, HI], slots[n % SLOTS], ACT.Copy).then_inc(w_hi, 1)

                def fill(turn, f, before, b):
                    act.wait_ge(fill_ready, before + 1)
                    if f[0] == "O":
                        if turn.count(1, 0) is not None and not (turn.reg is None and turn.at <= 0):
                            act.wait_ge(stored[f[2]], turn.count(16, 0))
                        act.activation(ost[:, f[2], 0:T2], ps_f[b][:, 0:T2], ACT.Copy).then_inc(fill_hi, 1)
                    else:
                        src, dst = source(f, ps_f[b])
                        act.activation(dst[HI], src, ACT.Copy).then_inc(fill_hi, 1)

                def probsT(turn, s):
                    for h in range(2):
                        act.wait_ge(probsT_ready, turn.count(16, 2 * s + h + 1))
                        if h == 0 and not (turn.reg is None and turn.at == 0 and s < 2):
                            act.wait_ge(pv_ready, turn.count(8, s - 1))
                        act.activation(pT[:, s % 2, HI, :, h * T:(h + 1) * T],
                                       ps_t[h][:, 0:NKC * T].rearrange("p (c t) -> p c t", c=NKC),
                                       ACT.Copy).then_inc(pT_hi, 1)

                def out(turn, s):
                    act.wait_ge(pv_ready, turn.count(8, s + 1))
                    g, odd = s % 4, s // 4
                    act.activation(oT[:, HI, 2 * g:2 * g + 2, odd * T:(odd + 1) * T],
                                   ps_o[:, 0:T2].rearrange("p (h t) -> p h t", h=2), ACT.Copy).then_inc(o_hi, 1)

                def exps(turn, s):
                    for h in range(2):
                        n = 2 * s + h
                        m = n % 4
                        act.wait_ge(bias_ready, turn.count(16, n + 1))
                        act.activation(probs[0:T, m, 0:SE], probs[0:T, m, 0:SE], ACT.Exp, bias=bias[:, m:m + 1], scale=SCALE,
                                       accum_out=total[:, m:m + 1]).then_inc(exp_ready, 1)

                def turn_of(turn):
                    first = turn.reg is None and turn.at == 0
                    for s, fills in enumerate(fills_of(turn)):
                        if not (first and s < 1):
                            probsT(*(turn, s - 1) if s else (turn.before(), 7))
                        exps(turn, s)
                        for f, before, b in fills:
                            if f[0] == "O":
                                fill(turn.before(), f, before, b)
                        if not (first and s < 2):
                            out(*(turn, s - 2) if s >= 2 else (turn.before(), s + 6))
                        for f, before, b in fills:
                            if f[0] != "O":
                                fill(turn, f, before, b)

                for n, f in enumerate(HEAD):
                    fill(Turn(-1), f, n, n % 3)
                turn_of(Turn(0))
                with act.Fori(0, turns_in_loop) as j:
                    turn_of(Turn(1, j))
                turn_of(Turn(TURNS - 1))
                last = Turn(TURNS - 1)
                probsT(last, 7)
                out(last, 6)
                out(last, 7)
                for n, f in enumerate(TAIL):
                    before = BASE + NF * (TURNS - 1) + len(flatl) + n
                    fill(last, f, before, before % 3)

            @block.vector
            def _(dve):
                dve.memset(ctxn[96:P, :, NKC - 1, :], 0.0).then_inc(padded, 1)
                if SE > S:
                    dve.memset(mrow[:, :, S:SE], -NEG).then_inc(padded, 1)
                else:
                    dve.sem_inc(padded, 1)
                for n, (_, dst) in enumerate(stages):
                    dve.wait_ge(w_hi, n + 1)
                    dve.tensor_tensor(dst[:, LO], slots[n % SLOTS], dst[:, HI].bitcast(F32), ALU.subtract) \
                        .then_inc(w_lo, 1)
                dve.wait_ge(w_lo, W_ALL)
                dve.memset(probs[0:T, :, SE:WIDE], 0.0).then_inc(padded, 1)

                def fill(turn, f, before, b):
                    dve.wait_ge(fill_hi, before + 1)
                    if f[0] == "O":
                        if not (turn.reg is None and turn.at <= 0):
                            dve.wait_ge(stored[f[2]], turn.count(16, 0))
                        dve.tensor_copy(ost[:, f[2], T2:2 * T2], ps_f[b][:, T2:2 * T2]).then_inc(fill_done, 1)
                    else:
                        src, dst = source(f, ps_f[b])
                        dve.tensor_tensor(dst[LO], src, dst[HI].bitcast(F32), ALU.subtract).then_inc(fill_done, 1)

                def mask_row(turn, odd):
                    dve.wait_ge(mask_in[odd], turn.count(16, 16))
                    dve.tensor_scalar(mrow[:, odd, 0:S], mraw[:, odd, :], -1.0, NEG, ALU.add, ALU.mult) \
                        .then_inc(mrow_ready, 1)
                    dve.wait_ge(mrow_ready, turn.count(2, odd + 1))

                def maxima(turn, s):
                    for h in range(2):
                        n = 2 * s + h
                        m = n % 4
                        dve.wait_ge(scores_ready, turn.count(16, n + 1))
                        if not (turn.reg is None and turn.at == 0 and n < 4):
                            dve.wait_ge(probsT_ready, turn.count(16, n - 3))
                        dve.nop(nofuse=True)
                        dve.tensor_tensor_reduce(out=probs[0:T, m, 0:SE], in0=ps_s[h][0:T, 0:SE], in1=mrow[:, s // 4, :],
                                                 scale=1.0, scalar=-3.0e38, op0=ALU.add, op1=ALU.max,
                                                 accum_out=top[:, m:m + 1]).then_inc(masked, 1)

                def probsT(turn, s):
                    for h in range(2):
                        dve.wait_ge(pT_hi, turn.count(16, 2 * s + h + 1))
                        dve.tensor_tensor(pT[:, s % 2, LO, :, h * T:(h + 1) * T],
                                          ps_t[h][:, 0:NKC * T].rearrange("p (c t) -> p c t", c=NKC),
                                          pT[:, s % 2, HI, :, h * T:(h + 1) * T].bitcast(F32),
                                          ALU.subtract).then_inc(pT_lo, 1)

                def out(turn, s):
                    dve.wait_ge(o_hi, turn.count(8, s + 1))
                    g, odd = s % 4, s // 4
                    dve.tensor_tensor(oT[:, LO, 2 * g:2 * g + 2, odd * T:(odd + 1) * T],
                                      ps_o[:, 0:T2].rearrange("p (h t) -> p h t", h=2),
                                      oT[:, HI, 2 * g:2 * g + 2, odd * T:(odd + 1) * T].bitcast(F32),
                                      ALU.subtract).then_inc(o_lo, 1)

                def inverses(turn, s):
                    for h in range(2):
                        n = 2 * s + h
                        m = n % 4
                        dve.wait_ge(exp_ready, turn.count(16, n + 1))
                        dve.tensor_scalar(total[:, m:m + 1], total[:, m:m + 1], 1e-30, None, ALU.max) \
                            .then_inc(total_ready, 1)
                        dve.wait_ge(total_ready, turn.count(16, n + 1))
                        dve.reciprocal(inv[:, m:m + 1], total[:, m:m + 1]).then_inc(inv_ready, 1)

                def turn_of(turn):
                    first = turn.reg is None and turn.at == 0
                    for s, fills in enumerate(fills_of(turn)):
                        if s % 4 == 0:
                            mask_row(turn, s // 4)
                        maxima(turn, s)
                        if not (first and s < 1):
                            probsT(*(turn, s - 1) if s else (turn.before(), 7))
                        inverses(turn, s)
                        for f, before, b in fills:
                            if f[0] == "O":
                                fill(turn.before(), f, before, b)
                        if not (first and s < 2):
                            out(*(turn, s - 2) if s >= 2 else (turn.before(), s + 6))
                        for f, before, b in fills:
                            if f[0] != "O":
                                fill(turn, f, before, b)

                for n, f in enumerate(HEAD):
                    fill(Turn(-1), f, n, n % 3)
                turn_of(Turn(0))
                with dve.Fori(0, turns_in_loop) as j:
                    turn_of(Turn(1, j))
                turn_of(Turn(TURNS - 1))
                last = Turn(TURNS - 1)
                probsT(last, 7)
                out(last, 6)
                out(last, 7)
                for n, f in enumerate(TAIL):
                    before = BASE + NF * (TURNS - 1) + len(flatl) + n
                    fill(last, f, before, before % 3)

            @block.tensor
            def _(pe):
                pe.wait_ge(ident_done, 2)
                seen = [0]

                def weights(n):
                    if seen[0] < n:
                        pe.wait_ge(w_lo, n)
                        seen[0] = n

                def fill(turn, f, before, b, fed):
                    kind, odd, n = f
                    if not (isinstance(before, int) and before < 3):
                        pe.wait_ge(fill_done, before - 2)
                    for s, value in fed:
                        pe.wait_ge(s, value)
                    out = ps_f[b]
                    if kind == "C":
                        for c, (k, rows) in enumerate(CHUNKS):
                            last = pe.transpose(out[:, k:k + rows], ctxn[0:rows, odd, c, n * P:(n + 1) * P],
                                                ident[0:rows, 0:rows])
                        last.then_inc(fill_ready, 1)
                        return
                    if kind == "K":
                        groups = [[(out[:, 0:SE], wk[:, a, c, n * D:(n + 1) * D], ctxT[:, odd, b_, c, :])
                                   for c in range(CC) for a, b_ in PASSES]]
                    elif kind == "V":
                        k, rows = CHUNKS[n]
                        groups = [[(out[0:rows, 0:G * D], ctxT[:, odd, a, c, k:k + rows], wv[:, b_, c, :])
                                   for c in range(CC) for a, b_ in PASSES]]
                    elif kind == "Q":
                        groups = [[(out[:, h * T2:(h + 1) * T2], wq[:, a, c, (2 * n + h) * D:(2 * n + h + 1) * D],
                                    x2[:, b_, c, :]) for c in range(KC) for a, b_ in PASSES] for h in range(2)]
                    else:
                        groups = [[(out[:, o * T2:(o + 1) * T2], wo[:, a, h, (2 * n + o) * P:(2 * n + o + 1) * P],
                                    oT[:, b_, h, :]) for h in range(H) for a, b_ in PASSES] for o in range(2)]
                    for jobs in groups:
                        for m, (o, w, x) in enumerate(jobs):
                            last = pe.matmul(o, w, x, start=m == 0, stop=m == len(jobs) - 1)
                    last.then_inc(fill_ready, 1)

                def fed(turn, f):
                    kind, odd, n = f
                    if kind == "C":
                        return [(ctx_in[odd], turn.count(32, 64))] if n == 0 else []
                    if kind == "Q":
                        return [(x_in, turn.count(32, 64))] if n == 0 else []
                    if kind == "O":
                        return [(o_lo, turn.count(8, 0))] if n == 0 else []
                    if n == 0 and kind == "K":
                        at = turn if odd == 0 else turn.before()
                        return [(fill_done, fills_until(at, ("C", odd, 1)))]
                    return []

                def scores(turn, s):
                    g, odd = s % 4, s // 4
                    pe.wait_ge(fill_done, made(turn, ("K", odd, g)))
                    if odd == 0 and turn.reg is None and turn.at == 0:
                        pe.wait_ge(fill_done, made(turn, ("Q", 0, g)))
                    for h in range(2):
                        n = 2 * s + h
                        if not (turn.reg is None and turn.at == 0 and n < 2):
                            pe.wait_ge(masked, turn.count(16, n - 1))
                        for m, (a, b_) in enumerate(PASSES):
                            last = pe.matmul(ps_s[h][0:T, 0:SE], qT[:, a, 2 * g + h, odd * T:(odd + 1) * T],
                                             kT[:, b_, g, :], start=m == 0, stop=m == 2)
                        last.then_inc(scores_ready, 1)

                def probsT(turn, s):
                    for h in range(2):
                        n = 2 * s + h
                        pe.wait_ge(normed, turn.count(16, n + 1))
                        if not (turn.reg is None and turn.at == 0 and n < 2):
                            pe.wait_ge(pT_lo, turn.count(16, n - 1))
                        for c in range(NKC):
                            last = pe.transpose(ps_t[h][:, c * T:(c + 1) * T],
                                                probs[0:T, n % 4, c * P:(c + 1) * P], ident[0:T, 0:T])
                        last.then_inc(probsT_ready, 1)

                def pv(turn, s):
                    g, odd = s % 4, s // 4
                    if g == 0:
                        pe.wait_ge(fill_done, made(turn, ("V", odd, NKC - 1)))
                    pe.wait_ge(pT_lo, turn.count(16, 2 * s + 2))
                    if not (turn.reg is None and turn.at == 0 and s == 0):
                        pe.wait_ge(o_lo, turn.count(8, s))
                    jobs = [(v[0:rows, odd, a, c, g * D:(g + 1) * D], pT[0:rows, s % 2, b_, c, :])
                            for c, (_, rows) in enumerate(CHUNKS) for a, b_ in PASSES]
                    for m, (w, x) in enumerate(jobs):
                        last = pe.matmul(ps_o[:, 0:T2], w, x, start=m == 0, stop=m == len(jobs) - 1)
                    last.then_inc(pv_ready, 1)

                def turn_of(turn):
                    first = turn.reg is None and turn.at == 0
                    for s, fills in enumerate(fills_of(turn)):
                        scores(turn, s)
                        if not (first and s < 1):
                            probsT(*(turn, s - 1) if s else (turn.before(), 7))
                        for f, before, b in fills:
                            if f[0] == "O":
                                fill(turn, f, before, b, fed(turn, f))
                        if not (first and s < 2):
                            pv(*(turn, s - 2) if s >= 2 else (turn.before(), s + 6))
                        for f, before, b in fills:
                            if f[0] != "O":
                                fill(turn, f, before, b, fed(turn, f))

                for n, f in enumerate(HEAD):
                    weights({"C": 0, "K": W_KV, "V": W_KV, "Q": W_Q}[f[0]])
                    waits = {("C", 0, 0): [(ctx_in[0], 32)], ("C", 1, 0): [(ctx_in[1], 32)],
                             ("K", 0, 0): [(fill_done, 2)], ("Q", 0, 0): [(x_in, 32)]}
                    fill(Turn(-1), f, n, n % 3, waits.get(f, []))
                weights(W_ALL)
                pe.wait_ge(padded, 3)
                turn_of(Turn(0))
                with pe.Fori(0, turns_in_loop) as j:
                    turn_of(Turn(1, j))
                turn_of(Turn(TURNS - 1))
                last = Turn(TURNS - 1)
                probsT(last, 7)
                pv(last, 6)
                pv(last, 7)
                for n, f in enumerate(TAIL):
                    before = BASE + NF * (TURNS - 1) + len(flatl) + n
                    fill(last, f, before, before % 3, [(o_lo, 8 * TURNS)] if n == 0 else [])


def expert_ffn(nc, B, T, x1, parts, wg, W, b, x2, slots, expert_out, out):
    C = x1.shape[2]
    KC = C // P
    E = W.shape[0]
    TILES = B * T // P
    SLOTS = TILES + E - 1
    EPS = 1e-5
    BF16 = mybir.dt.bfloat16

    with ExitStack() as stack:
        def sb(name, shape, dt=F32, to=stack):
            return to.enter_context(nc.sbuf_tensor(f"m_{name}", shape, dt))

        sem = stack.enter_context(semaphores(nc, "m"))

        wT = sb("wT", [P, 2, KC, E, C], F32R)
        slot = sb("slot", [P, TILES], U32)
        gate = sb("gate", [P, TILES])
        owner = sb("owner", [P, SLOTS], I32)
        ident = sb("ident", [P, P])

        x1_t = x1.rearrange("b t c -> (b t) c").rearrange("(n p) c -> n p c", p=P)
        x2_t = x2.rearrange("(n p) c -> n p c", p=P)
        out_t = out.rearrange("b t c -> (b t) c").rearrange("(n p) c -> n p c", p=P)

        with ExitStack() as inner:
            def ib(name, shape, dt=F32):
                return sb(name, shape, dt, inner)

            def bank(name):
                return inner.enter_context(nc.psum_tensor(f"m_{name}", [P, 512], F32))

            h3 = ib("h3", [P, TILES, C])
            wn = h3[:, 0:2 * KC, :].rearrange("p (e c) h -> p e c h", e=2)
            xt = ib("xt", [P, 2, C])
            pt = ib("pt", [P, 2, 2, KC, P])
            hn = ib("hn", [P, 2, C])
            hT = ib("hT", [P, KC, P])
            wgs = ib("wgs", [P, KC, E])
            logits = ib("logits", [P, TILES, E])
            order = ib("order", [P, TILES, E])
            before = ib("before", [P, TILES + 1, E])
            best = ib("best", [P, TILES])
            total = ib("total", [P, TILES])
            chosen = ib("chosen", [P, TILES, E], BF16)
            slotf = ib("slotf", [P, TILES])
            number = ib("number", [P, E])
            start = ib("start", [P, E + 1])
            ownerf = ib("ownerf", [P, SLOTS])
            lower = ib("lower", [P, P], BF16)
            ones = ib("ones", [P, P], BF16)
            zero = hn[:, 1, :]
            room = pt[:].rearrange("p a k c t -> p (a k c t)")
            N1, N2 = TILES * E, SLOTS * E
            like, places = (room[:, k * N1:(k + 1) * N1].rearrange("p (t e) -> p t e", e=E) for k in range(2))
            ends, steps = (room[:, 2 * N1 + k * N2:2 * N1 + (k + 1) * N2].rearrange("p (t e) -> p t e", e=E)
                           for k in range(2))
            power = ib("power", [P, 1])
            st = ib("st", [P, 2, 6])
            mv = ib("mv", [P, 2, 2])
            rs = ib("rs", [P, 2, 1])
            ps = [bank(f"a{n}") for n in range(4)]
            ps_l = [bank(f"l{n}") for n in range(2)]
            ps_r = [bank(f"r{n}") for n in range(2)]

            const_done, tri_done, set_done = sem("const"), sem("tri"), sem("set")
            wn_in = [sem(f"wn_in{n}") for n in range(2)]
            zeroed, wg_in = sem("zeroed"), sem("wg_in")
            xt_in = [sem(f"xt_in{n}") for n in range(2)]
            pt_in = [sem(f"pt_in{n}") for n in range(2)]
            x2_out = [sem(f"x2_out{n}") for n in range(2)]
            w_ready, w_hi, w_lo = sem("w_ready"), sem("w_hi"), sem("w_lo")
            summed, xT_ready, x2_ready = sem("summed"), sem("xT_ready"), sem("x2_ready")
            st_ready, mv_ready, ve_ready, rs_ready = sem("st"), sem("mv"), sem("ve"), sem("rs")
            hn_ready, h3_ready, hT_ps, hT_ready = sem("hn"), sem("h3"), sem("hT_ps"), sem("hT")
            logit_ps, logit_ready = sem("logit_ps"), sem("logit")
            less_ready, exp_ready, chosen_ready, ranked = sem("less"), sem("exp"), sem("chosen"), sem("ranked")
            chain, slots_ready, scattered = sem("chain"), sem("slots"), sem("scattered")

            TURNS = TILES // 2
            WT_TURNS = E // 2

            with nc.Block() as block:
                @block.sync
                def _(sp):
                    def load_w(turn, e):
                        n = turn.count(2, e)
                        n = sp.snap(n) if turn.reg is not None else n
                        if turn.at > 0:
                            sp.wait_ge(w_ready, turn.count(2 * KC, KC * (e + 1) - 2 * KC))
                            sp.nop(nofuse=True)
                        sp.dma_start(wn[:, e], W[bass.ds(n, 1)].rearrange("a (c p) h -> p (a c) h", p=P)) \
                            .then_inc(wn_in[e], 16)

                    def load_x(turn, par):
                        n = turn.count(2, par)
                        n = sp.snap(n) if turn.reg is not None else n
                        t = turn.count(2 * P, par * P)
                        t = sp.snap(t) if turn.reg is not None else t
                        if turn.at > 0:
                            sp.wait_ge(xT_ready, turn.count(2, par - 1))
                            sp.nop(nofuse=True)
                        for k, part in enumerate(parts):
                            sp.dma_start(pt[:, par, k], part[:, :, bass.ds(t, P)].rearrange("c p t -> p c t")) \
                                .then_inc(pt_in[par], 16)
                        if turn.at > 0:
                            sp.wait_ge(hn_ready, turn.count(2, par - 1))
                            sp.nop(nofuse=True)
                            sp.wait_ge(x2_out[par], turn.count(16, 0))
                            sp.nop(nofuse=True)
                        sp.dma_start(xt[:, par, :], x1_t[bass.ds(n, 1)].rearrange("a p c -> (a p) c")) \
                            .then_inc(xt_in[par], 16)

                    sp.dma_start(wgs[:], wg.rearrange("(c p) e -> p c e", p=P)).then_inc(wg_in, 16)
                    for e in range(2):
                        load_w(Turn(0), e)
                    for par in range(2):
                        load_x(Turn(0), par)
                    sp.wait_ge(set_done, 1)
                    sp.dma_start(slots.rearrange("(n p) c -> p n c", p=P),
                                 zero.unsqueeze(1).to_broadcast([P, SLOTS, C])).then_inc(zeroed, 16)
                    with sp.Fori(0, WT_TURNS - 1) as j:
                        for e in range(2):
                            load_w(Turn(1, j), e)
                    with sp.Fori(0, TURNS - 1) as j:
                        for par in range(2):
                            load_x(Turn(1, j), par)

                @block.gpsimd
                def _(pool):
                    make_identity(pool, ident[:], const_done)
                    pool.memset(ones[:], 1.0).then_inc(tri_done, 1)
                    pool.wait_ge(tri_done, 1)
                    pool.affine_select(out=lower[:], in_=ones[:], compare_op=ALU.is_gt, fill=0.0, base=0,
                                       pattern=[[1, P]], channel_multiplier=-1).then_inc(tri_done, 1)
                    pool.iota(order[:].rearrange("p t e -> p (t e)"), pattern=[[0, TILES], [1, E]], base=0,
                              channel_multiplier=0, allow_small_or_imprecise_dtypes=True).then_inc(tri_done, 1)
                    pool.wait_ge(set_done, 1)
                    pool.wait_ge(w_ready, E * KC)

                    def rstd(turn, par):
                        pool.wait_ge(mv_ready, turn.count(2, par + 1))
                        pool.nop(nofuse=True)
                        pool.tensor_scalar(rs[:, par, :], mv[:, par, 1:2], EPS, None, ALU.add).then_inc(ve_ready, 1)
                        pool.wait_ge(ve_ready, turn.count(2, par + 1))
                        pool.nop(nofuse=True)
                        pool.tensor_tensor(rs[:, par, :], rs[:, par, :], power[:], ALU.pow).then_inc(rs_ready, 1)

                    def keep(turn, par):
                        n = turn.count(2, par)
                        pool.wait_ge(hn_ready, turn.count(2, par + 1))
                        pool.nop(nofuse=True)
                        dst = h3[:, n, :] if turn.reg is None else h3[:, bass.ds(n, 1), :].rearrange("p a c -> p (a c)")
                        pool.tensor_copy(dst, hn[:, par, :]).then_inc(h3_ready, 1)

                    def turn_of(turn):
                        for par in range(2):
                            rstd(turn, par)
                            if par:
                                keep(turn, 0)
                            elif not (turn.reg is None and turn.at == 0):
                                keep(turn.before(), 1)

                    turn_of(Turn(0))
                    with pool.Fori(0, TURNS - 1) as j:
                        turn_of(Turn(1, j))
                    keep(Turn(TURNS - 1), 1)
                    pool.wait_ge(xT_ready, TILES)
                    pool.iota(steps.rearrange("p t e -> p (t e)"), pattern=[[1, SLOTS], [0, E]], base=0,
                              channel_multiplier=0, allow_small_or_imprecise_dtypes=True).then_inc(tri_done, 1)
                    pool.wait_ge(h3_ready, TILES)
                    pool.wait_ge(slots_ready, 1)
                    pool.wait_ge(zeroed, 16)
                    for t in range(TILES):
                        pool.indirect_dma_start(out=slots, out_offset=bass.IndirectOffsetOnAxis(ap=slot[:, t:t + 1], axis=0),
                                                in_=h3[:, t, :], in_offset=None).then_inc(scattered, 16)
                    pool.wait_ge(scattered, 16 * TILES)

                @block.scalar
                def _(act):
                    def fill_w(turn, e, c):
                        k = KC * e + c
                        act.wait_ge(w_ready, turn.count(2 * KC, k + 1))
                        dst = wT[:, HI, c, bass.ds(turn.count(2, e), 1), :].rearrange("p a o -> p (a o)")
                        act.activation(dst, ps[k % 4][:], ACT.Copy).then_inc(w_hi, 1)

                    def copy_hT(turn, par):
                        act.wait_ge(hT_ps, turn.count(2, par + 1))
                        if not (turn.reg is None and turn.at == 0 and par == 0):
                            act.wait_ge(logit_ps, turn.count(2, par))
                        act.activation(hT[:], ps[2 + par][:].rearrange("p (c t) -> p c t", c=KC), ACT.Copy) \
                            .then_inc(hT_ready, 1)

                    def store(turn, par):
                        n = turn.count(2, par)
                        n = act.snap(n) if turn.reg is not None else n
                        act.wait_ge(x2_ready, turn.count(2, par + 1))
                        act.nop(nofuse=True)
                        act.dma_start(x2_t[bass.ds(n, 1)].rearrange("a p c -> (a p) c"), xt[:, par, :]) \
                            .then_inc(x2_out[par], 16)

                    def turn_of(turn):
                        for par in range(2):
                            if par:
                                copy_hT(turn, 0)
                            elif not (turn.reg is None and turn.at == 0):
                                copy_hT(turn.before(), 1)
                            store(turn, par)

                    with act.Fori(0, WT_TURNS) as j:
                        for e in range(2):
                            for c in range(KC):
                                fill_w(Turn(0, j), e, c)
                    turn_of(Turn(0))
                    with act.Fori(0, TURNS - 1) as j:
                        turn_of(Turn(1, j))
                    copy_hT(Turn(TURNS - 1), 1)
                    act.wait_ge(less_ready, 1)
                    act.activation(places, places, ACT.Exp).then_inc(exp_ready, 1)
                    for par in range(2):
                        act.wait_ge(x2_out[par], 16 * TURNS)

                @block.vector
                def _(dve):
                    count = [0]

                    def link(ins):
                        count[0] += 1
                        ins.then_inc(chain, 1)
                        dve.wait_ge(chain, count[0])

                    dve.memset(power[:], -0.5)
                    dve.memset(before[:, 0, :], 0.0)
                    dve.memset(start[:, 0:1], 0.0)
                    dve.memset(zero, 0.0).then_inc(set_done, 1)

                    def fill_w(turn, e, c):
                        k = KC * e + c
                        dve.wait_ge(w_hi, turn.count(2 * KC, k + 1))
                        hi, lo = (wT[:, a, c, bass.ds(turn.count(2, e), 1), :].rearrange("p a o -> p (a o)")
                                  for a in (HI, LO))
                        dve.tensor_tensor(lo, ps[k % 4][:], hi.bitcast(F32), ALU.subtract).then_inc(w_lo, 1)

                    def add_parts(turn, par):
                        dve.wait_ge(pt_in[par], turn.count(32, 32))
                        dve.tensor_tensor(pt[:, par, 0], pt[:, par, 0], pt[:, par, 1], ALU.add).then_inc(summed, 1)

                    def residual(turn, par):
                        dve.wait_ge(xt_in[par], turn.count(16, 16))
                        dve.wait_ge(xT_ready, turn.count(2, par + 1))
                        dve.tensor_tensor(xt[:, par, :], ps[par][:], xt[:, par, :], ALU.add).then_inc(x2_ready, 1)
                        dve.wait_ge(x2_ready, turn.count(2, par + 1))
                        dve.bn_stats(st[:, par, :], xt[:, par, :]).then_inc(st_ready, 1)
                        dve.wait_ge(st_ready, turn.count(2, par + 1))
                        dve.nop(nofuse=True)
                        dve.bn_aggr(mv[:, par, :], st[:, par, :]).then_inc(mv_ready, 1)

                    def normal(turn, par):
                        if turn.reg is None and turn.at == 0 and par == 1:
                            dve.wait_ge(zeroed, 16)
                        dve.wait_ge(rs_ready, turn.count(2, par + 1))
                        if not (turn.reg is None and turn.at == 0):
                            dve.wait_ge(hT_ps, turn.count(2, par - 1))
                            dve.wait_ge(h3_ready, turn.count(2, par - 1))
                        dve.tensor_scalar(hn[:, par, :], xt[:, par, :], mv[:, par, 0:1], rs[:, par, :],
                                          ALU.subtract, ALU.mult).then_inc(hn_ready, 1)

                    def keep_logits(turn, par):
                        n = turn.count(2, par)
                        dve.wait_ge(logit_ps, turn.count(2, par + 1))
                        dst = logits[:, n, :] if turn.reg is None else \
                            logits[:, bass.ds(n, 1), :].rearrange("p a e -> p (a e)")
                        dve.tensor_copy(dst, ps_l[par][:, 0:E]).then_inc(logit_ready, 1)

                    def turn_of(turn, last=False):
                        for par in range(2):
                            residual(turn, par)
                            if par == 0:
                                add_parts(turn, 1)
                            elif not last:
                                add_parts(Turn(turn.at + 1, turn.reg), 0)
                            if not (turn.reg is None and turn.at == 0):
                                keep_logits(turn.before(), par)
                            normal(turn, par)

                    with dve.Fori(0, WT_TURNS) as j:
                        for e in range(2):
                            for c in range(KC):
                                fill_w(Turn(0, j), e, c)
                    add_parts(Turn(0), 0)
                    turn_of(Turn(0))
                    with dve.Fori(0, TURNS - 2) as j:
                        turn_of(Turn(1, j))
                    turn_of(Turn(TURNS - 1), last=True)
                    for par in range(2):
                        keep_logits(Turn(TURNS - 1), par)

                    def over_e(a):
                        return a.unsqueeze(2).to_broadcast([P, a.shape[1], E])

                    def over_t(a, n):
                        return a.unsqueeze(1).to_broadcast([P, n, E])

                    dve.wait_ge(logit_ready, TILES)
                    dve.wait_ge(tri_done, 4)
                    link(dve.tensor_reduce(best[:], logits[:], AX.X, ALU.max))
                    dve.tensor_tensor(places, logits[:], over_e(best[:]), ALU.subtract).then_inc(less_ready, 1)
                    link(dve.tensor_tensor(like, logits[:], over_e(best[:]), ALU.is_equal))
                    link(dve.scalar_tensor_tensor(out=logits[:], in0=like, scalar=-float(E), in1=order[:],
                                                  op0=ALU.mult, op1=ALU.add))
                    link(dve.tensor_reduce(best[:], logits[:], AX.X, ALU.min))
                    dve.tensor_tensor(chosen[:], logits[:], over_e(best[:]), ALU.is_equal).then_inc(chosen_ready, 1)
                    link(dve.tensor_tensor(like, logits[:], over_e(best[:]), ALU.is_equal))
                    dve.wait_ge(exp_ready, 1)
                    link(dve.tensor_reduce(total[:], places, AX.X, ALU.add))
                    link(dve.reciprocal(gate[:], total[:]))
                    dve.wait_ge(ranked, 1)
                    for t in range(TILES):
                        link(dve.tensor_tensor(before[:, t + 1, :], ps_r[1][:, t * E:(t + 1) * E], before[:, t, :],
                                               ALU.add))
                    link(dve.tensor_tensor(places, ps_r[0][:, 0:TILES * E].rearrange("p (t e) -> p t e", e=E),
                                           before[:, 0:TILES, :], ALU.add))
                    link(dve.tensor_scalar(number[:], before[:, TILES, :], 1.0 / P, 0.5 - 0.5 / P, ALU.mult, ALU.add))
                    link(dve.tensor_scalar(number[:], number[:], 8388608.0, None, ALU.add))
                    link(dve.tensor_scalar(number[:], number[:], -8388608.0, None, ALU.add))
                    for e in range(E):
                        link(dve.tensor_tensor(start[:, e + 1:e + 2], start[:, e:e + 1], number[:, e:e + 1], ALU.add))
                    link(dve.scalar_tensor_tensor(out=places, in0=over_t(start[:, 0:E], TILES), scalar=float(P),
                                                  in1=places, op0=ALU.mult, op1=ALU.add))
                    link(dve.tensor_tensor(places, places, like, ALU.mult))
                    link(dve.tensor_reduce(slotf[:], places, AX.X, ALU.add))
                    dve.tensor_copy(slot[:], slotf[:]).then_inc(slots_ready, 1)
                    link(dve.tensor_tensor(ends, steps, over_t(start[:, 1:E + 1], SLOTS), ALU.is_ge))
                    link(dve.tensor_reduce(ownerf[:], ends, AX.X, ALU.add))
                    link(dve.tensor_scalar(ownerf[:], ownerf[:], float(E - 1), None, ALU.min))
                    link(dve.tensor_copy(owner[:], ownerf[:]))

                @block.tensor
                def _(pe):
                    pe.wait_ge(const_done, 2)

                    def fill_w(turn, e, c):
                        k = KC * e + c
                        if c == 0:
                            pe.wait_ge(wn_in[e], turn.count(16, 16))
                        if not (turn.reg is None and turn.at == 0 and k < 4):
                            pe.wait_ge(w_lo, turn.count(2 * KC, k - 3))
                        for o in range(KC):
                            last = pe.transpose(ps[k % 4][:, o * P:(o + 1) * P], wn[:, e, o, c * P:(c + 1) * P], ident[:])
                        last.then_inc(w_ready, 1)

                    def shares(turn, par):
                        pe.wait_ge(summed, turn.count(2, par + 1))
                        if not (turn.reg is None and turn.at == 0):
                            pe.wait_ge(x2_ready, turn.count(2, par - 1))
                        for c in range(KC):
                            last = pe.transpose(ps[par][:, c * P:(c + 1) * P], pt[:, par, 0, c, :], ident[:])
                        last.then_inc(xT_ready, 1)

                    def rows(turn, par):
                        pe.wait_ge(hn_ready, turn.count(2, par + 1))
                        if not (turn.reg is None and turn.at == 0):
                            pe.wait_ge(hT_ready, turn.count(2, par - 1))
                        for c in range(KC):
                            last = pe.transpose(ps[2 + par][:, c * P:(c + 1) * P], hn[:, par, c * P:(c + 1) * P], ident[:])
                        last.then_inc(hT_ps, 1)

                    def router(turn, par):
                        pe.wait_ge(hT_ready, turn.count(2, par + 1))
                        if not (turn.reg is None and turn.at == 0):
                            pe.wait_ge(logit_ready, turn.count(2, par - 1))
                        for c in range(KC):
                            last = pe.matmul(ps_l[par][:, 0:E], hT[:, c, :], wgs[:, c, :],
                                             start=c == 0, stop=c == KC - 1)
                        last.then_inc(logit_ps, 1)

                    def turn_of(turn):
                        first = turn.reg is None and turn.at == 0
                        for par in range(2):
                            shares(turn, par)
                            if not first:
                                router(turn.before(), par)
                            if par:
                                rows(turn, 0)
                            elif not first:
                                rows(turn.before(), 1)

                    for e in range(2):
                        for c in range(KC):
                            fill_w(Turn(0), e, c)
                    with pe.Fori(0, WT_TURNS - 1) as j:
                        for e in range(2):
                            for c in range(KC):
                                fill_w(Turn(1, j), e, c)
                    pe.wait_ge(w_lo, E * KC)
                    pe.wait_ge(wg_in, 16)
                    turn_of(Turn(0))
                    turn_of(Turn(1))
                    with pe.Fori(0, TURNS - 2) as j:
                        turn_of(Turn(2, j))
                    router(Turn(TURNS - 1), 0)
                    rows(Turn(TURNS - 1), 1)
                    router(Turn(TURNS - 1), 1)
                    pe.wait_ge(chosen_ready, 1)
                    pe.wait_ge(tri_done, 2)
                    rhs = chosen[:].rearrange("p t e -> p (t e)")
                    pe.matmul(ps_r[0][:, 0:TILES * E], lower[:], rhs, start=True, stop=True)
                    pe.matmul(ps_r[1][:, 0:TILES * E], ones[:], rhs, start=True, stop=True).then_inc(ranked, 1)

        with ExitStack() as inner:
            def ib(name, shape, dt=F32):
                return sb(name, shape, dt, inner)

            def bank(name):
                return inner.enter_context(nc.psum_tensor(f"m_{name}", [P, 512], F32))

            bias = ib("bias", [P, E, C])
            rows = ib("rows", [P, 2, C])
            rT = ib("rT", [P, 2, 2, KC, P], F32R)
            y = ib("y", [P, 2, C])
            back = ib("back", [P, 4, C])
            xb = ib("xb", [P, 4, C])
            ps_t = [bank(f"t{n}") for n in range(2)]
            ps_y = [bank(f"y{n}") for n in range(2)]

            bias_in = sem("bias_in")
            rows_in = [sem(f"rows_in{n}") for n in range(2)]
            y_out = [sem(f"y_out{n}") for n in range(2)]
            rT_ready, rT_hi, rT_lo, y_ps, y_ready = sem("rT_ready"), sem("rT_hi"), sem("rT_lo"), sem("y_ps"), sem("y_ready")
            got = [sem(f"got{n}") for n in range(4)]
            xb_in = [sem(f"xb_in{n}") for n in range(4)]
            final = sem("final")
            final_out = [sem(f"final_out{n}") for n in range(4)]
            PAIRS = SLOTS // 2
            slots_t = slots.rearrange("(n p) c -> n p c", p=P)
            y_t = expert_out.rearrange("(n p) c -> n p c", p=P)
            assert SLOTS % 2 == 1

            with nc.Block() as block:
                @block.sync
                def _(sp):
                    def load(turn, par):
                        n = turn.count(2, par)
                        n = sp.snap(n) if turn.reg is not None else n
                        if turn.at > 0:
                            sp.wait_ge(rT_ready, turn.count(2, par - 1))
                            sp.nop(nofuse=True)
                        sp.dma_start(rows[:, par, :], slots_t[bass.ds(n, 1)].rearrange("a p c -> (a p) c")) \
                            .then_inc(rows_in[par], 16)

                    for par in range(2):
                        load(Turn(0), par)
                    sp.dma_start(bias[:].rearrange("p e o -> p (e o)"),
                                 b.rearrange("e o -> (e o)").rearrange("(a n) -> a n", a=1).to_broadcast([P, E * C])) \
                        .then_inc(bias_in, 16)
                    with sp.Fori(0, PAIRS - 1) as j:
                        for par in range(2):
                            load(Turn(1, j), par)
                    load(Turn(PAIRS), 0)
                    for t in range(TILES):
                        if t >= 4:
                            sp.wait_ge(final_out[t % 4], 16 * (t // 4))
                        sp.dma_start(xb[:, t % 4, :], x2_t[t]).then_inc(xb_in[t % 4], 16)

                @block.gpsimd
                def _(pool):
                    pool.wait_ge(y_out[0], 16 * (PAIRS + 1))
                    pool.wait_ge(y_out[1], 16 * PAIRS)
                    for t in range(TILES):
                        if t >= 4:
                            pool.wait_ge(final, t - 3)
                        pool.indirect_dma_start(out=back[:, t % 4, :], out_offset=None, in_=expert_out,
                                                in_offset=bass.IndirectOffsetOnAxis(ap=slot[:, t:t + 1], axis=0)) \
                            .then_inc(got[t % 4], 16)

                @block.scalar
                def _(act):
                    def copy_rT(turn, par):
                        act.wait_ge(rT_ready, turn.count(2, par + 1))
                        if turn.at > 0:
                            act.wait_ge(y_ps, turn.count(2, par - 1))
                        act.activation(rT[:, par, HI], ps_t[par][:].rearrange("p (c t) -> p c t", c=KC), ACT.Copy) \
                            .then_inc(rT_hi, 1)

                    def store(turn, par):
                        n = turn.count(2, par)
                        n = act.snap(n) if turn.reg is not None else n
                        act.wait_ge(y_ready, turn.count(2, par + 1))
                        act.nop(nofuse=True)
                        act.dma_start(y_t[bass.ds(n, 1)].rearrange("a p c -> (a p) c"), y[:, par, :]) \
                            .then_inc(y_out[par], 16)

                    copy_rT(Turn(0), 0)
                    copy_rT(Turn(0), 1)
                    store(Turn(0), 0)
                    with act.Fori(0, PAIRS - 1) as j:
                        copy_rT(Turn(1, j), 0)
                        store(Turn(0, j), 1)
                        copy_rT(Turn(1, j), 1)
                        store(Turn(1, j), 0)
                    copy_rT(Turn(PAIRS), 0)
                    store(Turn(PAIRS - 1), 1)
                    store(Turn(PAIRS), 0)
                    for t in range(TILES):
                        act.wait_ge(final, t + 1)
                        act.dma_start(out_t[t], xb[:, t % 4, :]).then_inc(final_out[t % 4], 16)
                    for n in range(4):
                        act.wait_ge(final_out[n], 16 * (TILES // 4))

                @block.vector
                def _(dve):
                    def copy_rT(turn, par):
                        dve.wait_ge(rT_hi, turn.count(2, par + 1))
                        dve.tensor_tensor(rT[:, par, LO], ps_t[par][:].rearrange("p (c t) -> p c t", c=KC),
                                          rT[:, par, HI].bitcast(F32), ALU.subtract).then_inc(rT_lo, 1)

                    def add_bias(turn, par):
                        n = turn.count(2, par)
                        e = dve.value_load(owner[0:1, bass.ds(n, 1)], min_val=0, max_val=E - 1)
                        dve.wait_ge(y_ps, turn.count(2, par + 1))
                        if turn.at > 0:
                            dve.wait_ge(y_out[par], turn.count(16, 0))
                        dve.tensor_tensor(y[:, par, :], ps_y[par][:],
                                          bias[:, bass.ds(e, 1), :].rearrange("p a o -> p (a o)"), ALU.add) \
                            .then_inc(y_ready, 1)

                    dve.wait_ge(bias_in, 16)
                    copy_rT(Turn(0), 0)
                    copy_rT(Turn(0), 1)
                    add_bias(Turn(0), 0)

                    def turn_of(turn):
                        copy_rT(turn, 0)
                        add_bias(turn.before(), 1)
                        copy_rT(turn, 1)
                        add_bias(turn, 0)

                    turn_of(Turn(1))
                    with dve.Fori(0, PAIRS - 2) as j:
                        turn_of(Turn(2, j))
                    copy_rT(Turn(PAIRS), 0)
                    add_bias(Turn(PAIRS - 1), 1)
                    add_bias(Turn(PAIRS), 0)
                    for t in range(TILES):
                        dve.wait_ge(got[t % 4], 16 * (t // 4 + 1))
                        dve.wait_ge(xb_in[t % 4], 16 * (t // 4 + 1))
                        dve.scalar_tensor_tensor(out=xb[:, t % 4, :], in0=back[:, t % 4, :], scalar=gate[:, t:t + 1],
                                                 in1=xb[:, t % 4, :], op0=ALU.mult, op1=ALU.add).then_inc(final, 1)

                @block.tensor
                def _(pe):
                    def transpose(turn, par):
                        pe.wait_ge(rows_in[par], turn.count(16, 16))
                        if turn.at > 0:
                            pe.wait_ge(rT_lo, turn.count(2, par - 1))
                        for c in range(KC):
                            last = pe.transpose(ps_t[par][:, c * P:(c + 1) * P], rows[:, par, c * P:(c + 1) * P], ident[:])
                        last.then_inc(rT_ready, 1)

                    def product(turn, par):
                        n = turn.count(2, par)
                        e = pe.value_load(owner[0:1, bass.ds(n, 1)], min_val=0, max_val=E - 1)
                        pe.wait_ge(rT_lo, turn.count(2, par + 1))
                        if not (turn.reg is None and turn.at == 0):
                            pe.wait_ge(y_ready, turn.count(2, par - 1))
                        jobs = [(a, b_, c) for c in range(KC) for a, b_ in PASSES]
                        for m, (a, b_, c) in enumerate(jobs):
                            last = pe.matmul(ps_y[par][:], rT[:, par, a, c, :],
                                             wT[:, b_, c, bass.ds(e, 1), :].rearrange("p a o -> p (a o)"),
                                             start=m == 0, stop=m == len(jobs) - 1)
                        last.then_inc(y_ps, 1)

                    transpose(Turn(0), 0)
                    transpose(Turn(0), 1)
                    product(Turn(0), 0)
                    product(Turn(0), 1)
                    with pe.Fori(0, PAIRS - 1) as j:
                        for par in range(2):
                            transpose(Turn(1, j), par)
                        for par in range(2):
                            product(Turn(1, j), par)
                    transpose(Turn(PAIRS), 0)
                    product(Turn(PAIRS), 0)


def decoder_block(nc, x, ctx_1024, mask, attn_Wq, attn_bq, attn_Wk, attn_bk, attn_Wv, attn_bv, attn_Wo, attn_bo,
                  xattn_Wq, xattn_Wk, xattn_Wv, xattn_Wo, ffn_wg, ffn_W, ffn_b, out):
    B, T, C = x.shape
    S = ctx_1024.shape[1]
    E = ffn_W.shape[0]
    N = B * T
    slots = (N // P + E - 1) * P

    def scratch(name, shape):
        return nc.dram_tensor(name, shape, F32, kind="Internal").ap()

    x1 = scratch("x1", [B, T, C])
    h2T = scratch("h2T", [2, C // P, P, N])
    parts = [scratch(f"part{half}", [C // P, P, N]) for half in range(2)]
    x2 = scratch("x2", [N, C])
    expert_in = scratch("expert_in", [slots, C])
    expert_out = scratch("expert_out", [slots, C])

    window_attention(nc, B, T, x, attn_Wq, attn_bq, attn_Wk, attn_bk, attn_Wv, attn_bv, attn_Wo, attn_bo, x1, h2T)
    for half in range(2):
        cross_attention(nc, half, B, T, S, h2T, ctx_1024, mask, xattn_Wq, xattn_Wk, xattn_Wv, xattn_Wo, parts[half])
    expert_ffn(nc, B, T, x1, parts, ffn_wg, ffn_W, ffn_b, x2, expert_in, expert_out, out)


_INS = ['x', 'ctx_1024', 'mask_BxS2_bf1', 'L0_attn_Wq', 'L0_attn_bq', 'L0_attn_Wk', 'L0_attn_bk', 'L0_attn_Wv',
        'L0_attn_bv', 'L0_attn_Wo', 'L0_attn_bo', 'L0_xattn_Wq', 'L0_xattn_Wk', 'L0_xattn_Wv', 'L0_xattn_Wo',
        'L0_ffn_wg', 'L0_ffn_W', 'L0_ffn_b']
_OUTS = [((32, 112, 512), 'float32')]


def kernel(**inputs):
    import numpy as _np
    import concourse.bacc as _bacc
    from concourse import mybir as _mybir
    from concourse.bass_utils import run_bass_kernel_spmd as _run

    nc = _bacc.Bacc("TRN2", target_bir_lowering=False, num_devices=1)
    arrays, args = {}, []
    for name in _INS:
        a = _np.ascontiguousarray(inputs[name])
        arrays[f"in_{name}_dram"] = a
        args.append(nc.dram_tensor(f"in_{name}_dram", a.shape, _mybir.dt.from_np(a.dtype), kind="ExternalInput").ap())
    for i, (shape, dtype) in enumerate(_OUTS):
        dt = _mybir.dt.from_np(_np.dtype(dtype))
        args.append(nc.dram_tensor(f"out_{i}_dram", shape, dt, kind="ExternalOutput").ap())
    decoder_block(nc, *args)
    r = _run(nc, [arrays], core_ids=[0])
    got = tuple(r.results[0][f"out_{i}_dram"] for i in range(len(_OUTS)))
    return got[0]
```

```python
from contextlib import ExitStack, contextmanager

import numpy as np

import concourse.bass as bass
from concourse import mybir

F32 = mybir.dt.float32
F32R = mybir.dt.float32r
I32 = mybir.dt.int32
U32 = mybir.dt.uint32
ALU = mybir.AluOpType
ACT = mybir.ActivationFunctionType
AX = mybir.AxisListType
P = 128
HI, LO = 0, 1
PASSES = ((HI, HI), (HI, LO), (LO, HI))
NEG = 1.0e30


class Turn:

    def __init__(self, at, reg=None):
        self.at, self.reg = at, reg

    def count(self, per, more):
        if self.reg is None:
            return self.at * per + more
        return self.reg * per + (self.at * per + more)

    def before(self):
        return Turn(self.at - 1, self.reg)


def make_identity(pool, tile, done):
    pool.memset(tile, 0.0).then_inc(done, 1)
    pool.wait_ge(done, 1)
    pool.affine_select(out=tile, in_=tile, compare_op=ALU.not_equal, fill=1.0, base=0,
                       pattern=[[-1, tile.shape[-1]]], channel_multiplier=1).then_inc(done, 1)


@contextmanager
def semaphores(nc, phase):
    used = []

    def sem(name):
        used.append(nc.alloc_semaphore(name=f"{phase}_{name}"))
        return used[-1]

    yield sem
    nc.clear_and_free_semaphores(used)
    nc.all_engine_barrier()


class Fills:

    def __init__(self, head, first, full, last, tail, turns, banks):
        self.lists = {"head": head, "first": first, "full": full, "last": last, "tail": tail}
        self.turns, self.banks = turns, banks
        assert len(self.flat("full")) % banks == 0

    def flat(self, which):
        steps = self.lists[which]
        return [f for fs in steps for f in fs]

    def which(self, turn):
        if turn.reg is None and turn.at < 0:
            return "head"
        if turn.reg is None and turn.at == 0:
            return "first"
        if turn.reg is None and turn.at == self.turns:
            return "tail"
        return "last" if turn.reg is None and turn.at == self.turns - 1 else "full"

    def before(self, turn, kinds=None):
        def number(which):
            return sum(kinds is None or f[0] in kinds for f in self.flat(which))

        which = self.which(turn)
        if which == "head":
            return 0
        if which == "first":
            return number("head")
        if which == "tail":
            return self.before(Turn(self.turns - 1), kinds) + number("last")
        return turn.count(number("full"), number("head") + number("first") - number("full"))

    def until(self, turn, fill, kinds=None):
        flat = self.flat(self.which(turn))
        n = flat.index(fill) + 1
        return self.before(turn, kinds) + sum(kinds is None or f[0] in kinds for f in flat[:n])

    def bank(self, turn, fill):
        base = self.before(Turn(1) if turn.reg is not None else turn)
        return (base + self.flat(self.which(turn)).index(fill)) % self.banks

    def free(self, turn, fill):
        if turn.reg is None and self.until(turn, fill) <= self.banks:
            return 0
        return self.until(turn, fill) - self.banks


def window_attention(nc, B, T, x, Wq, bq, Wk, bk, Wv, bv, Wo, bo, x1, h2T, slots, rest):
    C = x.shape[2]
    KC = C // P
    WIN, D = 64, 32
    HEADS = C // D
    R0, R1 = WIN, T - WIN
    QT, KT = WIN // 2 + R1, WIN // 2 + WIN
    TB = 4
    TURNS = B // TB
    SCALE = float(1.0 / np.sqrt(D))
    EPS = 1e-5

    KQ = [("K", 0)] + [("Q", m) for m in range(KC)]
    HEAD = [[("N", s) for s in range(TB)] + KQ]
    FULL = [
        [("V", 0), ("O", 0), ("A", 0), ("W", 0), ("W", 1), ("M", 0)],
        [("O", 1), ("N", 0), ("A", 1), ("M", 1), ("N", 1)],
        [("O", 2), ("N", 2), ("A", 2), ("M", 2), ("N", 3)],
        [("O", 3), KQ[0], ("A", 3)] + KQ[1:] + [("M", 3)],
    ]
    FIRST = [[f for f in fs if not (f[0] == "A" and s < 1 or f[0] == "O" and s < 2 or f[0] == "M" and s < 3)]
             for s, fs in enumerate(FULL)]
    LAST = [[f for f in fs if f[0] not in "NKQ"] for fs in FULL]
    TAIL = [[("O", 0), ("A", 0), ("M", 0)], [("O", 1), ("M", 1)], [("M", 2)]]
    fills = Fills(HEAD, FIRST, FULL, LAST, TAIL, TURNS, 4)
    AHEAD = [([0], [1]), ([2], []), ([3], []), ([], [])]
    HALVED = "KQVWANM"

    def back(turn, s, n):
        return (turn, s - n) if s >= n else (turn.before(), s - n + TB)

    with ExitStack() as stack:
        def sb(name, shape, dt=F32):
            return stack.enter_context(nc.sbuf_tensor(f"w_{name}", shape, dt))

        sem = stack.enter_context(semaphores(nc, "w"))

        wq = sb("wq", [P, 2, KC, C], F32R)
        wk = sb("wk", [P, 2, KC, P], F32R)
        wv = sb("wv", [P, 2, KC, P], F32R)
        wo = sb("wo", [P, 2, KC, C], F32R)
        stage = sb("stage", [P, 2, 1024])
        bqs, bks, bvs = sb("bqs", [P, KC]), sb("bks", [P, 1]), sb("bvs", [P, 1])
        bos = sb("bos", [T, C])
        ident = sb("ident", [P, P])
        power = sb("power", [P, 1])
        xa = sb("xa", [T, TB, C])
        xr = sb("xr", [T, TB, C])
        h1 = sb("h1", [T, 2, C])
        h2 = sb("h2", [P, 2, C])
        hT = sb("hT", [P, 2, KC, TB, T], F32R)
        qa = sb("qa", [P, 2, KC, TB, T], F32R)
        qb = sb("qb", [P, 2, KC, TB, T], F32R)
        kd = sb("kd", [P, 2, TB, 2, 4 * WIN], F32R)
        vt = sb("vt", [WIN, 2, TB, 2, WIN])
        vd = sb("vd", [P, 2, TB, 2, 2, P], F32R)
        probs = sb("probs", [P, 2, HEADS // 2, WIN])
        pT = sb("pT", [P, 2, HEADS // 2, T], F32R)
        oT = sb("oT", [P, 2, 2, KC, T], F32R)
        hs = sb("hs", [P, 2, KC, 2 * T])
        top = sb("top", [T, 2, HEADS // 2])
        total = sb("total", [T, 2, HEADS // 2])
        inv = sb("inv", [T, 2, HEADS // 2])
        st1, st2 = sb("st1", [T, 2, 6]), sb("st2", [T, 2, 6])
        R = slots.shape[1]
        mark = sb("mark", [1, 1])
        blank = sb("blank", [P, 4, R])
        mv1, mv2 = sb("mv1", [T, 2, 2]), sb("mv2", [T, 2, 2])
        rs1, rs2 = sb("rs1", [T, 2, 1]), sb("rs2", [T, 2, 1])
        nb1, nb2 = sb("nb1", [T, 2, 1]), sb("nb2", [T, 2, 1])

        def bank(name):
            return stack.enter_context(nc.psum_tensor(f"w_{name}", [P, 512], F32))

        ps_s = [bank(f"ps_s{u}") for u in range(2)]
        ps_t = [bank(f"ps_t{u}") for u in range(2)]
        ps_f = [bank(f"ps_f{n}") for n in range(4)]

        w_in = [sem(f"w_in{n}") for n in range(4)]
        w_hi, w_lo, b_in = sem("w_hi"), sem("w_lo"), sem("b_in")
        ident_done, power_ready, zeroed = sem("ident"), sem("power"), sem("zeroed")
        xa_in = [sem(f"xa_in{s}") for s in range(TB)]
        xr_in = [sem(f"xr_in{s}") for s in range(TB)]
        blank_made, blank_out = sem("blank_made"), sem("blank_out")
        x1_out = [sem(f"x1_out{s}") for s in range(TB)]
        h2_out = [sem(f"h2_out{s}") for s in range(2)]
        st1_ready, mv1_ready, rs1_ready, h1_ready = sem("st1"), sem("mv1"), sem("rs1"), sem("h1")
        st2_ready, mv2_ready, rs2_ready, h2_ready = sem("st2"), sem("mv2"), sem("rs2"), sem("h2")
        ve1_ready, ve2_ready, pw1_ready, pw2_ready = sem("ve1"), sem("ve2"), sem("pw1"), sem("pw2")
        scores_ready, top_ready, less_ready, exp_ready = sem("scores"), sem("top"), sem("less"), sem("exp")
        total_ready, inv_ready, normed = sem("total"), sem("inv"), sem("normed")
        probsT_ready, pT_hi, pT_lo = sem("probsT"), sem("pT_hi"), sem("pT_lo")
        biased = sem("biased")
        fill_ready, fill_hi, fill_done = sem("fill_ready"), sem("fill_hi"), sem("fill_done")

        half = KC // 2
        stages = []
        for w, dst in ((Wq, wq), (Wo, wo)):
            for n in range(2):
                stages.append(([(w[n * half * P:(n + 1) * half * P, :].rearrange("(c p) n -> p c n", p=P), None)],
                               [dst[:, a, n * half:(n + 1) * half, :] for a in (HI, LO)], half))
        kv = 2 * D
        kv_src = [(w.rearrange("(c p) n -> p c n", p=P), (j, e)) for j, w in enumerate((Wk, Wv)) for e in range(2)]
        N_KV = 2

        rooms = [stage[:, 0, :], stage[:, 1, :], h2[:].rearrange("t n c -> t (n c)"),
                 probs[:].rearrange("t u h k -> t (u h k)")]
        ROOMS = len(rooms)

        def staged(n, c):
            return rooms[n % ROOMS].rearrange("p (c n) -> p c n", c=c)

        plan = [stages[0], stages[1], "kv", stages[2], stages[3]]
        KQ_PLAN = 3

        with nc.Block() as block:
            loop = TURNS - 2

            @block.sync
            def _(sp):
                def row(turn, s):
                    n = turn.count(TB, s)
                    return sp.snap(n) if turn.reg is not None else n

                def load_xa(turn, s, free):
                    n = row(turn, s)
                    if free is not None:
                        sp.wait_ge(h1_ready, free)
                        sp.nop(nofuse=True)
                    sp.dma_start(xa[:, s, :], x[bass.ds(n, 1)].rearrange("a t c -> (a t) c")).then_inc(xa_in[s], 16)

                def load_xr(turn, s):
                    n = row(turn, s)
                    if not (turn.reg is None and turn.at == 0):
                        sp.wait_ge(h2_ready, turn.count(TB, s + 1 - TB))
                        sp.nop(nofuse=True)
                        sp.wait_ge(x1_out[s], turn.count(16, 0))
                        sp.nop(nofuse=True)
                    sp.dma_start(xr[:, s, :], x[bass.ds(n, 1)].rearrange("a t c -> (a t) c")).then_inc(xr_in[s], 16)

                for s in range(TB):
                    load_xa(Turn(0), s, None)
                def load_w(n, what):
                    if what == "kv":
                        for src, (j, e) in kv_src:
                            at = staged(n, 2 * KC)[:, j * KC:(j + 1) * KC, e * kv:(e + 1) * kv]
                            sp.dma_start(at, src).then_inc(w_in[n % ROOMS], 16)
                    else:
                        sp.dma_start(staged(n, half), what[0][0][0]).then_inc(w_in[n % ROOMS], 16)

                for n, what in enumerate(plan[:ROOMS]):
                    load_w(n, what)
                for c in range(KC):
                    sp.dma_start(bqs[:, c:c + 1], bq[c * P:(c + 1) * P].rearrange("(p a) -> p a", a=1)) \
                        .then_inc(b_in, 16)
                for e in range(2):
                    sp.dma_start(bks[e * kv:(e + 1) * kv, :], bk.rearrange("(p a) -> p a", a=1)).then_inc(b_in, 16)
                    sp.dma_start(bvs[e * kv:(e + 1) * kv, :], bv.rearrange("(p a) -> p a", a=1)).then_inc(b_in, 16)
                sp.dma_start(bos[:], bo.rearrange("(a n) -> a n", a=1).to_broadcast([T, C])).then_inc(b_in, 16)
                for n, what in enumerate(plan[ROOMS:], ROOMS):
                    sp.wait_ge(w_lo, n - ROOMS + 1)
                    load_w(n, what)

                def store_x1(turn, s, at, f):
                    n = turn.count(TB, s)
                    n = sp.snap(n) if turn.reg is not None else n
                    sp.wait_ge(fill_done, fills.until(at, f))
                    sp.nop(nofuse=True)
                    sp.dma_start(x1[bass.ds(n, 1)].rearrange("a t c -> (a t) c"), xr[:, s, :]).then_inc(x1_out[s], 16)

                def store_h2(turn, s, at, f):
                    t = turn.count(TB * T, (s - 1) * T)
                    t = sp.snap(t) if turn.reg is not None else t
                    sp.wait_ge(fill_done, fills.until(at, f))
                    sp.nop(nofuse=True)
                    sp.dma_start(h2T[:, :, bass.ds(t, 2 * T)].rearrange("c p t -> p c t"), hs[:, s // 2]) \
                        .then_inc(h2_out[s // 2], 16)

                def stores(turn, s, fs):
                    for f in fs:
                        if f[0] == "O":
                            store_x1(*back(turn, s, 2), turn, f)
                        if f[0] == "M" and (s - 3) % 2:
                            store_h2(*back(turn, s, 3), turn, f)

                slots_t = slots.rearrange("(n p) r -> p n r", p=P)
                SLOTS = slots_t.shape[1]
                assert 4 * TURNS <= SLOTS < 4 * TURNS + 4

                def clear_slots(turn):
                    n = turn.count(4, 0)
                    n = sp.snap(n) if turn.reg is not None else n
                    sp.dma_start(slots_t[:, bass.ds(n, 4), :], blank[:]).then_inc(blank_out, 16)

                def turn_of(turn, last=False):
                    for s, fs in enumerate(fills.lists[fills.which(turn)]):
                        if s == 2:
                            clear_slots(turn)
                        if s == 0 and not last:
                            for n in range(TB):
                                load_xa(Turn(turn.at + 1, turn.reg), n, turn.count(TB, n + 1))
                        load_xr(turn, s)
                        stores(turn, s, fs)

                sp.wait_ge(blank_made, 2)
                turn_of(Turn(0))
                with sp.Fori(0, loop) as j:
                    turn_of(Turn(1, j))
                sp.dma_start(slots_t[:, 4 * TURNS:SLOTS, :], blank[:, 0:SLOTS - 4 * TURNS, :]).then_inc(blank_out, 16)
                sp.dma_start(rest.rearrange("(n p) c -> p n c", p=P), blank[:, :, 0:C]).then_inc(blank_out, 16)
                turn_of(Turn(TURNS - 1), last=True)
                for s, fs in enumerate(TAIL):
                    stores(Turn(TURNS), s, fs)
                sp.wait_ge(blank_out, 16 * (TURNS + 2))
                for s in range(TB):
                    sp.wait_ge(x1_out[s], 16 * TURNS)
                for s in range(2):
                    sp.wait_ge(h2_out[s], 16 * TURNS)

            B_ALL = 16 * (KC + 5)

            @block.gpsimd
            def _(pool):
                make_identity(pool, ident[:], ident_done)
                pool.wait_ge(power_ready, 1)

                def factors(turn, s, mv, rs, nb, mv_ready, ve_ready, pw_ready, rs_ready):
                    par = s % 2
                    pool.wait_ge(mv_ready, turn.count(TB, s + 1))
                    pool.nop(nofuse=True)
                    pool.tensor_scalar(rs[:, par, :], mv[:, par, 1:2], EPS, None, ALU.add).then_inc(ve_ready, 1)
                    pool.wait_ge(ve_ready, turn.count(TB, s + 1))
                    pool.nop(nofuse=True)
                    pool.tensor_tensor(rs[:, par, :], rs[:, par, :], power[0:T, :], ALU.pow).then_inc(pw_ready, 1)
                    pool.wait_ge(pw_ready, turn.count(TB, s + 1))
                    pool.nop(nofuse=True)
                    pool.tensor_scalar(nb[:, par, :], mv[:, par, 0:1], rs[:, par, :], -1.0, ALU.mult, ALU.mult) \
                        .then_inc(rs_ready, 1)

                def factors1(turn, s):
                    factors(turn, s, mv1, rs1, nb1, mv1_ready, ve1_ready, pw1_ready, rs1_ready)

                def factors2(turn, s):
                    factors(turn, s, mv2, rs2, nb2, mv2_ready, ve2_ready, pw2_ready, rs2_ready)

                def add_bias(turn, s):
                    pool.wait_ge(xr_in[s], turn.count(16, 16))
                    pool.nop(nofuse=True)
                    pool.tensor_tensor(xr[:, s, :], xr[:, s, :], bos[:], ALU.add).then_inc(biased, 1)

                def normalise(turn, s):
                    for u in range(2):
                        pool.wait_ge(inv_ready, turn.count(8, 2 * s + u + 1))
                        pool.nop(nofuse=True)
                        pool.tensor_tensor(probs[0:T, u], probs[0:T, u],
                                           inv[:, u, :].unsqueeze(2).to_broadcast([T, HEADS // 2, WIN]),
                                           ALU.mult).then_inc(normed, 1)

                def turn_of(turn, last=False):
                    first = turn.reg is None and turn.at == 0
                    for s in range(TB):
                        if not last:
                            for n in AHEAD[s][0]:
                                factors1(Turn(turn.at + 1, turn.reg), n)
                        normalise(turn, s)
                        if not last:
                            for n in AHEAD[s][1]:
                                factors1(Turn(turn.at + 1, turn.reg), n)
                        if not (first and s < 1):
                            add_bias(*back(turn, s, 1))
                        if not (first and s < 2):
                            factors2(*back(turn, s, 2))

                for a in (HI, LO):
                    pool.memset(kd[:, a].bitcast(F32), 0.0).then_inc(zeroed, 1)
                for s in range(TB):
                    factors1(Turn(0), s)
                for a in (HI, LO):
                    pool.memset(vd[:, a].bitcast(F32), 0.0).then_inc(zeroed, 1)
                pool.memset(blank[:], 0.0).then_inc(blank_made, 1)
                pool.wait_ge(blank_made, 1)
                pool.iota(blank[:, :, R - 1:R].rearrange("p n a -> p (n a)").bitcast(I32), pattern=[[P, 4]],
                          base=B * T, channel_multiplier=1).then_inc(blank_made, 1)
                pool.wait_ge(b_in, B_ALL)
                turn_of(Turn(0))
                with pool.Fori(0, loop) as j:
                    turn_of(Turn(1, j))
                turn_of(Turn(TURNS - 1), last=True)
                add_bias(Turn(TURNS - 1), TB - 1)
                factors2(Turn(TURNS - 1), 2)
                factors2(Turn(TURNS - 1), 3)

            def places(f, b):
                kind, n = f
                if kind == "K":
                    src = b[:, 0:TB * KT].rearrange("p (b t) -> p b t", b=TB)
                    return [(src[D * j:D * (j + 1), :, 32 * w:32 * w + WIN],
                             *[kd[D * j:D * (j + 1), a, :, w, WIN * j:WIN * (j + 1)] for a in (HI, LO)],
                             bks[D * j:D * (j + 1), :]) for w in range(2) for j in range(4)]
                if kind == "Q":
                    src = b[:, 0:TB * QT].rearrange("p (b t) -> p b t", b=TB)
                    return [(src[:, :, 0:R0], *[qa[:, a, n, :, 0:R0] for a in (HI, LO)], bqs[:, n:n + 1]),
                            (src[:, :, WIN // 2:QT], *[qb[:, a, n, :, R0:T] for a in (HI, LO)], bqs[:, n:n + 1])]
                if kind == "W":
                    src = b[:, 0:TB * WIN].rearrange("p (b t) -> p b t", b=TB)
                    return [(src[WIN * g:WIN * (g + 1), :, D * g:D * (g + 1)],
                             *[vd[WIN * g:WIN * (g + 1), a, :, n, q, WIN * q + D * g:WIN * q + D * (g + 1)]
                               for a in (HI, LO)], None) for q in range(2) for g in range(2)]
                src = b[:, 0:KC * T].rearrange("p (c t) -> p c t", c=KC)
                if kind == "N":
                    return [(src, *[hT[:, a, :, n, :] for a in (HI, LO)], None)]
                if kind == "A":
                    par = (n - 1) % 2
                    return [(src, *[oT[:, par, a] for a in (HI, LO)], None)]
                batch = (n - 3) % TB
                return [(src, hs[:, batch // 2, :, (batch % 2) * T:(batch % 2 + 1) * T], None, None)]

            @block.scalar
            def _(act):
                def both_windows(b, j):
                    w0 = b[D * j:D * (j + 1), 0:TB * KT].rearrange("p (b t) -> p b t", b=TB)[:, :, 0:WIN]
                    parts, batches, keys = w0.ap
                    return bass.AP(tensor=w0.tensor, offset=w0.offset, ap=[parts, batches, [WIN // 2, 2], keys])

                def fill(turn, f):
                    b = ps_f[fills.bank(turn, f)]
                    act.wait_ge(fill_ready, fills.until(turn, f))
                    if f[0] == "V":
                        src = b[0:WIN, 0:TB * KT].rearrange("p (b t) -> p b t", b=TB)[:, :, 0:WIN]
                        for e in range(2):
                            last = act.activation(vt[:, 0, :, e, :], src, ACT.Identity, bias=bvs[0:WIN, :])
                        last.then_inc(fill_hi, 1)
                        return
                    if f[0] == "M" and f[1] % 2 and not (turn.reg is None and turn.at == 0):
                        act.wait_ge(h2_out[((f[1] - 3) % TB) // 2], turn.count(16, 0) if f[1] == 3 else turn.count(16, -16))
                    if f[0] == "K":
                        for j in range(4):
                            last = act.activation(kd[D * j:D * (j + 1), HI, :, :, WIN * j:WIN * (j + 1)], both_windows(b, j),
                                                  ACT.Identity, bias=bks[D * j:D * (j + 1), :])
                        last.then_inc(fill_hi, 1)
                        return
                    for src, hi, lo, bias in places(f, b):
                        if bias is None:
                            last = act.activation(hi, src, ACT.Copy)
                        else:
                            last = act.activation(hi, src, ACT.Identity, bias=bias)
                    last.then_inc(fill_hi, 1)

                def probsT(turn, s):
                    for u in range(2):
                        act.wait_ge(probsT_ready, turn.count(8, 2 * s + u + 1))
                        act.activation(pT[:, HI, 4 * u:4 * u + 4, :],
                                       ps_t[u][:, 0:4 * T].rearrange("p (c t) -> p c t", c=4), ACT.Copy) \
                            .then_inc(pT_hi, 1)

                def exps(turn, s):
                    for u in range(2):
                        act.wait_ge(less_ready, turn.count(8, 2 * s + u + 1))
                        act.activation(probs[0:T, u], probs[0:T, u], ACT.Exp, scale=SCALE).then_inc(exp_ready, 1)

                def norm(turn, s, xin, rs, nb, h, rs_ready, free, done):
                    par = s % 2
                    act.wait_ge(rs_ready, turn.count(TB, s + 1))
                    if free is not None:
                        act.wait_ge(fill_ready, free)
                    act.activation(h[0:T, par, :], xin[:, s, :], ACT.Identity, bias=nb[:, par, :], scale=rs[:, par, :]) \
                        .then_inc(done, 1)

                def norm1(turn, s):
                    at = turn.before()
                    if at.reg is None and at.at < 0:
                        free = fills.until(at, ("N", s - 2)) if s >= 2 else None
                    elif s >= 2:
                        free = fills.until(at, ("N", s - 2))
                    else:
                        free = fills.until(at.before(), ("N", s + 2))
                    norm(turn, s, xa, rs1, nb1, h1, rs1_ready, free, h1_ready)

                def norm2(turn, s):
                    first = turn.reg is None and turn.at == 0
                    at, step = (turn, s + 1) if s + 1 < TB else (Turn(turn.at + 1, turn.reg), 0)
                    free = None if first and s < 2 else fills.until(at, ("M", step))
                    norm(turn, s, xr, rs2, nb2, h2, rs2_ready, free, h2_ready)

                def step(turn, s, fs, kinds):
                    first = turn.reg is None and turn.at == 0
                    if "T" in kinds and not (first and s < 1):
                        probsT(*back(turn, s, 1))
                    if not (first and s < 3):
                        norm2(*back(turn, s, 3))
                    if "S" in kinds:
                        exps(turn, s)
                    early, late = AHEAD[s] if fills.which(turn) in ("first", "full") else ([], [])
                    if ("A", s) not in fs:
                        for n in early:
                            norm1(Turn(turn.at + 1, turn.reg), n)
                    for f in fs:
                        if f[0] == "A":
                            for n in early:
                                norm1(Turn(turn.at + 1, turn.reg), n)
                        if f == fs[-1]:
                            for n in late:
                                norm1(Turn(turn.at + 1, turn.reg), n)
                        if f[0] in HALVED:
                            fill(turn, f)

                def turn_of(turn):
                    for s, fs in enumerate(fills.lists[fills.which(turn)]):
                        step(turn, s, fs, "TS")

                def split(n, what):
                    arrivals = sum(len(kv_src) if plan[m] == "kv" else 1 for m in range(n % ROOMS, n + 1, ROOMS))
                    act.wait_ge(w_in[n % ROOMS], 16 * arrivals)
                    if what == "kv":
                        act.activation(wk[:, HI], staged(n, 2 * KC)[:, 0:KC], ACT.Copy)
                        act.activation(wv[:, HI], staged(n, 2 * KC)[:, KC:2 * KC], ACT.Copy).then_inc(w_hi, 1)
                    else:
                        act.activation(what[1][HI], staged(n, half), ACT.Copy).then_inc(w_hi, 1)

                norm1(Turn(0), 0)
                norm1(Turn(0), 1)
                for n in range(TB):
                    fill(Turn(-1), ("N", n))
                    if n + 2 < TB:
                        norm1(Turn(0), n + 2)
                for n in range(KQ_PLAN):
                    split(n, plan[n])
                act.wait_ge(b_in, B_ALL)
                act.wait_ge(zeroed, 5)
                for f in KQ:
                    fill(Turn(-1), f)
                for n in range(KQ_PLAN, len(plan)):
                    split(n, plan[n])
                turn_of(Turn(0))
                with act.Fori(0, loop) as j:
                    turn_of(Turn(1, j))
                turn_of(Turn(TURNS - 1))
                for s, fs in enumerate(TAIL):
                    step(Turn(TURNS), s, fs, "T" if s == 0 else "")

            @block.vector
            def _(dve):
                dve.memset(power[:], -0.5).then_inc(power_ready, 1)
                for a in (HI, LO):
                    dve.memset(qa[:, a, :, :, R0:T].bitcast(F32), 0.0)
                    last = dve.memset(qb[:, a, :, :, 0:R0].bitcast(F32), 0.0)
                last.then_inc(zeroed, 1)

                def split(n, what):
                    dve.wait_ge(w_hi, n + 1)
                    if what == "kv":
                        dve.tensor_tensor(wk[:, LO], staged(n, 2 * KC)[:, 0:KC], wk[:, HI].bitcast(F32), ALU.subtract)
                        dve.tensor_tensor(wv[:, LO], staged(n, 2 * KC)[:, KC:2 * KC], wv[:, HI].bitcast(F32),
                                          ALU.subtract).then_inc(w_lo, 1)
                    else:
                        dve.tensor_tensor(what[1][LO], staged(n, half), what[1][HI].bitcast(F32), ALU.subtract) \
                            .then_inc(w_lo, 1)

                def stats(turn, s, xin, st, mv, st_ready, mv_ready):
                    dve.bn_stats(st[:, s % 2, :], xin[:, s, :]).then_inc(st_ready, 1)
                    dve.wait_ge(st_ready, turn.count(TB, s + 1))
                    dve.nop(nofuse=True)
                    dve.bn_aggr(mv[:, s % 2, :], st[:, s % 2, :]).then_inc(mv_ready, 1)

                def stats1(turn, s):
                    dve.wait_ge(xa_in[s], turn.count(16, 16))
                    if not (turn.reg is None and turn.at == 0 and s < 2):
                        dve.wait_ge(h1_ready, turn.count(TB, s - 1))
                    stats(turn, s, xa, st1, mv1, st1_ready, mv1_ready)

                def fill(turn, f):
                    b = ps_f[fills.bank(turn, f)]
                    dve.wait_ge(fill_hi, fills.until(turn, f, HALVED))
                    if f[0] == "M":
                        dve.wait_ge(fill_done, fills.until(turn, f) - 1)
                        dve.nop(nofuse=True)
                        dve.memset(mark[:], 0.0).then_inc(fill_done, 1)
                        return
                    if f[0] == "V":
                        src = b[0:WIN, 0:TB * KT].rearrange("p (b t) -> p b t", b=TB)[:, :, WIN // 2:WIN // 2 + WIN]
                        for e in range(2):
                            last = dve.tensor_scalar(vt[:, 1, :, e, :], src, bvs[0:WIN, :], None, ALU.add)
                        last.then_inc(fill_done, 1)
                        return
                    for src, hi, lo, bias in places(f, b):
                        if bias is None:
                            last = dve.tensor_tensor(lo, src, hi.bitcast(F32), ALU.subtract)
                        else:
                            last = dve.scalar_tensor_tensor(out=lo, in0=src, scalar=bias, in1=hi.bitcast(F32),
                                                            op0=ALU.add, op1=ALU.subtract)
                    last.then_inc(fill_done, 1)

                def probsT(turn, s):
                    for u in range(2):
                        dve.wait_ge(pT_hi, turn.count(8, 2 * s + u + 1))
                        dve.tensor_tensor(pT[:, LO, 4 * u:4 * u + 4, :],
                                          ps_t[u][:, 0:4 * T].rearrange("p (c t) -> p c t", c=4),
                                          pT[:, HI, 4 * u:4 * u + 4, :].bitcast(F32), ALU.subtract) \
                            .then_inc(pT_lo, 1)

                def less_top(turn, s):
                    for u in range(2):
                        n = turn.count(8, 2 * s + u + 1)
                        scores = ps_s[u][0:T, :].rearrange("p (h k) -> p h k", k=WIN)
                        dve.wait_ge(scores_ready, n)
                        dve.tensor_reduce(top[:, u, :], scores, AX.X, ALU.max).then_inc(top_ready, 1)
                        dve.wait_ge(top_ready, n)
                        if not (turn.reg is None and turn.at == 0 and s == 0):
                            dve.wait_ge(probsT_ready, turn.count(8, 2 * s + u - 1))
                        dve.tensor_tensor(probs[0:T, u], scores,
                                          top[:, u, :].unsqueeze(2).to_broadcast([T, HEADS // 2, WIN]),
                                          ALU.subtract).then_inc(less_ready, 1)

                def totals(turn, s, u):
                    n = turn.count(8, 2 * s + u + 1)
                    dve.wait_ge(exp_ready, n)
                    dve.tensor_reduce(total[:, u, :], probs[0:T, u], AX.X, ALU.add).then_inc(total_ready, 1)
                    dve.wait_ge(total_ready, n)
                    dve.reciprocal(inv[:, u, :], total[:, u, :]).then_inc(inv_ready, 1)

                def residual(at, f, turn, s):
                    dve.wait_ge(fill_ready, fills.until(at, f))
                    dve.wait_ge(biased, turn.count(TB, s + 1))
                    dve.tensor_tensor(xr[:, s, :], ps_f[fills.bank(at, f)][0:T, :], xr[:, s, :], ALU.add) \
                        .then_inc(fill_done, 1)
                    dve.wait_ge(fill_done, fills.until(at, f))
                    if not (turn.reg is None and turn.at == 0 and s < 2):
                        dve.wait_ge(h2_ready, turn.count(TB, s - 1))
                    dve.bn_stats(st2[:, s % 2, :], xr[:, s, :]).then_inc(st2_ready, 1)
                    dve.wait_ge(st2_ready, turn.count(TB, s + 1))
                    dve.nop(nofuse=True)
                    dve.bn_aggr(mv2[:, s % 2, :], st2[:, s % 2, :]).then_inc(mv2_ready, 1)

                def step(turn, s, fs, kinds):
                    first = turn.reg is None and turn.at == 0
                    early, late = AHEAD[s] if fills.which(turn) in ("first", "full") else ([], [])
                    for n in early:
                        stats1(Turn(turn.at + 1, turn.reg), n)
                    if "T" in kinds and not (first and s < 1):
                        probsT(*back(turn, s, 1))
                    if "S" in kinds:
                        less_top(turn, s)
                        totals(turn, s, 0)
                    for n in late:
                        stats1(Turn(turn.at + 1, turn.reg), n)
                    if "S" in kinds:
                        totals(turn, s, 1)
                    for f in fs:
                        if f[0] == "O":
                            residual(turn, f, *back(turn, s, 2))
                        else:
                            fill(turn, f)

                def turn_of(turn):
                    for s, fs in enumerate(fills.lists[fills.which(turn)]):
                        step(turn, s, fs, "TS")

                for s in range(TB):
                    stats1(Turn(0), s)
                for n in range(TB):
                    fill(Turn(-1), ("N", n))
                for n in range(KQ_PLAN):
                    split(n, plan[n])
                for f in KQ:
                    fill(Turn(-1), f)
                for n in range(KQ_PLAN, len(plan)):
                    split(n, plan[n])
                dve.wait_ge(w_lo, len(plan))
                turn_of(Turn(0))
                with dve.Fori(0, loop) as j:
                    turn_of(Turn(1, j))
                turn_of(Turn(TURNS - 1))
                for s, fs in enumerate(TAIL):
                    step(Turn(TURNS), s, fs, "T" if s == 0 else "")

            @block.tensor
            def _(pe):
                pe.wait_ge(ident_done, 2)

                def product(out, jobs):
                    for m, (w, r) in enumerate(jobs):
                        last = pe.matmul(out, w, r, start=m == 0, stop=m == len(jobs) - 1)
                    return last

                def fill(turn, f):
                    kind, n = f
                    k = fills.free(turn, f)
                    if not (isinstance(k, int) and k == 0):
                        pe.wait_ge(fill_done, k)
                        if turn.reg is not None and (kind in "KOW" or (kind, n) == ("A", 0)):
                            pe.nop(nofuse=True)
                    out = ps_f[fills.bank(turn, f)]
                    if kind in "NM":
                        at, s = (Turn(turn.at + 1, turn.reg), n) if kind == "N" else back(turn, n, 3)
                        h, ready = (h1, h1_ready) if kind == "N" else (h2, h2_ready)
                        pe.wait_ge(ready, at.count(TB, s + 1))
                        for c in range(KC):
                            last = pe.transpose(out[:, c * T:(c + 1) * T], h[0:T, s % 2, c * P:(c + 1) * P],
                                                ident[0:T, 0:T])
                    elif kind in "KV":
                        w = wk if kind == "K" else wv
                        if kind == "K":
                            pe.wait_ge(fill_done, fills.until(turn, ("N", TB - 1)))
                        last = product(out[:, 0:TB * KT].rearrange("p (b t) -> p b t", b=TB),
                                       [(w[:, a, c, :], hT[:, b_, c, :, 0:KT]) for c in range(KC) for a, b_ in PASSES])
                    elif kind == "Q":
                        last = product(out[:, 0:TB * QT].rearrange("p (b t) -> p b t", b=TB),
                                       [(wq[:, a, c, n * P:(n + 1) * P], hT[:, b_, c, :, 0:QT])
                                        for c in range(KC) for a, b_ in PASSES])
                    elif kind == "W":
                        pe.wait_ge(fill_done, fills.until(turn, ("V", 0)))
                        pe.nop(nofuse=True)
                        for b in range(TB):
                            last = pe.transpose(out[:, b * WIN:(b + 1) * WIN], vt[:, n, b, :, :].rearrange("p e k -> p (e k)"),
                                                ident[0:WIN, 0:WIN])
                    elif kind == "A":
                        at, s = back(turn, n, 1)
                        pe.wait_ge(pT_lo, at.count(8, 2 * s + 2))
                        if s == 0:
                            pe.wait_ge(fill_done, fills.until(at, ("W", 1)))
                        rows = out[:, 0:KC * T].rearrange("p (c t) -> p c t", c=KC)
                        for w, (lo, hi) in enumerate(((0, R0), (R0, T))):
                            last = product(rows[:, :, lo:hi],
                                           [(vd[:, a, s, w, q, :],
                                             pT[:, b_].rearrange("p (c q) t -> p q c t", q=2)[:, q, :, lo:hi])
                                            for q in range(2) for a, b_ in PASSES])
                    else:
                        at, s = back(turn, n, 2)
                        a_turn, a_step = (at, s + 1) if s + 1 < TB else (Turn(at.at + 1, at.reg), 0)
                        pe.wait_ge(fill_done, fills.until(a_turn, ("A", a_step)))
                        if turn.reg is None and (turn.at, n) == (0, 2):
                            pe.wait_ge(w_lo, len(plan))
                        last = product(out[0:T, :], [(oT[:, s % 2, a, c, :], wo[:, b_, c, :])
                                                     for c in range(KC) for a, b_ in PASSES])
                    last.then_inc(fill_ready, 1)

                def scores(turn, s):
                    if s == 0:
                        pe.wait_ge(fill_done, fills.until(turn.before(), ("Q", KC - 1)))
                    for u in range(2):
                        if not (turn.reg is None and turn.at == 0 and s == 0):
                            pe.wait_ge(less_ready, turn.count(8, 2 * s + u - 1))
                        for m in range(2 * u, 2 * u + 2):
                            last = product(ps_s[u][0:T, (m % 2) * 4 * WIN:(m % 2 + 1) * 4 * WIN],
                                           [(q[:, a, m, s, :], kd[:, b_, s, w, :])
                                            for w, q in enumerate((qa, qb)) for a, b_ in PASSES])
                        last.then_inc(scores_ready, 1)

                def probsT(turn, s):
                    for u in range(2):
                        pe.wait_ge(normed, turn.count(8, 2 * s + u + 1))
                        if not (turn.reg is None and turn.at == 0 and s == 0):
                            pe.wait_ge(pT_lo, turn.count(8, 2 * s + u - 1))
                        for c in range(4):
                            last = pe.transpose(ps_t[u][:, c * T:(c + 1) * T],
                                                probs[0:T, u, 2 * c:2 * c + 2, :].rearrange("p h k -> p (h k)"),
                                                ident[0:T, 0:T])
                        last.then_inc(probsT_ready, 1)

                def turn_of(turn):
                    first = turn.reg is None and turn.at == 0
                    for s, fs in enumerate(fills.lists[fills.which(turn)]):
                        if not (first and s < 1):
                            probsT(*back(turn, s, 1))
                        scores(turn, s)
                        for f in fs:
                            fill(turn, f)

                for s in range(TB):
                    fill(Turn(-1), ("N", s))
                pe.wait_ge(zeroed, 5)
                pe.wait_ge(w_lo, KQ_PLAN)
                for f in KQ:
                    fill(Turn(-1), f)
                turn_of(Turn(0))
                with pe.Fori(0, loop) as j:
                    turn_of(Turn(1, j))
                turn_of(Turn(TURNS - 1))
                for s, fs in enumerate(TAIL):
                    if s == 0:
                        probsT(Turn(TURNS - 1), TB - 1)
                    for f in fs:
                        fill(Turn(TURNS), f)


def cross_attention(nc, half, B, T, S, h2T, ctx, mask, Wq, Wk, Wv, Wo, base, result):
    D = 128
    C = h2T.shape[0] * P
    KC = C // P
    CD = ctx.shape[2]
    CC = CD // P
    G = 4
    H = 2 * G
    SE = S + S % 2
    CHUNKS = [(k, min(P, SE - k)) for k in range(0, SE, P)]
    NKC = len(CHUNKS)
    WIDE = NKC * P
    assert 0 < SE - S or S % 2 == 0
    T2 = 2 * T
    TURNS = B // 2
    SCALE = float(1.0 / np.sqrt(D))
    mdt = mask.dtype

    LATE = [("Q", 0, 3), ("K", 0, 3), ("V", 0, 1), ("V", 0, 2)]
    FULL = [
        [("Q", 0, 3), ("K", 1, 0), ("V", 0, 1)],
        [("K", 0, 3), ("V", 0, 2), ("K", 1, 1), ("V", 1, 0)],
        [("O", 0, 1)],
        [("K", 1, 2), ("C", 0, 0), ("V", 1, 1), ("C", 0, 1)],
        [("K", 1, 3), ("V", 1, 2), ("Q", 0, 0)],
        [("K", 0, 0), ("Q", 0, 1)],
        [("K", 0, 1), ("Q", 0, 2)],
        [("O", 1, 0), ("K", 0, 2), ("C", 1, 0), ("V", 0, 0), ("C", 1, 1)],
    ]
    HEAD = [f for f in [("C", 0, 0), ("C", 0, 1)] + [("K", 0, g) for g in range(G)] + [("V", 0, c) for c in range(NKC)] +
            [("C", 1, 0), ("C", 1, 1)] + [("Q", 0, g) for g in range(G)] if f not in LATE]
    FIRST = [[f for f in fs if f != ("O", 0, 1)] for fs in FULL]
    LAST = [[f for f in fs if f[0] == "O" or f in LATE or (f[0] in "KV" and f[1] == 1)] for fs in FULL]
    TAIL = [("O", 0, 1)]
    NF = sum(map(len, FULL))
    NF0 = sum(map(len, FIRST))
    BASE = len(HEAD) + NF0 - NF
    flat = [f for fs in FULL for f in fs]
    flat0 = [f for fs in FIRST for f in fs]
    flatl = [f for fs in LAST for f in fs]

    def fills_until(turn, fill):
        if turn.reg is None and turn.at == -1:
            return HEAD.index(fill) + 1
        if turn.reg is None and turn.at == 0:
            return len(HEAD) + flat0.index(fill) + 1
        if turn.reg is None and turn.at == TURNS - 1:
            return BASE + NF * turn.at + flatl.index(fill) + 1
        return turn.count(NF, BASE + flat.index(fill) + 1)

    def halved(turn, fill):
        if turn.reg is None and turn.at < 0:
            return fills_until(turn, fill)
        own = flat if turn.reg is not None else {0: flat0, TURNS - 1: flatl}.get(turn.at, flat)
        return turn.count(NF - 2, len(HEAD) + sum(f[0] != "O" for f in own[:own.index(fill) + 1]))

    def made(turn, fill):
        return fills_until(turn if fill[1] == 1 or fill in LATE else turn.before(), fill)

    def fills_of(turn):
        steps = LAST if turn.at == TURNS - 1 else FIRST if turn.at == 0 and turn.reg is None else FULL
        n, out = 0, []
        for fs in steps:
            row = []
            for f in fs:
                if turn.at == 0 and turn.reg is None:
                    before = len(HEAD) + n
                    row.append((f, before, before % 3))
                else:
                    row.append((f, turn.count(NF, BASE + n), (BASE + n) % 3))
                n += 1
            out.append(row)
        return out

    assert NF % 3 == 0 and BASE >= 0

    with ExitStack() as stack:
        def sb(name, shape, dt=F32):
            return stack.enter_context(nc.sbuf_tensor(f"x{half}_{name}", shape, dt))

        sem = stack.enter_context(semaphores(nc, f"x{half}"))

        wq = sb("wq", [P, 2, KC, H * D], F32R)
        wk = sb("wk", [P, 2, CC, G * D], F32R)
        wv = sb("wv", [P, 2, CC, G * D], F32R)
        wo = sb("wo", [P, 2, H, C], F32R)
        stage = sb("stage", [P, 4, 512])
        ident = sb("ident", [P, P])
        xf = sb("xf", [P, KC, T2])
        x2 = sb("xT", [P, 2, KC, T2], F32R)
        ctxn = sb("ctxn", [P, 2, NKC, CD])
        ctxT = sb("ctxT", [P, 2, 2, CC, SE], F32R)
        kT = sb("kT", [P, 2, G, SE], F32R)
        v = sb("v", [P, 2, 2, NKC, G * D], F32R)
        qT = sb("qT", [P, 2, H, T2], F32R)
        oT = sb("oT", [P, 2, H, T2], F32R)
        probs = sb("probs", [P, 4, WIDE])
        pT = sb("pT", [P, 2, 2, NKC, T2], F32R)
        mraw = sb("mraw", [T, 2, S], mdt)
        mrow = sb("mrow", [T, 2, SE])
        top = sb("top", [T, 4])
        bias = sb("bias", [T, 4])
        total = sb("total", [T, 4])
        inv = sb("inv", [T, 4])
        sums = sb("sums", [P, 2, C])

        def bank(name):
            return stack.enter_context(nc.psum_tensor(f"x{half}_{name}", [P, 512], F32))

        ps_s = [bank(f"ps_s{h}") for h in range(2)]
        ps_t = [bank(f"ps_t{h}") for h in range(2)]
        ps_o = bank("ps_o")
        ps_f = [bank(f"ps_f{n}") for n in range(3)]

        w_in = [sem(f"w_in{n}") for n in range(9)]
        w_hi, w_lo = sem("w_hi"), sem("w_lo")
        ident_done = sem("ident_done")
        padded = sem("padded")
        ctx_in = [sem(f"ctx_in{n}") for n in range(2)]
        mask_in = [sem(f"mask_in{n}") for n in range(2)]
        x_in, x_hi, x_lo = sem("x_in"), sem("x_hi"), sem("x_lo")
        mrow_ready = sem("mrow_ready")
        scores_ready, masked, bias_ready, exp_ready = sem("scores"), sem("masked"), sem("bias_ready"), sem("exp")
        total_ready, inv_ready, normed, probsT_ready = sem("total"), sem("inv_ready"), sem("normed"), sem("probsT")
        pT_hi, pT_lo, pv_ready, o_hi, o_lo = sem("pT_hi"), sem("pT_lo"), sem("pv"), sem("o_hi"), sem("o_lo")
        fill_ready, fill_hi, fill_done = sem("fill_ready"), sem("fill_hi"), sem("fill_done")
        base_in = [sem(f"base_in{n}") for n in range(2)]
        stored = [sem(f"stored{n}") for n in range(2)]

        WIDTH = 512
        lo_col = half * H * D
        kv_col = half * G * D
        stages = [(W[c * P:(c + 1) * P, kv_col:kv_col + G * D], w[:, :, c, :]) for W, w in ((Wk, wk), (Wv, wv))
                  for c in range(CC)]
        stages += [(Wq[k * P:(k + 1) * P, lo_col + n:lo_col + n + WIDTH], wq[:, :, k, n:n + WIDTH])
                   for k in range(KC) for n in range(0, H * D, WIDTH)]
        stages += [(Wo[lo_col + h * D:lo_col + (h + 1) * D, :], wo[:, :, h, :]) for h in range(H)]
        W_KV, W_Q, W_ALL = 2 * CC, 2 * CC + KC * H * D // WIDTH, len(stages)
        assert G * D == C == WIDTH and H * D % WIDTH == 0

        probs_flat = probs[:].rearrange("t n k -> t (n k)")
        slots = [stage[:, n, :] for n in range(4)] + \
                [probs_flat[:, n:n + WIDTH] for n in range(0, 4 * WIDE - WIDTH + 1, WIDTH)] + \
                [sums[:, n, :] for n in range(2)]
        SLOTS = len(slots)

        prologue = [("split", n) for n in range(W_KV)]
        for n, f in enumerate(HEAD):
            done = sum(what == "split" for what, _ in prologue)
            more = min(W_ALL - done, {"C": 0, "K": 2, "V": 2, "Q": 3}[f[0]])
            if f == ("C", 1, 0):
                prologue.append(("x", 0))
            prologue += [("fill", n)] + [("split", done + m) for m in range(more)]
        assert sum(what == "split" for what, _ in prologue) == W_ALL

        with nc.Block() as block:
            turns_in_loop = TURNS - 2

            @block.sync
            def _(sp):
                def load_ctx(turn, odd, waits):
                    b = sp.snap(turn.count(2, odd)) if turn.reg is not None else turn.count(2, odd)
                    for s, value in waits:
                        sp.wait_ge(s, value)
                        sp.nop(nofuse=True)
                    whole = S // P * P
                    sp.dma_start(ctxn[:, odd, 0:S // P, :],
                                 ctx[bass.ds(b, 1), 0:whole, :].rearrange("a (c p) d -> p (a c) d", p=P)) \
                        .then_inc(ctx_in[odd], 16)
                    sp.dma_start(ctxn[0:S - whole, odd, NKC - 1, :],
                                 ctx[bass.ds(b, 1), whole:S, :].rearrange("a p d -> (a p) d")) \
                        .then_inc(ctx_in[odd], 16)
                    sp.dma_start(mraw[:, odd], mask[bass.ds(b, 1), :].to_broadcast([T, S])).then_inc(mask_in[odd], 16)

                def load_x(turn, waits):
                    t = sp.snap(turn.count(T2, 0)) if turn.reg is not None else turn.count(T2, 0)
                    for s, value in waits:
                        sp.wait_ge(s, value)
                        sp.nop(nofuse=True)
                    sp.dma_start(xf[:], h2T[:, :, bass.ds(t, T2)].rearrange("c p t -> p c t")).then_inc(x_in, 16)

                def row(turn, n):
                    b = turn.count(2, n)
                    return bass.ds(sp.snap(b) if turn.reg is not None else b, 1)

                def load_base(turn, n):
                    b = row(turn, n)
                    if turn.reg is not None or turn.at > 0:
                        sp.wait_ge(stored[n], turn.count(16, 0))
                        sp.nop(nofuse=True)
                    sp.dma_start(sums[0:T, n, :], base[b].rearrange("a t c -> (a t) c")).then_inc(base_in[n], 16)

                def store(turn, n, until):
                    b = row(turn, n)
                    sp.wait_ge(fill_done, until)
                    sp.nop(nofuse=True)
                    sp.dma_start(result[b].rearrange("a t c -> (a t) c"), sums[0:T, n, :]).then_inc(stored[n], 16)

                for n, (src, _) in enumerate(stages):
                    if n >= SLOTS:
                        sp.wait_ge(w_lo, n - SLOTS + 1)
                    sp.dma_start(slots[n % SLOTS], src).then_inc(w_in[n % SLOTS], 16)
                    if n == W_KV - 1:
                        sp.wait_ge(padded, 1)
                        load_ctx(Turn(0), 0, [])
                    if n == SLOTS - 1:
                        load_x(Turn(0), [])
                        load_ctx(Turn(0), 1, [])

                def turn_of(turn, last=False):
                    after = Turn(turn.at + 1, turn.reg)
                    if not last:
                        load_ctx(after, 0, [(fill_ready, fills_until(turn.before(), ("C", 0, 1))),
                                            (mrow_ready, turn.count(2, 1))])
                        load_x(after, [(x_lo, turn.count(1, 1))])
                    if not last:
                        load_ctx(after, 1, [(fill_ready, fills_until(turn.before(), ("C", 1, 1))),
                                            (mrow_ready, turn.count(2, 2))])
                    if turn.at == 0 and turn.reg is None:
                        sp.wait_ge(w_lo, W_ALL)
                        load_base(turn, 0)
                    else:
                        load_base(turn, 0)
                        store(turn.before(), 1, fills_until(turn, ("O", 0, 1)))
                    load_base(turn, 1)
                    store(turn, 0, fills_until(turn, ("O", 1, 0)))

                turn_of(Turn(0))
                with sp.Fori(0, turns_in_loop) as j:
                    turn_of(Turn(1, j))
                turn_of(Turn(TURNS - 1), last=True)
                store(Turn(TURNS - 1), 1, BASE + NF * (TURNS - 1) + len(flatl) + 1)
                for n in range(2):
                    sp.wait_ge(stored[n], 16 * TURNS)

            @block.gpsimd
            def _(pool):
                make_identity(pool, ident[:], ident_done)

                def heads(turn, s):
                    for h in range(2):
                        n = 2 * s + h
                        m = n % 4
                        pool.wait_ge(masked, turn.count(16, n + 1))
                        pool.nop(nofuse=True)
                        pool.tensor_scalar(bias[:, m:m + 1], top[:, m:m + 1], -0.1 * NEG, -SCALE, ALU.max, ALU.mult) \
                            .then_inc(bias_ready, 1)
                    for h in range(2):
                        n = 2 * s + h
                        m = n % 4
                        pool.wait_ge(inv_ready, turn.count(16, n + 1))
                        pool.nop(nofuse=True)
                        pool.tensor_scalar(probs[0:T, m, 0:SE], probs[0:T, m, 0:SE], inv[:, m:m + 1], None,
                                           ALU.mult).then_inc(normed, 1)

                def turn_of(turn):
                    for s in range(8):
                        heads(turn, s)

                turn_of(Turn(0))
                with pool.Fori(0, turns_in_loop) as j:
                    turn_of(Turn(1, j))
                turn_of(Turn(TURNS - 1))

            def source(f, b):
                kind, odd, n = f
                if kind == "K":
                    return b[:, 0:SE], [kT[:, a, n, :] for a in (HI, LO)]
                if kind == "V":
                    rows = CHUNKS[n][1]
                    return b[0:rows, 0:G * D], [v[0:rows, odd, a, n, :] for a in (HI, LO)]
                if kind == "Q":
                    return (b[:, 0:2 * T2].rearrange("p (h t) -> p h t", h=2),
                            [qT[:, a, 2 * n:2 * n + 2, :] for a in (HI, LO)])
                return b[:, 0:SE], [ctxT[:, odd, a, n, :] for a in (HI, LO)]

            @block.scalar
            def _(act):
                def split(n):
                    act.wait_ge(w_in[n % SLOTS], 16 * (n // SLOTS + 1))
                    act.activation(stages[n][1][:, HI], slots[n % SLOTS], ACT.Copy).then_inc(w_hi, 1)

                def fill(turn, f, before, b):
                    act.wait_ge(fill_ready, before + 1)
                    src, dst = source(f, ps_f[b])
                    act.activation(dst[HI], src, ACT.Copy).then_inc(fill_hi, 1)

                def probsT(turn, s):
                    for h in range(2):
                        act.wait_ge(probsT_ready, turn.count(16, 2 * s + h + 1))
                        if h == 0 and not (turn.reg is None and turn.at == 0 and s < 2):
                            act.wait_ge(pv_ready, turn.count(8, s - 1))
                        act.activation(pT[:, s % 2, HI, :, h * T:(h + 1) * T],
                                       ps_t[h][:, 0:NKC * T].rearrange("p (c t) -> p c t", c=NKC),
                                       ACT.Copy).then_inc(pT_hi, 1)

                def out(turn, s):
                    act.wait_ge(pv_ready, turn.count(8, s + 1))
                    g, odd = s % 4, s // 4
                    act.activation(oT[:, HI, 2 * g:2 * g + 2, odd * T:(odd + 1) * T],
                                   ps_o[:, 0:T2].rearrange("p (h t) -> p h t", h=2), ACT.Copy).then_inc(o_hi, 1)

                def split_x(turn):
                    act.wait_ge(x_in, turn.count(16, 16))
                    if not (turn.reg is None and turn.at == 0):
                        act.wait_ge(fill_ready, made(turn.before(), ("Q", 0, G - 1)))
                    act.activation(x2[:, HI], xf[:], ACT.Copy).then_inc(x_hi, 1)

                def exps(turn, s):
                    for h in range(2):
                        n = 2 * s + h
                        m = n % 4
                        act.wait_ge(bias_ready, turn.count(16, n + 1))
                        act.activation(probs[0:T, m, 0:SE], probs[0:T, m, 0:SE], ACT.Exp, bias=bias[:, m:m + 1], scale=SCALE,
                                       accum_out=total[:, m:m + 1]).then_inc(exp_ready, 1)

                def turn_of(turn):
                    first = turn.reg is None and turn.at == 0
                    for s, fills in enumerate(fills_of(turn)):
                        if not (first and s < 1):
                            probsT(*(turn, s - 1) if s else (turn.before(), 7))
                        exps(turn, s)
                        if s == 2 and not (turn.reg is None and turn.at == TURNS - 1):
                            split_x(Turn(turn.at + 1, turn.reg))
                        if not (first and s < 2):
                            out(*(turn, s - 2) if s >= 2 else (turn.before(), s + 6))
                        for f, before, b in fills:
                            if f[0] != "O":
                                fill(turn, f, before, b)

                for what, n in prologue:
                    if what == "split":
                        split(n)
                    elif what == "x":
                        split_x(Turn(0))
                    else:
                        fill(Turn(-1), HEAD[n], n, n % 3)
                turn_of(Turn(0))
                with act.Fori(0, turns_in_loop) as j:
                    turn_of(Turn(1, j))
                turn_of(Turn(TURNS - 1))
                last = Turn(TURNS - 1)
                probsT(last, 7)
                out(last, 6)
                out(last, 7)

            @block.vector
            def _(dve):
                dve.memset(ctxn[96:P, :, NKC - 1, :], 0.0).then_inc(padded, 1)
                if SE > S:
                    dve.memset(mrow[:, :, S:SE], -NEG).then_inc(padded, 1)
                else:
                    dve.sem_inc(padded, 1)

                def split(n):
                    dst = stages[n][1]
                    dve.wait_ge(w_hi, n + 1)
                    dve.tensor_tensor(dst[:, LO], slots[n % SLOTS], dst[:, HI].bitcast(F32), ALU.subtract) \
                        .then_inc(w_lo, 1)

                def fill(turn, f, before, b):
                    src, dst = source(f, ps_f[b])
                    dve.wait_ge(fill_hi, halved(turn, f))
                    dve.tensor_tensor(dst[LO], src, dst[HI].bitcast(F32), ALU.subtract).then_inc(fill_done, 1)

                def add(turn, f, before, b):
                    n = f[2]
                    dve.wait_ge(fill_ready, before + 1)
                    dve.wait_ge(base_in[n], turn.count(16, 16))
                    dve.tensor_tensor(sums[0:T, n, :], ps_f[b][0:T, :], sums[0:T, n, :], ALU.add).then_inc(fill_done, 1)

                def split_x(turn):
                    dve.wait_ge(x_hi, turn.count(1, 1))
                    dve.tensor_tensor(x2[:, LO], xf[:], x2[:, HI].bitcast(F32), ALU.subtract).then_inc(x_lo, 1)

                def mask_row(turn, odd):
                    dve.wait_ge(mask_in[odd], turn.count(16, 16))
                    dve.tensor_scalar(mrow[:, odd, 0:S], mraw[:, odd, :], -1.0, NEG, ALU.add, ALU.mult) \
                        .then_inc(mrow_ready, 1)
                    dve.wait_ge(mrow_ready, turn.count(2, odd + 1))

                def maxima(turn, s):
                    for h in range(2):
                        n = 2 * s + h
                        m = n % 4
                        dve.wait_ge(scores_ready, turn.count(16, n + 1))
                        if not (turn.reg is None and turn.at == 0 and n < 4):
                            dve.wait_ge(probsT_ready, turn.count(16, n - 3))
                        dve.nop(nofuse=True)
                        dve.tensor_tensor_reduce(out=probs[0:T, m, 0:SE], in0=ps_s[h][0:T, 0:SE], in1=mrow[:, s // 4, :],
                                                 scale=1.0, scalar=-3.0e38, op0=ALU.add, op1=ALU.max,
                                                 accum_out=top[:, m:m + 1]).then_inc(masked, 1)

                def probsT(turn, s):
                    for h in range(2):
                        dve.wait_ge(pT_hi, turn.count(16, 2 * s + h + 1))
                        dve.tensor_tensor(pT[:, s % 2, LO, :, h * T:(h + 1) * T],
                                          ps_t[h][:, 0:NKC * T].rearrange("p (c t) -> p c t", c=NKC),
                                          pT[:, s % 2, HI, :, h * T:(h + 1) * T].bitcast(F32),
                                          ALU.subtract).then_inc(pT_lo, 1)

                def out(turn, s):
                    dve.wait_ge(o_hi, turn.count(8, s + 1))
                    g, odd = s % 4, s // 4
                    dve.tensor_tensor(oT[:, LO, 2 * g:2 * g + 2, odd * T:(odd + 1) * T],
                                      ps_o[:, 0:T2].rearrange("p (h t) -> p h t", h=2),
                                      oT[:, HI, 2 * g:2 * g + 2, odd * T:(odd + 1) * T].bitcast(F32),
                                      ALU.subtract).then_inc(o_lo, 1)

                def inverses(turn, s):
                    for h in range(2):
                        n = 2 * s + h
                        m = n % 4
                        dve.wait_ge(exp_ready, turn.count(16, n + 1))
                        dve.tensor_scalar(total[:, m:m + 1], total[:, m:m + 1], 1e-30, None, ALU.max) \
                            .then_inc(total_ready, 1)
                        dve.wait_ge(total_ready, turn.count(16, n + 1))
                        dve.reciprocal(inv[:, m:m + 1], total[:, m:m + 1]).then_inc(inv_ready, 1)

                def turn_of(turn):
                    first = turn.reg is None and turn.at == 0
                    for s, fills in enumerate(fills_of(turn)):
                        if s % 4 == 0:
                            mask_row(turn, s // 4)
                        maxima(turn, s)
                        if not (first and s < 1):
                            probsT(*(turn, s - 1) if s else (turn.before(), 7))
                        inverses(turn, s)
                        if s == 2 and not (turn.reg is None and turn.at == TURNS - 1):
                            split_x(Turn(turn.at + 1, turn.reg))
                        for f, before, b in fills:
                            if f[0] == "O":
                                add(turn if f[1] else turn.before(), f, before, b)
                        if not (first and s < 2):
                            out(*(turn, s - 2) if s >= 2 else (turn.before(), s + 6))
                        for f, before, b in fills:
                            if f[0] != "O":
                                fill(turn, f, before, b)

                for what, n in prologue:
                    if what == "split":
                        split(n)
                    elif what == "x":
                        split_x(Turn(0))
                    else:
                        fill(Turn(-1), HEAD[n], n, n % 3)
                dve.wait_ge(w_lo, W_ALL)
                dve.memset(probs[0:T, :, SE:WIDE], 0.0).then_inc(padded, 1)
                turn_of(Turn(0))
                with dve.Fori(0, turns_in_loop) as j:
                    turn_of(Turn(1, j))
                turn_of(Turn(TURNS - 1))
                last = Turn(TURNS - 1)
                probsT(last, 7)
                out(last, 6)
                out(last, 7)
                for n, f in enumerate(TAIL):
                    before = BASE + NF * (TURNS - 1) + len(flatl) + n
                    add(last, f, before, before % 3)

            @block.tensor
            def _(pe):
                pe.wait_ge(ident_done, 2)
                seen = [0]

                def weights(n):
                    if seen[0] < n:
                        pe.wait_ge(w_lo, n)
                        seen[0] = n

                def fill(turn, f, before, b, fed):
                    kind, odd, n = f
                    if not (isinstance(before, int) and before < 3):
                        pe.wait_ge(fill_done, before - 2)
                    for s, value in fed:
                        pe.wait_ge(s, value)
                    out = ps_f[b]
                    if kind == "C":
                        for c, (k, rows) in enumerate(CHUNKS):
                            last = pe.transpose(out[:, k:k + rows], ctxn[0:rows, odd, c, n * P:(n + 1) * P],
                                                ident[0:rows, 0:rows])
                        last.then_inc(fill_ready, 1)
                        return
                    if kind == "K":
                        groups = [[(out[:, 0:SE], wk[:, a, c, n * D:(n + 1) * D], ctxT[:, odd, b_, c, :])
                                   for c in range(CC) for a, b_ in PASSES]]
                    elif kind == "V":
                        k, rows = CHUNKS[n]
                        groups = [[(out[0:rows, 0:G * D], ctxT[:, odd, a, c, k:k + rows], wv[:, b_, c, :])
                                   for c in range(CC) for a, b_ in PASSES]]
                    elif kind == "Q":
                        groups = [[(out[:, h * T2:(h + 1) * T2], wq[:, a, c, (2 * n + h) * D:(2 * n + h + 1) * D],
                                    x2[:, b_, c, :]) for c in range(KC) for a, b_ in PASSES] for h in range(2)]
                    else:
                        groups = [[(out[0:T, :], oT[:, a, h, n * T:(n + 1) * T], wo[:, b_, h, :])
                                   for h in range(H) for a, b_ in PASSES]]
                    for jobs in groups:
                        for m, (o, w, x) in enumerate(jobs):
                            last = pe.matmul(o, w, x, start=m == 0, stop=m == len(jobs) - 1)
                    last.then_inc(fill_ready, 1)

                def fed(turn, f):
                    kind, odd, n = f
                    if kind == "C":
                        return [(ctx_in[odd], turn.count(32, 64))] if n == 0 else []
                    if kind == "Q":
                        return [(x_lo, turn.count(1, 2))] if n == 0 else []
                    if kind == "O":
                        return [(o_lo, turn.count(8, 4 if odd else 0))]
                    if n == 0 and kind == "K":
                        at = turn if odd == 0 else turn.before()
                        return [(fill_done, fills_until(at, ("C", odd, 1)))]
                    return []

                def scores(turn, s):
                    g, odd = s % 4, s // 4
                    pe.wait_ge(fill_done, made(turn, ("K", odd, g)))
                    if odd == 0 and turn.reg is None and turn.at == 0:
                        pe.wait_ge(fill_done, made(turn, ("Q", 0, g)))
                    for h in range(2):
                        n = 2 * s + h
                        if not (turn.reg is None and turn.at == 0 and n < 2):
                            pe.wait_ge(masked, turn.count(16, n - 1))
                        for m, (a, b_) in enumerate(PASSES):
                            last = pe.matmul(ps_s[h][0:T, 0:SE], qT[:, a, 2 * g + h, odd * T:(odd + 1) * T],
                                             kT[:, b_, g, :], start=m == 0, stop=m == 2)
                        last.then_inc(scores_ready, 1)

                def probsT(turn, s):
                    for h in range(2):
                        n = 2 * s + h
                        pe.wait_ge(normed, turn.count(16, n + 1))
                        if not (turn.reg is None and turn.at == 0 and n < 2):
                            pe.wait_ge(pT_lo, turn.count(16, n - 1))
                        for c in range(NKC):
                            last = pe.transpose(ps_t[h][:, c * T:(c + 1) * T],
                                                probs[0:T, n % 4, c * P:(c + 1) * P], ident[0:T, 0:T])
                        last.then_inc(probsT_ready, 1)

                def pv(turn, s):
                    g, odd = s % 4, s // 4
                    if g == 0:
                        pe.wait_ge(fill_done, made(turn, ("V", odd, NKC - 1)))
                    pe.wait_ge(pT_lo, turn.count(16, 2 * s + 2))
                    if not (turn.reg is None and turn.at == 0 and s == 0):
                        pe.wait_ge(o_lo, turn.count(8, s))
                    jobs = [(v[0:rows, odd, a, c, g * D:(g + 1) * D], pT[0:rows, s % 2, b_, c, :])
                            for c, (_, rows) in enumerate(CHUNKS) for a, b_ in PASSES]
                    for m, (w, x) in enumerate(jobs):
                        last = pe.matmul(ps_o[:, 0:T2], w, x, start=m == 0, stop=m == len(jobs) - 1)
                    last.then_inc(pv_ready, 1)

                def turn_of(turn):
                    first = turn.reg is None and turn.at == 0
                    for s, fills in enumerate(fills_of(turn)):
                        scores(turn, s)
                        if not (first and s < 1):
                            probsT(*(turn, s - 1) if s else (turn.before(), 7))
                        for f, before, b in fills:
                            if f[0] == "O":
                                fill(turn, f, before, b, fed(turn, f))
                        if not (first and s < 2):
                            pv(*(turn, s - 2) if s >= 2 else (turn.before(), s + 6))
                        for f, before, b in fills:
                            if f[0] != "O":
                                fill(turn, f, before, b, fed(turn, f))

                for n, f in enumerate(HEAD):
                    weights({"C": 0, "K": W_KV, "V": W_KV, "Q": W_Q}[f[0]])
                    waits = {("C", 0, 0): [(ctx_in[0], 32)], ("C", 1, 0): [(ctx_in[1], 32)],
                             ("K", 0, 0): [(fill_done, 2)], ("Q", 0, 0): [(x_lo, 1)]}
                    fill(Turn(-1), f, n, n % 3, waits.get(f, []))
                weights(W_ALL)
                pe.wait_ge(padded, 3)
                turn_of(Turn(0))
                with pe.Fori(0, turns_in_loop) as j:
                    turn_of(Turn(1, j))
                turn_of(Turn(TURNS - 1))
                last = Turn(TURNS - 1)
                probsT(last, 7)
                pv(last, 6)
                pv(last, 7)
                for n, f in enumerate(TAIL):
                    before = BASE + NF * (TURNS - 1) + len(flatl) + n
                    fill(last, f, before, before % 3, [(o_lo, 8 * TURNS)])


def expert_ffn(nc, B, T, x2, wg, W, b, slots, out):
    C = x2.shape[2]
    R = slots.shape[1]
    MEAN, RSTD, GATE, TOKEN = range(C, C + 4)
    KC = C // P
    E = W.shape[0]
    TILES = B * T // P
    SLOTS = TILES + E - 1
    EPS = 1e-5
    BF16 = mybir.dt.bfloat16

    with ExitStack() as stack:
        def sb(name, shape, dt=F32, to=stack):
            return to.enter_context(nc.sbuf_tensor(f"m_{name}", shape, dt))

        sem = stack.enter_context(semaphores(nc, "m"))

        wT = sb("wT", [P, 2, KC, E, C], F32R)
        owner = sb("owner", [P, SLOTS], I32)
        ident = sb("ident", [P, P])

        with ExitStack() as inner:
            def ib(name, shape, dt=F32):
                return sb(name, shape, dt, inner)

            def bank(name):
                return inner.enter_context(nc.psum_tensor(f"m_{name}", [P, 512], F32))

            tokens = ib("tokens", [P, TILES, R])
            hn = ib("hn", [P, 4, C])
            hT = ib("hT", [P, 2, KC, P])
            wgs = ib("wgs", [P, KC, E])
            logits = ib("logits", [P, TILES, E])
            order = ib("order", [P, TILES, E])
            before = ib("before", [P, TILES, E])
            best = ib("best", [P, TILES])
            total = ib("total", [P, TILES])
            chosen = ib("chosen", [P, TILES, E], BF16)
            slotf = ib("slotf", [P, TILES])
            slot = ib("slot", [P, TILES], U32)
            number = ib("number", [P, 2, 1, E])
            start = ib("start", [P, E])
            ownerf = ib("ownerf", [P, SLOTS])
            lower = ib("lower", [P, P], BF16)
            ones = ib("ones", [P, P], BF16)
            room = hT[:].rearrange("p a c t -> p (a c t)")
            N1, N2 = TILES * E, SLOTS * E
            like, places = (room[:, k * N1:(k + 1) * N1].rearrange("p (t e) -> p t e", e=E) for k in range(2))
            ends, steps = (room[:, 2 * N1 + k * N2:2 * N1 + (k + 1) * N2].rearrange("p (t e) -> p t e", e=E)
                           for k in range(2))
            assert 2 * (N1 + N2) <= 2 * C
            power = ib("power", [P, 1])
            st = ib("st", [P, 4, 6])
            mv = ib("mv", [P, 4, 2])
            rs = ib("rs", [P, 4, 1])
            ps = [bank(f"a{n}") for n in range(4)]
            ps_l = [bank(f"l{n}") for n in range(2)]
            ps_r = [bank(f"r{n}") for n in range(2)]

            const_done, tri_done, set_done, wg_in = sem("const"), sem("tri"), sem("set"), sem("wg_in")
            x_in = [sem(f"x_in{n}") for n in range(2)]
            w_in = [sem(f"w_in{n}") for n in range(4)]
            w_ready, w_hi, w_lo = sem("w_ready"), sem("w_hi"), sem("w_lo")
            st_ready, mv_ready, ve_ready, rs_ready, kept = sem("st"), sem("mv"), sem("ve"), sem("rs"), sem("kept")
            hn_ready, hT_ps, hT_ready = sem("hn"), sem("hT_ps"), sem("hT")
            logit_ps, logit_ready = sem("logit_ps"), sem("logit")
            less_ready, exp_ready, chosen_ready, ranked = sem("less"), sem("exp"), sem("chosen"), sem("ranked")
            chain, slots_ready, scattered = sem("chain"), sem("slots"), sem("scattered")

            TURNS = TILES // 4
            assert TILES % 4 == 0

            def previous(turn, half):
                return (turn, 0) if half else (turn.before(), 1)

            with nc.Block() as block:
                @block.sync
                def _(sp):
                    x2_t = x2.rearrange("b t c -> (b t) c").rearrange("(n p) c -> p n c", p=P)

                    def load_x(turn, half):
                        n = turn.count(4, 2 * half)
                        n = sp.snap(n) if turn.reg is not None else n
                        if turn.at > 0:
                            sp.wait_ge(x_in[half], turn.count(16, 0))
                            sp.nop(nofuse=True)
                        sp.dma_start(tokens[:, bass.ds(n, 2), 0:C], x2_t[:, bass.ds(n, 2), :]).then_inc(x_in[half], 16)

                    def load_w(turn, o):
                        n = turn.count(1, 0)
                        n = sp.snap(n) if turn.reg is not None else n
                        if turn.at > 0:
                            sp.wait_ge(w_ready, turn.count(KC, o - KC + 1))
                            sp.nop(nofuse=True)
                        sp.dma_start(hn[:, o, :], W[bass.ds(n, 1), o * P:(o + 1) * P, :].rearrange("a p h -> (a p) h")) \
                            .then_inc(w_in[o], 16)

                    for half in range(2):
                        load_x(Turn(0), half)
                    sp.dma_start(wgs[:], wg.rearrange("(c p) e -> p c e", p=P)).then_inc(wg_in, 16)
                    with sp.Fori(0, TURNS - 1) as j:
                        for half in range(2):
                            load_x(Turn(1, j), half)
                    sp.wait_ge(hT_ps, 2 * TURNS)
                    for o in range(KC):
                        load_w(Turn(0), o)
                    with sp.Fori(0, E - 1) as j:
                        for o in range(KC):
                            load_w(Turn(1, j), o)

                @block.gpsimd
                def _(pool):
                    make_identity(pool, ident[:], const_done)
                    pool.memset(ones[:], 1.0).then_inc(tri_done, 1)
                    pool.wait_ge(tri_done, 1)
                    pool.affine_select(out=lower[:], in_=ones[:], compare_op=ALU.is_gt, fill=0.0, base=0,
                                       pattern=[[1, P]], channel_multiplier=-1).then_inc(tri_done, 1)
                    pool.iota(order[:].rearrange("p t e -> p (t e)"), pattern=[[0, TILES], [1, E]], base=0,
                              channel_multiplier=0, allow_small_or_imprecise_dtypes=True).then_inc(tri_done, 1)
                    pool.iota(tokens[:, :, TOKEN:TOKEN + 1].rearrange("p t a -> p (t a)").bitcast(I32),
                              pattern=[[P, TILES]], base=0, channel_multiplier=1).then_inc(tri_done, 1)
                    pool.wait_ge(set_done, 1)

                    def rstd(turn, half):
                        at = slice(2 * half, 2 * half + 2)
                        pool.wait_ge(mv_ready, turn.count(4, 2 * half + 2))
                        pool.nop(nofuse=True)
                        if not (turn.reg is None and turn.at == 0):
                            pool.wait_ge(hn_ready, turn.count(2, half - 1))
                            pool.nop(nofuse=True)
                        pool.tensor_scalar(rs[:, at, :], mv[:, at, 1:2], EPS, None, ALU.add).then_inc(ve_ready, 1)
                        pool.wait_ge(ve_ready, turn.count(2, half + 1))
                        pool.nop(nofuse=True)
                        pool.tensor_tensor(rs[:, at, :], rs[:, at, :], power[:].unsqueeze(1).to_broadcast([P, 2, 1]),
                                           ALU.pow).then_inc(rs_ready, 1)

                    for half in range(2):
                        rstd(Turn(0), half)
                    with pool.Fori(0, TURNS - 1) as j:
                        for half in range(2):
                            rstd(Turn(1, j), half)
                    pool.wait_ge(logit_ps, 2 * TURNS)
                    pool.iota(steps.rearrange("p t e -> p (t e)"), pattern=[[1, SLOTS], [0, E]], base=0,
                              channel_multiplier=0, allow_small_or_imprecise_dtypes=True).then_inc(tri_done, 1)
                    pool.wait_ge(tri_done, 4)
                    pool.wait_ge(slots_ready, 1)
                    for t in range(TILES):
                        pool.indirect_dma_start(out=slots, out_offset=bass.IndirectOffsetOnAxis(ap=slot[:, t:t + 1], axis=0),
                                                in_=tokens[:, t, :], in_offset=None).then_inc(scattered, 16)
                    pool.wait_ge(scattered, 16 * TILES)

                @block.scalar
                def _(act):
                    def copy_hT(turn, half):
                        act.wait_ge(hT_ps, turn.count(2, half + 1))
                        if not (turn.reg is None and turn.at == 0 and half == 0):
                            act.wait_ge(logit_ps, turn.count(2, half))
                        for k in range(2):
                            last = act.activation(hT[:, k], ps[2 * half + k][:].rearrange("p (c t) -> p c t", c=KC),
                                                  ACT.Copy)
                        last.then_inc(hT_ready, 1)

                    def fill_w(turn, o):
                        act.wait_ge(w_ready, turn.count(KC, o + 1))
                        dst = wT[:, HI, :, bass.ds(turn.count(1, 0), 1), o * P:(o + 1) * P]
                        act.activation(dst.rearrange("p c a o -> p (c a) o"), ps[o][:].rearrange("p (c t) -> p c t", c=KC),
                                       ACT.Copy).then_inc(w_hi, 1)

                    for half in range(2):
                        copy_hT(Turn(0), half)
                    with act.Fori(0, TURNS - 1) as j:
                        for half in range(2):
                            copy_hT(Turn(1, j), half)
                    act.wait_ge(less_ready, 1)
                    act.activation(places, places, ACT.Exp).then_inc(exp_ready, 1)
                    with act.Fori(0, E) as j:
                        for o in range(KC):
                            fill_w(Turn(0, j), o)

                @block.vector
                def _(dve):
                    count = [0]

                    def link(ins):
                        count[0] += 1
                        ins.then_inc(chain, 1)
                        dve.wait_ge(chain, count[0])

                    dve.memset(power[:], -0.5).then_inc(set_done, 1)

                    def stats(turn, half):
                        dve.wait_ge(x_in[half], turn.count(16, 16))
                        if not (turn.reg is None and turn.at == 0):
                            dve.wait_ge(hn_ready, turn.count(2, half - 1))
                        dve.nop(nofuse=True)
                        for k in range(2):
                            src = tokens[:, bass.ds(turn.count(4, 2 * half + k), 1), 0:C].rearrange("p a c -> p (a c)")
                            dve.bn_stats(st[:, 2 * half + k, :], src).then_inc(st_ready, 1)
                        for k in range(2):
                            dve.wait_ge(st_ready, turn.count(4, 2 * half + k + 1))
                            dve.nop(nofuse=True)
                            dve.bn_aggr(mv[:, 2 * half + k, :], st[:, 2 * half + k, :]).then_inc(mv_ready, 1)

                    def normal(turn, half):
                        n = turn.count(4, 2 * half)
                        dve.wait_ge(rs_ready, turn.count(2, half + 1))
                        dve.nop(nofuse=True)
                        two = slice(2 * half, 2 * half + 2)
                        for src, col in ((mv[:, two, 0:1], MEAN), (rs[:, two, :], RSTD)):
                            last = dve.tensor_copy(tokens[:, bass.ds(n, 2), col:col + 1], src)
                        last.then_inc(kept, 1)
                        if not (turn.reg is None and turn.at == 0):
                            dve.wait_ge(hT_ps, turn.count(2, half - 1))
                            dve.nop(nofuse=True)
                        for k in range(2 * half, 2 * half + 2):
                            src = tokens[:, bass.ds(turn.count(4, k), 1), 0:C].rearrange("p a c -> p (a c)")
                            last = dve.tensor_scalar(hn[:, k, :], src, mv[:, k, 0:1], rs[:, k, :],
                                                     ALU.subtract, ALU.mult)
                        last.then_inc(hn_ready, 1)

                    def keep_logits(turn, half):
                        dve.wait_ge(logit_ps, turn.count(2, half + 1))
                        dve.tensor_copy(logits[:, bass.ds(turn.count(4, 2 * half), 2), :],
                                        ps_l[half][:, 0:2 * E].rearrange("p (k e) -> p k e", k=2)).then_inc(logit_ready, 1)

                    def turn_of(turn):
                        for half in range(2):
                            stats(turn, half)
                            if not (turn.reg is None and turn.at == 0 and half == 0):
                                normal(*previous(turn, half))
                            if not (turn.reg is None and turn.at * 2 + half < 3):
                                keep_logits(*((turn.before(), 0) if half else (turn.before().before(), 1)))

                    def fill_w(turn, o):
                        dve.wait_ge(w_hi, turn.count(KC, o + 1))
                        hi, lo = (wT[:, a, :, bass.ds(turn.count(1, 0), 1), o * P:(o + 1) * P]
                                  .rearrange("p c a o -> p (c a) o") for a in (HI, LO))
                        dve.tensor_tensor(lo, ps[o][:].rearrange("p (c t) -> p c t", c=KC), hi.bitcast(F32),
                                          ALU.subtract).then_inc(w_lo, 1)

                    turn_of(Turn(0))
                    turn_of(Turn(1))
                    with dve.Fori(0, TURNS - 2) as j:
                        turn_of(Turn(2, j))
                    normal(Turn(TURNS - 1), 1)
                    keep_logits(Turn(TURNS - 2), 1)
                    for half in range(2):
                        keep_logits(Turn(TURNS - 1), half)

                    def over_e(a):
                        return a.unsqueeze(2).to_broadcast([P, a.shape[1], E])

                    def over_t(a, n):
                        return a.unsqueeze(1).to_broadcast([P, n, E])

                    def running_sum(a, b_, n):
                        d = 1
                        while d < n:
                            dve.tensor_copy(b_[:, 0:d], a[:, 0:d])
                            link(dve.tensor_tensor(b_[:, d:n], a[:, d:n], a[:, 0:n - d], ALU.add))
                            a, b_, d = b_, a, 2 * d
                        return a

                    dve.wait_ge(logit_ready, 2 * TURNS)
                    dve.wait_ge(tri_done, 5)
                    link(dve.tensor_reduce(best[:], logits[:], AX.X, ALU.max))
                    dve.tensor_tensor(places, logits[:], over_e(best[:]), ALU.subtract).then_inc(less_ready, 1)
                    link(dve.tensor_tensor(like, logits[:], over_e(best[:]), ALU.is_equal))
                    link(dve.scalar_tensor_tensor(out=logits[:], in0=like, scalar=-float(E), in1=order[:],
                                                  op0=ALU.mult, op1=ALU.add))
                    link(dve.tensor_reduce(best[:], logits[:], AX.X, ALU.min))
                    dve.tensor_tensor(chosen[:], logits[:], over_e(best[:]), ALU.is_equal).then_inc(chosen_ready, 1)
                    link(dve.tensor_tensor(like, logits[:], over_e(best[:]), ALU.is_equal))
                    dve.wait_ge(exp_ready, 1)
                    link(dve.tensor_reduce(total[:], places, AX.X, ALU.add))
                    dve.reciprocal(tokens[:, :, GATE:GATE + 1].rearrange("p t a -> p (t a)"), total[:])
                    dve.wait_ge(ranked, 1)
                    inside, each = (ps_r[k][:, 0:TILES * E].rearrange("p (t e) -> p t e", e=E) for k in range(2))
                    link(dve.tensor_copy(before[:], each))
                    upto = running_sum(before[:], order[:], TILES)
                    tiles = number[:, 0].rearrange("p a e -> p (a e)")
                    link(dve.tensor_scalar(tiles, upto[:, TILES - 1, :], 1.0 / P, 0.5 - 0.5 / P, ALU.mult, ALU.add))
                    link(dve.tensor_scalar(tiles, tiles, 8388608.0, None, ALU.add))
                    link(dve.tensor_scalar(tiles, tiles, -8388608.0, None, ALU.add))
                    link(dve.tensor_copy(start[:], tiles))
                    past = running_sum(start[:], number[:, 1].rearrange("p a e -> p (a e)"), E)
                    first = ownerf[:, 0:E]
                    dve.tensor_tensor(first, past, tiles, ALU.subtract)
                    link(dve.tensor_tensor(places, inside, upto, ALU.add))
                    link(dve.tensor_tensor(places, places, each, ALU.subtract))
                    link(dve.scalar_tensor_tensor(out=places, in0=over_t(first, TILES), scalar=float(P),
                                                  in1=places, op0=ALU.mult, op1=ALU.add))
                    link(dve.tensor_tensor(places, places, like, ALU.mult))
                    link(dve.tensor_reduce(slotf[:], places, AX.X, ALU.add))
                    dve.tensor_copy(slot[:], slotf[:]).then_inc(slots_ready, 1)
                    link(dve.tensor_tensor(ends, steps, over_t(past, SLOTS), ALU.is_ge))
                    link(dve.tensor_reduce(ownerf[:], ends, AX.X, ALU.add))
                    link(dve.tensor_scalar(ownerf[:], ownerf[:], float(E - 1), None, ALU.min))
                    link(dve.tensor_copy(owner[:], ownerf[:]))
                    with dve.Fori(0, E) as j:
                        for o in range(KC):
                            fill_w(Turn(0, j), o)

                @block.tensor
                def _(pe):
                    pe.wait_ge(const_done, 2)

                    def rows(turn, half):
                        pe.wait_ge(hn_ready, turn.count(2, half + 1))
                        if not (turn.reg is None and turn.at == 0):
                            pe.wait_ge(hT_ready, turn.count(2, half - 1))
                        for k in range(2 * half, 2 * half + 2):
                            for c in range(KC):
                                last = pe.transpose(ps[k][:, c * P:(c + 1) * P], hn[:, k, c * P:(c + 1) * P], ident[:])
                        last.then_inc(hT_ps, 1)

                    def router(turn, half):
                        pe.wait_ge(hT_ready, turn.count(2, half + 1))
                        if not (turn.reg is None and turn.at == 0):
                            pe.wait_ge(logit_ready, turn.count(2, half - 1))
                        for k in range(2):
                            for c in range(KC):
                                last = pe.matmul(ps_l[half][:, k * E:(k + 1) * E], hT[:, k, c, :], wgs[:, c, :],
                                                 start=c == 0, stop=c == KC - 1)
                        last.then_inc(logit_ps, 1)

                    def turn_of(turn):
                        for half in range(2):
                            rows(turn, half)
                            if not (turn.reg is None and turn.at == 0 and half == 0):
                                router(*previous(turn, half))

                    def fill_w(turn, o):
                        pe.wait_ge(w_in[o], turn.count(16, 16))
                        if turn.at > 0:
                            pe.wait_ge(w_lo, turn.count(KC, o - KC + 1))
                        for c in range(KC):
                            last = pe.transpose(ps[o][:, c * P:(c + 1) * P], hn[:, o, c * P:(c + 1) * P], ident[:])
                        last.then_inc(w_ready, 1)

                    pe.wait_ge(wg_in, 16)
                    turn_of(Turn(0))
                    with pe.Fori(0, TURNS - 1) as j:
                        turn_of(Turn(1, j))
                    router(Turn(TURNS - 1), 1)
                    pe.wait_ge(chosen_ready, 1)
                    pe.wait_ge(tri_done, 2)
                    rhs = chosen[:].rearrange("p t e -> p (t e)")
                    pe.matmul(ps_r[0][:, 0:TILES * E], lower[:], rhs, start=True, stop=True)
                    pe.matmul(ps_r[1][:, 0:TILES * E], ones[:], rhs, start=True, stop=True).then_inc(ranked, 1)
                    for o in range(KC):
                        fill_w(Turn(0), o)
                    with pe.Fori(0, E - 1) as j:
                        for o in range(KC):
                            fill_w(Turn(1, j), o)

        with ExitStack() as inner:
            def ib(name, shape, dt=F32):
                return sb(name, shape, dt, inner)

            def bank(name):
                return inner.enter_context(nc.psum_tensor(f"m_{name}", [P, 512], F32))

            U = 8
            Y = 4
            bias = ib("bias", [P, E, C])
            rows = ib("rows", [P, U, R])
            h = ib("h", [P, 2, C])
            rT = ib("rT", [P, 2, 2, KC, P], F32R)
            y = ib("y", [P, Y, C])
            ps_t = [bank(f"t{n}") for n in range(2)]
            ps_y = [bank(f"y{n}") for n in range(2)]

            bias_in = sem("bias_in")
            rows_in = [sem(f"rows_in{n}") for n in range(U)]
            out_done = [sem(f"out_done{n}") for n in range(U)]
            h_ready, rT_ready, rT_hi, rT_lo = sem("h_ready"), sem("rT_ready"), sem("rT_hi"), sem("rT_lo")
            y_ps, y_biased, y_ready = sem("y_ps"), sem("y_biased"), sem("y_ready")

            TURNS, REST = SLOTS // U, SLOTS % U
            assert REST >= 2
            slots_t = slots.rearrange("(n p) c -> n p c", p=P)

            def later(turn, k, d):
                return Turn(turn.at + (k + d) // U, turn.reg), (k + d) % U

            def exists(turn, k):
                return turn.reg is not None or turn.at * U + k < SLOTS

            def is_first(turn, k, n):
                return turn.reg is None and turn.at * U + k < n

            def all_turns(eng, step):
                for k in range(U):
                    step(Turn(0), k)
                with eng.Fori(0, TURNS - 1) as j:
                    for k in range(U):
                        step(Turn(1, j), k)
                for k in range(REST):
                    step(Turn(TURNS), k)

            with nc.Block() as block:
                @block.sync
                def _(sp):
                    def load(turn, k):
                        n = turn.count(U, k)
                        n = sp.snap(n) if turn.reg is not None else n
                        if not is_first(turn, k, U):
                            sp.wait_ge(out_done[k], turn.count(16, 0))
                            sp.nop(nofuse=True)
                        sp.dma_start(rows[:, k, :], slots_t[bass.ds(n, 1)].rearrange("a p c -> (a p) c")) \
                            .then_inc(rows_in[k], 16)
                        if is_first(turn, k, U) and k == 3:
                            sp.dma_start(bias[:].rearrange("p e o -> p (e o)"),
                                         b.rearrange("e o -> (e o)").rearrange("(a n) -> a n", a=1)
                                         .to_broadcast([P, E * C])).then_inc(bias_in, 16)

                    all_turns(sp, load)

                @block.gpsimd
                def _(pool):
                    def scatter(turn, k):
                        pool.wait_ge(y_ready, turn.count(U, k + 1))
                        pool.nop(nofuse=True)
                        pool.indirect_dma_start(
                            out=out, out_offset=bass.IndirectOffsetOnAxis(
                                ap=rows[:, k, TOKEN:TOKEN + 1].bitcast(U32), axis=0),
                            in_=y[:, k % Y, :], in_offset=None).then_inc(out_done[k], 16)

                    all_turns(pool, scatter)
                    for k in range(U):
                        pool.wait_ge(out_done[k], 16 * (TURNS + (k < REST)))

                @block.scalar
                def _(act):
                    def copy_rT(turn, k):
                        act.wait_ge(rT_ready, turn.count(U, k + 1))
                        if not is_first(turn, k, 2):
                            act.wait_ge(y_ps, turn.count(U, k - 1))
                        act.activation(rT[:, k % 2, HI], ps_t[k % 2][:].rearrange("p (c t) -> p c t", c=KC), ACT.Copy) \
                            .then_inc(rT_hi, 1)

                    all_turns(act, copy_rT)

                @block.vector
                def _(dve):
                    def normal(turn, k):
                        dve.wait_ge(rows_in[k], turn.count(16, 16))
                        if not is_first(turn, k, 2):
                            dve.wait_ge(rT_ready, turn.count(U, k - 1))
                        dve.tensor_scalar(h[:, k % 2, :], rows[:, k, 0:C], rows[:, k, MEAN:MEAN + 1],
                                          rows[:, k, RSTD:RSTD + 1], ALU.subtract, ALU.mult).then_inc(h_ready, 1)

                    def copy_rT(turn, k):
                        dve.wait_ge(rT_hi, turn.count(U, k + 1))
                        dve.tensor_tensor(rT[:, k % 2, LO], ps_t[k % 2][:].rearrange("p (c t) -> p c t", c=KC),
                                          rT[:, k % 2, HI].bitcast(F32), ALU.subtract).then_inc(rT_lo, 1)

                    def finish(turn, k):
                        e = dve.value_load(owner[0:1, bass.ds(turn.count(U, k), 1)], min_val=0, max_val=E - 1)
                        dve.wait_ge(y_ps, turn.count(U, k + 1))
                        if not is_first(turn, k, Y):
                            before, m = later(turn, k, -Y)
                            dve.wait_ge(out_done[m], before.count(16, 16))
                        dve.tensor_tensor(y[:, k % Y, :], ps_y[k % 2][:],
                                          bias[:, bass.ds(e, 1), :].rearrange("p a o -> p (a o)"), ALU.add) \
                            .then_inc(y_biased, 1)
                        dve.wait_ge(y_biased, turn.count(U, k + 1))
                        dve.nop(nofuse=True)
                        dve.scalar_tensor_tensor(out=y[:, k % Y, :], in0=y[:, k % Y, :], scalar=rows[:, k, GATE:GATE + 1],
                                                 in1=rows[:, k, 0:C], op0=ALU.mult, op1=ALU.add).then_inc(y_ready, 1)

                    def step(turn, k):
                        if exists(*later(turn, k, 2)):
                            normal(*later(turn, k, 2))
                        if exists(*later(turn, k, 1)):
                            copy_rT(*later(turn, k, 1))
                        finish(turn, k)

                    normal(Turn(0), 0)
                    normal(Turn(0), 1)
                    copy_rT(Turn(0), 0)
                    dve.wait_ge(bias_in, 16)
                    all_turns(dve, step)

                @block.tensor
                def _(pe):
                    def transpose(turn, k):
                        pe.wait_ge(h_ready, turn.count(U, k + 1))
                        if not is_first(turn, k, 2):
                            pe.wait_ge(rT_lo, turn.count(U, k - 1))
                        for c in range(KC):
                            last = pe.transpose(ps_t[k % 2][:, c * P:(c + 1) * P], h[:, k % 2, c * P:(c + 1) * P], ident[:])
                        last.then_inc(rT_ready, 1)

                    def product(turn, k):
                        e = pe.value_load(owner[0:1, bass.ds(turn.count(U, k), 1)], min_val=0, max_val=E - 1)
                        pe.wait_ge(rT_lo, turn.count(U, k + 1))
                        if not is_first(turn, k, 2):
                            pe.wait_ge(y_biased, turn.count(U, k - 1))
                        jobs = [(a, b_, c) for c in range(KC) for a, b_ in PASSES]
                        for m, (a, b_, c) in enumerate(jobs):
                            last = pe.matmul(ps_y[k % 2][:], rT[:, k % 2, a, c, :],
                                             wT[:, b_, c, bass.ds(e, 1), :].rearrange("p a o -> p (a o)"),
                                             start=m == 0, stop=m == len(jobs) - 1)
                        last.then_inc(y_ps, 1)

                    def step(turn, k):
                        if exists(*later(turn, k, 1)):
                            transpose(*later(turn, k, 1))
                        product(turn, k)

                    transpose(Turn(0), 0)
                    all_turns(pe, step)


def decoder_block(nc, x, ctx_1024, mask, attn_Wq, attn_bq, attn_Wk, attn_bk, attn_Wv, attn_bv, attn_Wo, attn_bo,
                  xattn_Wq, xattn_Wk, xattn_Wv, xattn_Wo, ffn_wg, ffn_W, ffn_b, out):
    B, T, C = x.shape
    S = ctx_1024.shape[1]
    E = ffn_W.shape[0]
    N = B * T
    rows = (N // P + E - 1) * P
    R = C + 4

    def scratch(name, shape):
        return nc.dram_tensor(name, shape, F32, kind="Internal").ap()

    x1 = scratch("x1", [B, T, C])
    h2T = scratch("h2T", [C // P, P, N])
    x1_half = scratch("x1_half", [B, T, C])
    x2 = scratch("x2", [B, T, C])
    slots = scratch("slots", [rows, R])

    window_attention(nc, B, T, x, attn_Wq, attn_bq, attn_Wk, attn_bk, attn_Wv, attn_bv, attn_Wo, attn_bo, x1, h2T,
                     slots, out[N:])
    for half, (base, result) in enumerate(((x1, x1_half), (x1_half, x2))):
        cross_attention(nc, half, B, T, S, h2T, ctx_1024, mask, xattn_Wq, xattn_Wk, xattn_Wv, xattn_Wo, base, result)
    expert_ffn(nc, B, T, x2, ffn_wg, ffn_W, ffn_b, slots, out)


_INS = ['x', 'ctx_1024', 'mask_BxS2_bf1', 'L0_attn_Wq', 'L0_attn_bq', 'L0_attn_Wk', 'L0_attn_bk', 'L0_attn_Wv',
        'L0_attn_bv', 'L0_attn_Wo', 'L0_attn_bo', 'L0_xattn_Wq', 'L0_xattn_Wk', 'L0_xattn_Wv', 'L0_xattn_Wo',
        'L0_ffn_wg', 'L0_ffn_W', 'L0_ffn_b']
_OUTS = [((32 * 112 + 4 * P, 512), 'float32')]


def kernel(**inputs):
    import numpy as _np
    import concourse.bacc as _bacc
    from concourse import mybir as _mybir
    from concourse.bass_utils import run_bass_kernel_spmd as _run

    nc = _bacc.Bacc("TRN2", target_bir_lowering=False, num_devices=1)
    arrays, args = {}, []
    for name in _INS:
        a = _np.ascontiguousarray(inputs[name])
        arrays[f"in_{name}_dram"] = a
        args.append(nc.dram_tensor(f"in_{name}_dram", a.shape, _mybir.dt.from_np(a.dtype), kind="ExternalInput").ap())
    for i, (shape, dtype) in enumerate(_OUTS):
        dt = _mybir.dt.from_np(_np.dtype(dtype))
        args.append(nc.dram_tensor(f"out_{i}_dram", shape, dt, kind="ExternalOutput").ap())
    decoder_block(nc, *args)
    r = _run(nc, [arrays], core_ids=[0])
    got = tuple(r.results[0][f"out_{i}_dram"] for i in range(len(_OUTS)))
    B, T, C = inputs['x'].shape
    return got[0][:B * T].reshape(B, T, C)
```
